# Optimizing a Trainium2 kernel written in Bass

```python
import numpy as np
import jax
import jax.numpy as jnp

def _softmax(x, axis=-1):
    return jax.nn.softmax(x, axis=axis)

def _gelu(x):
    return jax.nn.gelu(x, approximate=True)

def _silu(x):
    return jax.nn.silu(x)

def _sigmoid(x):
    return jax.nn.sigmoid(x)

def _layernorm(x, axis=-1, eps=1e-05):
    m = jnp.mean(x, axis=axis, keepdims=True)
    v = jnp.var(x, axis=axis, keepdims=True)
    return (x - m) / jnp.sqrt(v + eps)

def _scatter_add(tgt, idx, src, axis=0):
    return tgt.at[idx].add(src)

def _segment_sum(src, seg, n):
    return jax.ops.segment_sum(src, seg, n)
kernel_name = 'mk_audio_tower_d1_tok_audfeat1024_r4_31e672'

def setup_inputs(seed: int=0):
    np.random.seed(seed)
    _w = jnp.asarray

    def _rec_inputs():
        import jax
        import jax.numpy as jnp
        _rk = jax.random.key(seed)
        x = -0.000123307 + 1.00004 * jax.random.normal(jax.random.fold_in(_rk, 1), (32, 375, 80), jnp.float32)
        return x
    x = _rec_inputs()

    def _L0_tok_setup():
        import jax, jax.numpy as jnp
        import numpy as np
        NUM_FRAMES = 8
        STRIDE = 4
        BN_EPS = 1e-05
        key = jax.random.key(seed)
        ks = jax.random.split(key, 7)
        B, L, D = (32, 1024, 80)
        H1, H2 = (256, 256)
        x = jax.random.normal(ks[0], (B, L, D), dtype=jnp.float32)
        W1 = jax.random.normal(ks[1], (D * NUM_FRAMES, H1), dtype=jnp.float32) * (1.0 / np.sqrt(D * NUM_FRAMES))
        b1 = jax.random.normal(ks[2], (H1,), dtype=jnp.float32) * 0.01
        W2 = jax.random.normal(ks[3], (H1, H2), dtype=jnp.float32) * (1.0 / np.sqrt(H1))
        b2 = jax.random.normal(ks[4], (H2,), dtype=jnp.float32) * 0.01
        gamma = 1.0 + 0.1 * jax.random.normal(ks[5], (H2,), dtype=jnp.float32)
        beta = 0.1 * jax.random.normal(ks[6], (H2,), dtype=jnp.float32)
        return {'x': x, 'W1': W1, 'b1': b1, 'W2': W2, 'b2': b2, 'gamma': gamma, 'beta': beta}
    _L0_tok_all = _L0_tok_setup()
    _L0_tok_in = {k: v for k, v in _L0_tok_all.items() if k in ('W1', 'b1', 'W2', 'b2', 'gamma', 'beta')}
    del _L0_tok_all

    def _L0_attn_setup():
        import jax, jax.numpy as jnp
        import numpy as np
        B, S, D_IN = (2, 512, 256)
        H, D_HEAD = (16, 64)
        key = jax.random.key(seed)
        k1, k2, k3 = jax.random.split(key, 3)
        x = jax.random.normal(k1, (B, S, D_IN), dtype=jnp.float32)
        kernel = jax.random.normal(k2, (3, H, D_IN, D_HEAD), dtype=jnp.float32) * np.float32(np.sqrt(2.0 / D_IN))
        WO = jax.random.normal(k3, (1, H * D_HEAD, D_IN), dtype=jnp.float32) * np.float32(np.sqrt(2.0 / (H * D_HEAD)))
        return {'x': x, 'kernel': kernel, 'WO': WO}
    _L0_attn_all = _L0_attn_setup()
    _L0_attn_in = {k: v for k, v in _L0_attn_all.items() if k in ('kernel', 'WO')}
    del _L0_attn_all

    def _L0_ffn_setup():
        import jax, jax.numpy as jnp
        import numpy as np
        H, F, E_SHARED, E_ROUTED, K = (256, 1024, 1, 8, 2)

        def _expert(x, w_up, w_down):
            h = jax.nn.gelu(jnp.einsum('bsh,hf->bsf', x, w_up), approximate=False)
            return jnp.einsum('bsf,fh->bsh', h, w_down)
        key = jax.random.key(seed)
        ks = jax.random.split(key, 6)
        x = jax.random.normal(ks[0], (4, 512, H), dtype=jnp.float32)
        s = 0.02
        shared_up = jax.random.normal(ks[1], (E_SHARED, H, F), dtype=jnp.float32) * s
        shared_down = jax.random.normal(ks[2], (E_SHARED, F, H), dtype=jnp.float32) * s
        routed_up = jax.random.normal(ks[3], (E_ROUTED, H, F), dtype=jnp.float32) * s
        routed_down = jax.random.normal(ks[4], (E_ROUTED, F, H), dtype=jnp.float32) * s
        router_w = jax.random.normal(ks[5], (H, E_ROUTED), dtype=jnp.float32) * s
        return {'x': x, 'shared_up': shared_up, 'shared_down': shared_down, 'routed_up': routed_up, 'routed_down': routed_down, 'router_w': router_w}
    _L0_ffn_all = _L0_ffn_setup()
    _L0_ffn_in = {k: v for k, v in _L0_ffn_all.items() if k in ('shared_up', 'shared_down', 'routed_up', 'routed_down', 'router_w')}
    del _L0_ffn_all
    return {'x': x, 'L0_tok_W1': _L0_tok_in['W1'], 'L0_tok_b1': _L0_tok_in['b1'], 'L0_tok_W2': _L0_tok_in['W2'], 'L0_tok_b2': _L0_tok_in['b2'], 'L0_tok_gamma': _L0_tok_in['gamma'], 'L0_tok_beta': _L0_tok_in['beta'], 'L0_attn_kernel': _L0_attn_in['kernel'], 'L0_attn_WO': _L0_attn_in['WO'], 'L0_ffn_shared_up': _L0_ffn_in['shared_up'], 'L0_ffn_shared_down': _L0_ffn_in['shared_down'], 'L0_ffn_routed_up': _L0_ffn_in['routed_up'], 'L0_ffn_routed_down': _L0_ffn_in['routed_down'], 'L0_ffn_router_w': _L0_ffn_in['router_w']}

def reference(x, L0_tok_W1, L0_tok_b1, L0_tok_W2, L0_tok_b2, L0_tok_gamma, L0_tok_beta, L0_attn_kernel, L0_attn_WO, L0_ffn_shared_up, L0_ffn_shared_down, L0_ffn_routed_up, L0_ffn_routed_down, L0_ffn_router_w):
    import jax
    import jax.numpy as jnp

    def _L0_tok_ref(x, W1, b1, W2, b2, gamma, beta):
        import jax, jax.numpy as jnp
        import numpy as np
        NUM_FRAMES = 8
        STRIDE = 4
        BN_EPS = 1e-05
        B, L, D = x.shape
        remove_top = L - NUM_FRAMES
        if remove_top < 0:
            pad = -remove_top
        else:
            pad = STRIDE - remove_top % STRIDE
        xp = jnp.pad(x, ((0, 0), (0, pad), (0, 0)))
        Lp = L + pad
        num_slices = 1 + (Lp - NUM_FRAMES) // STRIDE
        idx = np.arange(num_slices)[:, None] * STRIDE + np.arange(NUM_FRAMES)[None, :]
        win = xp[:, idx, :].reshape(B, num_slices, NUM_FRAMES * D)
        h = jax.nn.relu(jnp.einsum('bsk,kh->bsh', win, W1) + b1)
        h = jax.nn.relu(jnp.einsum('bsk,kh->bsh', h, W2) + b2)
        mean = jnp.mean(h, axis=(0, 1))
        var = jnp.var(h, axis=(0, 1))
        out = (h - mean) * jax.lax.rsqrt(var + BN_EPS) * gamma + beta
        return out

    def _L0_attn_ref(x, kernel, WO):
        import jax, jax.numpy as jnp
        import numpy as np
        B, S, D_IN = (2, 512, 256)
        H, D_HEAD = (16, 64)
        b, s, _ = x.shape
        h, d = (kernel.shape[1], kernel.shape[3])
        q = jnp.einsum('bsm,hmd->bhsd', x, kernel[0])
        k = jnp.einsum('bsm,hmd->bhsd', x, kernel[1])
        v = jnp.einsum('bsm,hmd->bhsd', x, kernel[2])
        scale = jnp.float32(1.0 / (d * d * h))
        scores = jnp.einsum('bhsd,bhtd->bhst', q, k) * scale
        attn = jax.nn.softmax(scores, axis=-1)
        out = jnp.einsum('bhst,bhtd->bhsd', attn, v)
        out = jnp.transpose(out, (0, 2, 3, 1)).reshape(b, s, d * h)
        out = jnp.einsum('bsf,fm->bsm', out, WO[0])
        return out

    def _L0_ffn_ref(x, shared_up, shared_down, routed_up, routed_down, router_w):
        import jax, jax.numpy as jnp
        import numpy as np
        H, F, E_SHARED, E_ROUTED, K = (256, 1024, 1, 8, 2)

        def _expert(x, w_up, w_down):
            h = jax.nn.gelu(jnp.einsum('bsh,hf->bsf', x, w_up), approximate=False)
            return jnp.einsum('bsf,fh->bsh', h, w_down)
        shared_out = jnp.zeros_like(x)
        for i in range(E_SHARED):
            shared_out = shared_out + _expert(x, shared_up[i], shared_down[i])
        probs = jax.nn.softmax(jnp.einsum('bsh,he->bse', x, router_w), axis=-1)
        top_k_prob, top_k_idx = jax.lax.top_k(probs, K)
        onehot = jax.nn.one_hot(top_k_idx, E_ROUTED, dtype=x.dtype)
        gates = jnp.einsum('bsk,bske->bse', top_k_prob, onehot)
        routed_out = jnp.zeros_like(x)
        for e in range(E_ROUTED):
            y = _expert(x, routed_up[e], routed_down[e])
            routed_out = routed_out + gates[..., e:e + 1] * y
        return shared_out + routed_out + x
    h = _L0_tok_ref(x, L0_tok_W1, L0_tok_b1, L0_tok_W2, L0_tok_b2, L0_tok_gamma, L0_tok_beta)
    h = h + _L0_attn_ref(_layernorm(h, axis=-1), L0_attn_kernel, L0_attn_WO)
    h = h + _L0_ffn_ref(_layernorm(h, axis=-1), L0_ffn_shared_up, L0_ffn_shared_down, L0_ffn_routed_up, L0_ffn_routed_down, L0_ffn_router_w)
    return h

_drawn_inputs = setup_inputs


def setup_inputs(seed=0):
    import zlib

    import numpy as np

    out = dict(_drawn_inputs(seed))
    spreads = {}
    factors = {'L0_tok_b1': 4.562,
     'L0_tok_b2': 4.993,
     'L0_ffn_routed_up': 4.305,
     'L0_ffn_routed_down': 4.206,
     'L0_ffn_router_w': 4.758}
    for name, (base, spread) in spreads.items():
        noise = np.random.default_rng([zlib.crc32(name.encode()), seed]).standard_normal(out[name].shape)
        drawn = base * np.exp(spread * noise) if base else spread * noise
        out[name] = jnp.asarray(drawn.astype(out[name].dtype))
    for name, factor in factors.items():
        out[name] = (out[name] * factor).astype(out[name].dtype)
    return out
```

```python
from contextlib import ExitStack

import concourse.bass as bass
from concourse import mybir

ALU = mybir.AluOpType
ACT = mybir.ActivationFunctionType
F32 = mybir.dt.float32
F32R = mybir.dt.float32r
I32 = mybir.dt.int32
U32 = mybir.dt.uint32
AX = mybir.AxisListType.X

P = 128
EPS = 1e-5

HI, LO = 0, 1
PASSES = ((HI, HI), (HI, LO), (LO, HI))


class Chain:

    def __init__(self, eng, sem, start=0):
        self.eng, self.sem, self.start, self.n = eng, sem, start, 0

    def then(self, ins):
        self.n += 1
        ins.then_inc(self.sem, 1)
        self.eng.wait_ge(self.sem, self.start + self.n)


def audio_tower_kernel(nc, x, W1, b1, W2, b2, gamma, beta, qkv_w, WO, sh_up, sh_down, rt_up, rt_down, router_w, out):
    B, L, D = x.shape
    STRIDE, FRAMES = 4, 8
    KF = STRIDE * D
    SL = 1 + (L + STRIDE - (L - FRAMES) % STRIDE - FRAMES) // STRIDE
    FG = SL + 1
    TP = 96
    GPITCH = TP + 2
    HD = W2.shape[1]
    MC = HD // P
    GB = 4
    NG = B // GB
    N = GB * TP
    NT = B * TP
    _, H, _, DH = qkv_w.shape
    NJ = H // 2
    SCALE = 1.0 / (DH * DH * H)
    F = sh_up.shape[2]
    FC = F // P
    E = rt_up.shape[0]
    ET = 256
    SLOTS = (2 * B * SL // ET + E) * ET
    MAXT = -(-B * SL // ET)
    KC = (112, 112, 96)
    KO = (0, 112, 224)

    ln_out = nc.dram_tensor("ln_out", (NG, P, 2, MC * N), F32).ap()
    slots_x = nc.dram_tensor("slots_x", (SLOTS, HD), F32).ap()
    slots_y = nc.dram_tensor("slots_y", (SLOTS, HD), F32).ap()
    base = nc.dram_tensor("base", (NG, TP, GB * HD), F32).ap()

    with ExitStack() as ctx:
        def sb(c, name, shape, dt=F32):
            return c.enter_context(nc.sbuf_tensor(name, shape, dt))

        def ps(c, name, shape, dt=F32):
            return c.enter_context(nc.psum_tensor(name, shape, dt))

        def sem(c, name):
            return c.enter_context(nc.semaphore(name))

        hT = sb(ctx, "hT", [P, MC, NT])
        wA = sb(ctx, "wA", [P, 2, 4096], F32R)
        wB = sb(ctx, "wB", [P, 2, 4096], F32R)
        ident = sb(ctx, "ident", [P, P])
        mean_w = sb(ctx, "mean_w", [P, P])
        eps_c = sb(ctx, "eps_c", [P, 1])
        zero_c = sb(ctx, "zero_c", [P, 1])
        bn_scale = sb(ctx, "bn_scale", [P, MC])
        bn_shift = sb(ctx, "bn_shift", [P, MC])
        top_p = sb(ctx, "top_p", [TP, B, 8])
        slot = sb(ctx, "slot", [TP, 2, B], U32)
        tiles_i = sb(ctx, "tiles_i", [TP, 2, E], I32)

        gcols = lambda g: bass.ds(g * N, N)

        with ExitStack() as c:
            raw_s = sb(c, "raw_s", [P, 2048])
            raw_w = sb(c, "raw_w", [P, 4096])
            w1 = sb(c, "w1", [P, 2, 6, HD], F32R)
            w2 = sb(c, "w2", [P, 2, MC, HD], F32R)
            b1c = sb(c, "b1c", [P, MC])
            b2c = sb(c, "b2c", [P, MC])
            gam = sb(c, "gam", [P, MC])
            bet = sb(c, "bet", [P, MC])
            frames = sb(c, "frames", [FG, GB, KF])
            grp = sb(c, "grp", [112, 2, 3, GB, GPITCH], F32R)
            t1 = sb(c, "t1", [P, MC, N])
            t1s = sb(c, "t1s", [P, 2, MC, N], F32R)
            stats = sb(c, "stats", [P, MC, NG, 6])
            mv = sb(c, "mv", [P, MC, 2])
            std = sb(c, "std", [P, MC])
            tr_ps = ps(c, "tr_ps", [112, 2, 4, P])
            l1_ps = ps(c, "l1_ps", [P, MC, 512])
            l2_ps = ps(c, "l2_ps", [P, MC, 512])

            ident_zero = sem(c, "ident_zero")
            consts = sem(c, "consts")
            pads = sem(c, "pads")
            w12_in = sem(c, "w12_in")
            vec_in = sem(c, "vec_in")
            w12_split = sem(c, "w12_split")
            attn_raw = sem(c, "attn_raw")
            attn_hi = sem(c, "attn_hi")
            attn_split = sem(c, "attn_split")
            x_in = sem(c, "x_in")
            turned = sem(c, "turned")
            grp_hi = sem(c, "grp_hi")
            grp_lo = sem(c, "grp_lo")
            l1_done = sem(c, "l1_done")
            l1_relu = sem(c, "l1_relu")
            l1_hi = sem(c, "l1_hi")
            l1_split = sem(c, "l1_split")
            l2_done = sem(c, "l2_done")
            l2_relu = sem(c, "l2_relu")
            bn_seen = sem(c, "bn_seen")
            bn_var = sem(c, "bn_var")
            bn_std = sem(c, "bn_std")
            v_chain = sem(c, "v_chain")

            block = c.enter_context(nc.Block())

            @block.sync
            def _(sp):
                def load_frames(g):
                    sp.dma_start(frames[0:SL, :, :],
                                 x[bass.ds(g * GB, GB), 0:SL * STRIDE, :].rearrange("b (s f) d -> s b (f d)", f=STRIDE)
                                 ).then_inc(x_in, 16)
                    rest = L - SL * STRIDE
                    sp.dma_start(frames[SL:FG, :, 0:rest * D],
                                 x[bass.ds(g * GB, GB), SL * STRIDE:L, :].rearrange("b f d -> b (f d)").unsqueeze(0)
                                 ).then_inc(x_in, 16)

                sp.wait_ge(pads, 2)
                load_frames(0)
                for s in range(2):
                    for q in range(3):
                        sp.dma_start(raw_s[0:KC[q], (3 * s + q) * HD:(3 * s + q + 1) * HD],
                                     W1[s * KF + KO[q]:s * KF + KO[q] + KC[q], :]).then_inc(w12_in, 16)
                sp.dma_start(raw_s[:, 6 * HD:8 * HD].rearrange("p (c n) -> p c n", c=MC),
                             W2.rearrange("(c p) n -> p c n", p=P)).then_inc(w12_in, 16)
                for v, t in ((b1, b1c), (b2, b2c), (gamma, gam), (beta, bet)):
                    sp.dma_start(t[:, :].unsqueeze(2), v.rearrange("(c p o) -> p c o", p=P, o=1),
                                 allow_slow_non_contiguous=True).then_inc(vec_in, 16)
                for t in range(2):
                    for m in range(MC):
                        sp.dma_start(raw_w[:, m * 2048 + t * 1024:m * 2048 + (t + 1) * 1024].rearrange("p (h d) -> p h d", h=H),
                                     qkv_w[t, :, m * P:(m + 1) * P, :].rearrange("h p d -> p h d")).then_inc(attn_raw, 16)
                for g in range(1, 2):
                    sp.wait_ge(turned, GB * g)
                    load_frames(g)
                sp.wait_ge(attn_split, 1)
                for m in range(MC):
                    sp.dma_start(raw_w[:, m * 1024:(m + 1) * 1024].rearrange("p (h d) -> p h d", h=H),
                                 qkv_w[2, :, m * P:(m + 1) * P, :].rearrange("h p d -> p h d")).then_inc(attn_raw, 16)
                for hh in range(2):
                    sp.dma_start(raw_w[hh * DH:(hh + 1) * DH, 2048:4096].rearrange("p (j n) -> p j n", j=NJ),
                                 WO[0].rearrange("(d j hh) n -> hh d j n", hh=2, j=NJ)[hh]).then_inc(attn_raw, 16)
                with sp.Fori(2, NG) as g:
                    sp.wait_ge(turned, g * GB)
                    load_frames(g)

            @block.gpsimd
            def _(pool):
                pool.memset(frames[:, :, (STRIDE - 1) * D:KF], 0.0).then_inc(pads, 1)
                pool.memset(grp[:, :, :, :, :].bitcast(F32), 0.0).then_inc(pads, 1)
                pool.memset(ident[:, :], 0.0).then_inc(ident_zero, 1)
                pool.wait_ge(ident_zero, 1)
                pool.affine_select(out=ident[:, :], in_=ident[:, :], compare_op=ALU.not_equal, fill=1.0, base=0,
                                   pattern=[[-1, P]], channel_multiplier=1).then_inc(consts, 1)
                pool.memset(mean_w[:, :], 1.0 / HD).then_inc(consts, 1)
                pool.memset(eps_c[:, :], EPS).then_inc(consts, 1)
                pool.memset(zero_c[:, :], 0.0).then_inc(consts, 1)
                pool.wait_ge(consts, 4)
                for t, w in ((0, wA), (1, wB)):
                    pool.wait_ge(attn_raw, 64 * (t + 1))
                    for q in range(4):
                        cols = slice(q * 1024, (q + 1) * 1024)
                        pool.tensor_tensor(w[:, HI, cols], raw_w[:, cols], zero_c[:, 0:1].broadcast_to([P, 1024]), ALU.add).then_inc(attn_hi, 1)
                        pool.wait_ge(attn_hi, 4 * t + q + 1)
                        ins = pool.tensor_tensor(w[:, LO, cols], raw_w[:, cols], w[:, HI, cols], ALU.subtract)
                    ins.then_inc(attn_split, 1)
                pool.wait_ge(attn_split, 2)

            @block.tensor
            def _(pe):
                def turn(g):
                    pe.wait_ge(x_in, (g + 1) * 32)
                    for b in range(GB):
                        if b >= 2 or not (isinstance(g, int) and g == 0):
                            pe.wait_ge(grp_lo, g * GB + (b - 1))
                        for q in range(3):
                            ins = pe.transpose(tr_ps[0:KC[q], b % 2, q, 0:FG], frames[:, b, KO[q]:KO[q] + KC[q]],
                                               ident[0:FG, 0:FG])
                        ins.then_inc(turned, 1)

                def layer1(g):
                    pe.wait_ge(grp_lo, g * GB + GB)
                    for m in range(MC):
                        k = 0
                        for s in range(2):
                            for q in range(3):
                                for wp, dp in PASSES:
                                    ins = pe.matmul(l1_ps[:, m, 0:N], w1[0:KC[q], wp, 3 * s + q, m * P:(m + 1) * P],
                                                    grp[0:KC[q], dp, q, :, s:s + TP], start=(k == 0), stop=(k == 17))
                                    k += 1
                        ins.then_inc(l1_done, 1)

                def layer2(g):
                    pe.wait_ge(l1_split, g * MC + MC)
                    pe.wait_ge(l2_relu, g * MC)
                    for m in range(MC):
                        k = 0
                        for q in range(MC):
                            for wp, dp in PASSES:
                                ins = pe.matmul(l2_ps[:, m, 0:N], w2[:, wp, q, m * P:(m + 1) * P], t1s[:, dp, q, :],
                                                start=(k == 0), stop=(k == 5))
                                k += 1
                        ins.then_inc(l2_done, 1)

                pe.wait_ge(consts, 4)
                turn(0)
                pe.wait_ge(w12_split, 1)
                with pe.Fori(0, NG - 1) as g:
                    layer1(g)
                    turn(g + 1)
                    layer2(g)
                layer1(NG - 1)
                layer2(NG - 1)

            @block.scalar
            def _(act):
                def turned_hi(g):
                    if not (isinstance(g, int) and g == 0):
                        act.wait_ge(l1_done, g * MC)
                    for b in range(GB):
                        act.wait_ge(turned, g * GB + (b + 1))
                        act.activation(grp[0:112, HI, 0:2, b, 0:FG], tr_ps[0:112, b % 2, 0:2, 0:FG], ACT.Copy)
                        act.activation(grp[0:96, HI, 2, b, 0:FG], tr_ps[0:96, b % 2, 2, 0:FG], ACT.Copy
                                       ).then_inc(grp_hi, 1)

                def relu1(g):
                    act.wait_ge(l1_split, g * MC)
                    for m in range(MC):
                        act.wait_ge(l1_done, g * MC + (m + 1))
                        act.activation(t1[:, m, :], l1_ps[:, m, 0:N], ACT.Relu, bias=b1c[:, m:m + 1]).then_inc(l1_relu, 1)

                def relu2(g):
                    for m in range(MC):
                        act.wait_ge(l2_done, g * MC + (m + 1))
                        act.activation(hT[:, m, gcols(g)], l2_ps[:, m, 0:N], ACT.Relu, bias=b2c[:, m:m + 1]
                                       ).then_inc(l2_relu, 1)

                act.wait_ge(pads, 2)
                turned_hi(0)
                act.wait_ge(vec_in, 64)
                with act.Fori(0, NG - 1) as g:
                    relu1(g)
                    turned_hi(g + 1)
                    relu2(g)
                relu1(NG - 1)
                relu2(NG - 1)
                act.wait_ge(bn_var, 1)
                act.activation(std[:, :], mv[:, :, 1], ACT.Sqrt, bias=eps_c[:, :]).then_inc(bn_std, 1)

            @block.vector
            def _(dve):
                def turned_lo(g):
                    for b in range(GB):
                        dve.wait_ge(grp_hi, g * GB + (b + 1))
                        dve.tensor_tensor(grp[0:112, LO, 0:2, b, 0:FG], tr_ps[0:112, b % 2, 0:2, 0:FG],
                                          grp[0:112, HI, 0:2, b, 0:FG], ALU.subtract)
                        dve.tensor_tensor(grp[0:96, LO, 2, b, 0:FG], tr_ps[0:96, b % 2, 2, 0:FG],
                                          grp[0:96, HI, 2, b, 0:FG], ALU.subtract).then_inc(grp_lo, 1)

                def split1(g):
                    dve.wait_ge(l2_done, g * MC)
                    for m in range(MC):
                        dve.wait_ge(l1_relu, g * MC + (m + 1))
                        dve.tensor_copy(t1s[:, HI, m, :], t1[:, m, :]).then_inc(l1_hi, 1)
                        dve.wait_ge(l1_hi, g * MC + (m + 1))
                        dve.tensor_tensor(t1s[:, LO, m, :], t1[:, m, :], t1s[:, HI, m, :], ALU.subtract
                                          ).then_inc(l1_split, 1)

                def count(g):
                    for m in range(MC):
                        dve.wait_ge(l2_relu, g * MC + (m + 1))
                        dve.bn_stats(stats[:, m, bass.ds(g, 1), :].rearrange("p o s -> p (o s)"),
                                     hT[:, m, gcols(g)].rearrange("p (b t) -> p b t", b=GB)[:, :, 0:SL]
                                     ).then_inc(bn_seen, 1)

                dve.wait_ge(w12_in, 7 * 16)
                chain = Chain(dve, v_chain)
                for q in range(6):
                    dve.tensor_copy(w1[0:KC[q % 3], HI, q, :], raw_s[0:KC[q % 3], q * HD:(q + 1) * HD])
                w2raw = raw_s[:, 6 * HD:8 * HD].rearrange("p (c n) -> p c n", c=MC)
                chain.then(dve.tensor_copy(w2[:, HI, :, :], w2raw))
                for q in range(6):
                    dve.tensor_tensor(w1[0:KC[q % 3], LO, q, :], raw_s[0:KC[q % 3], q * HD:(q + 1) * HD],
                                      w1[0:KC[q % 3], HI, q, :], ALU.subtract)
                dve.tensor_tensor(w2[:, LO, :, :], w2raw, w2[:, HI, :, :], ALU.subtract).then_inc(w12_split, 1)
                dve.wait_ge(pads, 2)
                turned_lo(0)
                with dve.Fori(0, NG - 1) as g:
                    split1(g)
                    turned_lo(g + 1)
                    count(g)
                split1(NG - 1)
                count(NG - 1)
                dve.wait_ge(bn_seen, NG * MC)
                for m in range(MC):
                    ins = dve.bn_aggr(mv[:, m, :], stats[:, m, :, :].rearrange("p g s -> p (g s)"))
                ins.then_inc(bn_var, 1)
                dve.wait_ge(bn_std, 1)
                chain.then(dve.reciprocal(bn_scale[:, :], std[:, :]))
                dve.wait_ge(vec_in, 64)
                chain.then(dve.tensor_tensor(bn_scale[:, :], bn_scale[:, :], gam[:, :], ALU.mult))
                chain.then(dve.tensor_tensor(bn_shift[:, :], mv[:, :, 0], bn_scale[:, :], ALU.mult))
                chain.then(dve.tensor_tensor(bn_shift[:, :], bet[:, :], bn_shift[:, :], ALU.subtract))

        def layernorm(second):
            tag = "ln2_" if second else "ln1_"
            c = ExitStack()
            dev = sb(c, tag + "dev", [P, MC, NT])
            sq = sb(c, tag + "sq", [P, MC, N])
            std = sb(c, tag + "std", [P, N])
            rstd = sb(c, tag + "rstd", [P, N])
            xn = sb(c, tag + "xn", [P, MC, N])
            split = sb(c, tag + "split", [P, 2, MC, N], F32R)
            mean_ps = ps(c, tag + "mean", [P, 512])
            var_ps = ps(c, tag + "var", [P, 512])
            affine = sem(c, tag + "affine")
            mean_done = sem(c, tag + "mean_done")
            dev_done = sem(c, tag + "dev_done")
            sq_done = sem(c, tag + "sq_done")
            var_done = sem(c, tag + "var_done")
            std_done = sem(c, tag + "std_done")
            rstd_done = sem(c, tag + "rstd_done")
            xn_done = sem(c, tag + "xn_done")
            hi_done = sem(c, tag + "hi_done")
            lo_done = sem(c, tag + "lo_done")
            stored = sem(c, tag + "stored")
            if second:
                raw = sb(c, "ln2_raw", [P, 4096])
                rw = sb(c, "rw", [P, MC, P])
                lgT = sb(c, "lgT", [P, N])
                lg_ps = ps(c, "lg_ps", [P, 512])
                lgt_ps = ps(c, "lgt_ps", [TP, GB, P])
                xt_ps = ps(c, "xt_ps", [TP, 2, 2, HD])
                rw_zero = sem(c, "rw_zero")
                rw_in = sem(c, "rw_in")
                sh_raw = sem(c, "sh_raw")
                sh_hi = sem(c, "sh_hi")
                sh_split = sem(c, "sh_split")
                added = sem(c, "added")
                lg_done = sem(c, "lg_done")
                lg_out = sem(c, "lg_out")
                lgt_done = sem(c, "lgt_done")
                lgt_out = sem(c, "lgt_out")
                xt_done = sem(c, "xt_done")
                xt_out = sem(c, "xt_out")
            block = c.enter_context(nc.Block())

            @block.sync
            def _(sp):
                if second:
                    sp.wait_ge(rw_zero, 1)
                    sp.dma_start(rw[:, :, 0:E], router_w.rearrange("(c p) e -> p c e", p=P)).then_inc(rw_in, 16)
                    sp.dma_start(raw[:, 0:2048].rearrange("p (c n) -> p c n", c=MC),
                                 sh_up[0].rearrange("(c p) n -> p c n", p=P)).then_inc(sh_raw, 16)
                    sp.dma_start(raw[:, 2048:4096].rearrange("p (c n) -> p c n", c=FC),
                                 sh_down[0].rearrange("(c p) n -> p c n", p=P)).then_inc(sh_raw, 16)
                with sp.Fori(0, NG) as g:
                    sp.wait_ge(lo_done, g + 1)
                    sp.dma_start(ln_out[bass.ds(g, 1)].rearrange("o p s n -> p (o s) n"),
                                 split[:, :, :, :].rearrange("p s m n -> p s (m n)").bitcast(F32)).then_inc(stored, 16)
                sp.wait_ge(stored, NG * 16)

            @block.tensor
            def _(pe):
                def mean(g):
                    if second:
                        if not (isinstance(g, int) and g == 0):
                            pe.wait_ge(dev_done, g)
                    else:
                        pe.wait_ge(affine, g + 1)
                        if not (isinstance(g, int) and g == 0):
                            pe.wait_ge(dev_done, g)
                    for m in range(MC):
                        ins = pe.matmul(mean_ps[:, 0:N], mean_w[:, :], hT[:, m, gcols(g)], start=(m == 0), stop=(m == 1))
                    ins.then_inc(mean_done, 1)

                def var(g):
                    pe.wait_ge(sq_done, g + 1)
                    pe.wait_ge(std_done, g)
                    for m in range(MC):
                        ins = pe.matmul(var_ps[:, 0:N], mean_w[:, :], sq[:, m, :], start=(m == 0), stop=(m == 1))
                    ins.then_inc(var_done, 1)

                def route(g):
                    pe.wait_ge(xn_done, g + 1)
                    pe.wait_ge(lg_out, g)
                    for m in range(MC):
                        ins = pe.matmul(lg_ps[:, 0:N], rw[:, m, :], xn[:, m, :], start=(m == 0), stop=(m == 1))
                    ins.then_inc(lg_done, 1)
                    pe.wait_ge(xt_out, g * 2)
                    for r in range(2):
                        for q in range(2):
                            for m in range(MC):
                                b = 2 * r + q
                                ins = pe.transpose(xt_ps[:, r, q, m * P:(m + 1) * P], xn[:, m, b * TP:(b + 1) * TP],
                                                   ident[:, :])
                        ins.then_inc(xt_done, 1)
                    pe.wait_ge(lg_out, g + 1)
                    pe.wait_ge(lgt_out, g)
                    for b in range(GB):
                        ins = pe.transpose(lgt_ps[:, b, :], lgT[:, b * TP:(b + 1) * TP], ident[:, :])
                    ins.then_inc(lgt_done, 1)

                if second:
                    pe.wait_ge(rw_in, 16)
                mean(0)
                with pe.Fori(0, NG - 1) as g:
                    mean(g + 1)
                    var(g)
                    if second:
                        route(g)
                var(NG - 1)
                if second:
                    route(NG - 1)

            @block.scalar
            def _(act):
                def normalise_batch(g):
                    for m in range(MC):
                        ins = act.activation(hT[:, m, gcols(g)], hT[:, m, gcols(g)], ACT.Identity,
                                             bias=bn_shift[:, m:m + 1], scale=bn_scale[:, m:m + 1])
                    ins.then_inc(affine, 1)

                def square(g):
                    act.wait_ge(dev_done, g + 1)
                    if not (isinstance(g, int) and g == 0):
                        act.wait_ge(var_done, g)
                    act.activation(sq[:, :, :], dev[:, :, gcols(g)], ACT.Square).then_inc(sq_done, 1)

                def root(g):
                    act.wait_ge(var_done, g + 1)
                    act.wait_ge(rstd_done, g)
                    act.activation(std[:, :], var_ps[:, 0:N], ACT.Sqrt, bias=eps_c[:, :]).then_inc(std_done, 1)

                def hi(g):
                    act.wait_ge(xn_done, g + 1)
                    act.wait_ge(stored, g * 16)
                    act.activation(split[:, HI, :, :], xn[:, :, :], ACT.Copy).then_inc(hi_done, 1)
                    if second:
                        act.wait_ge(lg_done, g + 1)
                        act.activation(lgT[:, :], lg_ps[:, 0:N], ACT.Copy).then_inc(lg_out, 1)
                        for r in range(2):
                            act.wait_ge(xt_done, g * 2 + (r + 1))
                            act.activation(x_rows[:, bass.ds(g * GB + 2 * r, 2), :], xt_ps[:, r, :, :], ACT.Copy
                                           ).then_inc(xt_out, 1)

                if not second:
                    normalise_batch(0)
                    normalise_batch(1)
                square(0)
                with act.Fori(0, NG - 2) as g:
                    if not second:
                        normalise_batch(g + 2)
                    root(g)
                    square(g + 1)
                    hi(g)
                root(NG - 2)
                square(NG - 1)
                hi(NG - 2)
                root(NG - 1)
                hi(NG - 1)

            @block.vector
            def _(dve):
                def deviation(g):
                    dve.wait_ge(mean_done, g + 1)
                    for m in range(MC):
                        ins = dve.tensor_tensor(dev[:, m, gcols(g)], hT[:, m, gcols(g)], mean_ps[:, 0:N], ALU.subtract)
                    ins.then_inc(dev_done, 1)

                def normalise(g):
                    dve.wait_ge(std_done, g + 1)
                    dve.wait_ge(xn_done, g)
                    dve.reciprocal(rstd[:, :], std[:, :]).then_inc(rstd_done, 1)
                    dve.wait_ge(hi_done, g)
                    if second:
                        dve.wait_ge(xt_done, g * 2)
                        dve.wait_ge(added, g)
                    dve.wait_ge(lo_done, g)
                    dve.wait_ge(rstd_done, g + 1)
                    for m in range(MC):
                        ins = dve.tensor_tensor(xn[:, m, :], dev[:, m, gcols(g)], rstd[:, :], ALU.mult)
                    ins.then_inc(xn_done, 1)

                def lo(g):
                    dve.wait_ge(hi_done, g + 1)
                    dve.tensor_tensor(split[:, LO, :, :], xn[:, :, :], split[:, HI, :, :], ALU.subtract
                                      ).then_inc(lo_done, 1)
                    if second:
                        dve.wait_ge(lgt_done, g + 1)
                        dve.tensor_copy(logits[:, bass.ds(g * GB, GB), :], lgt_ps[:, :, 0:E]).then_inc(lgt_out, 1)

                deviation(0)
                with dve.Fori(0, NG - 1) as g:
                    deviation(g + 1)
                    normalise(g)
                    lo(g)
                normalise(NG - 1)
                lo(NG - 1)

            if second:
                @block.gpsimd
                def _(pool):
                    pool.memset(rw[:, :, :], 0.0).then_inc(rw_zero, 1)
                    pool.wait_ge(sh_raw, 32)
                    for q in range(4):
                        cols = slice(q * 1024, (q + 1) * 1024)
                        pool.tensor_tensor(wB[:, HI, cols], raw[:, cols], zero_c[:, 0:1].broadcast_to([P, 1024]), ALU.add).then_inc(sh_hi, 1)
                        pool.wait_ge(sh_hi, q + 1)
                        pool.tensor_tensor(wB[:, LO, cols], raw[:, cols], wB[:, HI, cols], ALU.subtract)
                    with pool.Fori(0, NG) as g:
                        pool.wait_ge(xn_done, g + 1)
                        pool.tensor_tensor(hT[:, :, gcols(g)], hT[:, :, gcols(g)], xn[:, :, :], ALU.add
                                           ).then_inc(added, 1)

            c.close()

        layernorm(False)

        with ExitStack() as c:
            xg = sb(c, "xg", [P, 2, MC, N], F32R)
            qT = sb(c, "qT", [P, 2, N])
            kB = sb(c, "kB", [P, 2, GB, 2, TP])
            v_rows = sb(c, "v_rows", [TP, GB, H * DH])
            prob = sb(c, "prob", [TP, 4, 4, TP])
            probT = sb(c, "probT", [TP, 2, 4 * TP])
            mx = sb(c, "mx", [TP, 2, 4])
            sm = sb(c, "sm", [TP, 2, 4])
            rc = sb(c, "rc", [TP, 2, 4])
            oT = sb(c, "oT", [P, 2, 2, GB, TP], F32R)
            pj_ps = ps(c, "pj_ps", [P, 2, 512])
            s_ps = ps(c, "s_ps", [TP, 2, 512])
            t_ps = ps(c, "t_ps", [TP, 512])
            o_ps = ps(c, "o_ps", [P, 512])
            y_ps = ps(c, "y_ps", [P, MC, 512])

            zeros = sb(c, "zeros", [P, 8 * HD])
            ring_zero = sem(c, "ring_zero")
            zeros_set = sem(c, "zeros_set")
            cleared = sem(c, "cleared")
            xg_in = sem(c, "xg_in")
            proj = [sem(c, "proj_act"), sem(c, "proj_dve")]
            taken = [sem(c, "taken_act"), sem(c, "taken_dve")]
            scores_done = sem(c, "scores_done")
            max_done = sem(c, "max_done")
            shifted = sem(c, "shifted")
            exp_done = sem(c, "exp_done")
            sum_done = sem(c, "sum_done")
            recip_done = sem(c, "recip_done")
            scaled = sem(c, "scaled")
            turned = sem(c, "p_turned")
            turned_out = sem(c, "p_turned_out")
            pv_done = sem(c, "pv_done")
            o_hi = sem(c, "o_hi")
            o_lo = sem(c, "o_lo")
            wo_done = sem(c, "wo_done")
            wo_added = sem(c, "wo_added")
            block = c.enter_context(nc.Block())

            NU = 2 * NJ
            PG = GB + NJ

            @block.sync
            def _(sp):
                with sp.Fori(0, NG) as g:
                    sp.wait_ge(proj[1], g * PG)
                    sp.dma_start(xg[:, :, :, :].rearrange("p s m n -> p s (m n)").bitcast(F32),
                                 ln_out[bass.ds(g, 1)].rearrange("o p s n -> p (o s) n")).then_inc(xg_in, 16)

            @block.tensor
            def _(pe):
                def project_v(g):
                    pe.wait_ge(xg_in, (g + 1) * 16)
                    for b in range(GB):
                        for n in range(2):
                            pe.wait_ge(taken[n], g * PG + (1 + b))
                            k = 0
                            for m in range(MC):
                                for dp, wp in PASSES:
                                    ins = pe.matmul(pj_ps[0:TP, n, :], xg[:, dp, m, b * TP:(b + 1) * TP],
                                                    wB[:, wp, m * 1024 + n * 512:m * 1024 + (n + 1) * 512],
                                                    start=(k == 0), stop=(k == 5))
                                    k += 1
                            ins.then_inc(proj[n], 1)

                def project_qk(g, j, t):
                    before = GB + j if j else 0
                    if not (isinstance(g, int) and g == 0 and j == 0):
                        pe.wait_ge(taken[t], g * PG + before)
                    k = 0
                    for m in range(MC):
                        for wp, dp in PASSES:
                            at = m * 2048 + t * 1024 + j * P
                            ins = pe.matmul(pj_ps[:, t, 0:N], wA[:, wp, at:at + P], xg[:, dp, m, :],
                                            start=(k == 0), stop=(k == 5))
                            k += 1
                    ins.then_inc(proj[t], 1)

                def scores(g, u):
                    j, half = divmod(u, 2)
                    for t in range(2):
                        pe.wait_ge(taken[t], g * PG + (GB + j + 1 if j else 1))
                    if u >= 2:
                        pe.wait_ge(shifted, g * NU + (u - 1))
                    for i in range(2):
                        b = 2 * half + i
                        ins = pe.matmul(s_ps[:, u % 2, i * 2 * TP:(i + 1) * 2 * TP], qT[:, j % 2, b * TP:(b + 1) * TP],
                                        kB[:, j % 2, b, :, :].rearrange("p h t -> p (h t)"), start=True, stop=True)
                    ins.then_inc(scores_done, 1)

                def turn(g, u):
                    pe.wait_ge(scaled, g * NU + (u + 1))
                    pe.wait_ge(turned_out, g * NU + u)
                    for i in range(4):
                        ins = pe.transpose(t_ps[:, i * TP:(i + 1) * TP], prob[:, u % 4, i, :], ident[0:TP, 0:TP])
                    ins.then_inc(turned, 1)

                def values(g, u):
                    j, half = divmod(u, 2)
                    pe.wait_ge(turned_out, g * NU + (u + 1))
                    pe.wait_ge(o_lo, g * NU + u)
                    for i in range(2):
                        b = 2 * half + i
                        ins = pe.matmul(o_ps[:, i * 2 * TP:(i + 1) * 2 * TP], v_rows[:, b, j * P:(j + 1) * P],
                                        probT[:, u % 2, i * 2 * TP:(i + 1) * 2 * TP], start=True, stop=True)
                    ins.then_inc(pv_done, 1)

                def output(g, j):
                    pe.wait_ge(o_lo, g * NU + 2 * (j + 1))
                    if j == 0:
                        pe.wait_ge(wo_added, g)
                    for m in range(MC):
                        k = 0
                        for wp, dp in PASSES:
                            at = 2048 + j * HD + m * P
                            ins = pe.matmul(y_ps[:, m, 0:N], wB[:, wp, at:at + P],
                                            oT[:, j % 2, dp, :, :].rearrange("p b t -> p (b t)"),
                                            start=(j == 0 and k == 0), stop=(j == NJ - 1 and k == 2))
                            k += 1
                    ins.then_inc(wo_done, 1)

                def group(g, last):
                    project_v(g)
                    for u in range(NU):
                        j, half = divmod(u, 2)
                        if j + 1 < NJ:
                            project_qk(g, j + 1, half)
                        scores(g, u)
                        if u >= 2:
                            turn(g, u - 2)
                        if u >= 3:
                            values(g, u - 3)
                        if u >= 5 and u % 2:
                            output(g, (u - 5) // 2)
                    if not last:
                        pe.wait_ge(xg_in, (g + 2) * 16)
                        project_qk(g + 1, 0, 0)
                        project_qk(g + 1, 0, 1)
                    turn(g, NU - 2)
                    values(g, NU - 3)
                    turn(g, NU - 1)
                    values(g, NU - 2)
                    output(g, NJ - 2)
                    values(g, NU - 1)
                    output(g, NJ - 1)

                pe.wait_ge(xg_in, 16)
                project_qk(0, 0, 0)
                project_qk(0, 0, 1)
                with pe.Fori(0, NG - 1) as g:
                    group(g, False)
                group(NG - 1, True)

            @block.scalar
            def _(act):
                def take_q(g, j):
                    act.wait_ge(proj[0], g * PG + (GB + j + 1 if j else 1))
                    if j >= 2:
                        act.wait_ge(scores_done, g * NU + 2 * (j - 1))
                    elif not (isinstance(g, int) and g == 0):
                        act.wait_ge(scores_done, g * NU + 2 * (j - 1))
                    act.activation(qT[:, j % 2, :], pj_ps[:, 0, 0:N], ACT.Copy).then_inc(taken[0], 1)

                def exps(g, u):
                    act.wait_ge(shifted, g * NU + (u + 1))
                    act.activation(prob[:, u % 4, :, 0:SL], prob[:, u % 4, :, 0:SL], ACT.Exp, scale=SCALE
                                   ).then_inc(exp_done, 1)

                def take_turned(g, u):
                    act.wait_ge(turned, g * NU + (u + 1))
                    if u >= 2:
                        act.wait_ge(pv_done, g * NU + (u - 1))
                    act.activation(probT[:, u % 2, :], t_ps[:, 0:4 * TP], ACT.Copy).then_inc(turned_out, 1)

                def take_o(g, u):
                    j, half = divmod(u, 2)
                    act.wait_ge(pv_done, g * NU + (u + 1))
                    if not half and j >= 2:
                        act.wait_ge(wo_done, g * NJ + (j - 1))
                    o4 = o_ps[:, 0:4 * TP].rearrange("p (b h t) -> p b h t", b=2, h=2)
                    for h in range(2):
                        rows = slice(h * DH, (h + 1) * DH)
                        ins = act.activation(oT[rows, j % 2, HI, 2 * half:2 * half + 2, :], o4[rows, :, h, :], ACT.Copy)
                    ins.then_inc(o_hi, 1)

                def group(g, last):
                    for b in range(GB):
                        act.wait_ge(proj[0], g * PG + (b + 2))
                        act.wait_ge(pv_done, g * NU)
                        act.activation(v_rows[:, b, 0:512], pj_ps[0:TP, 0, :], ACT.Copy).then_inc(taken[0], 1)
                    for u in range(NU):
                        j, half = divmod(u, 2)
                        if j + 1 < NJ and not half:
                            take_q(g, j + 1)
                        exps(g, u)
                        if u >= 2:
                            take_turned(g, u - 2)
                        if u >= 3:
                            take_o(g, u - 3)
                    if not last:
                        take_q(g + 1, 0)
                    take_turned(g, NU - 2)
                    take_o(g, NU - 3)
                    take_turned(g, NU - 1)
                    take_o(g, NU - 2)
                    take_o(g, NU - 1)

                act.wait_ge(ring_zero, 2)
                take_q(0, 0)
                with act.Fori(0, NG - 1) as g:
                    group(g, False)
                group(NG - 1, True)

            @block.vector
            def _(dve):
                def take_k(g, j):
                    dve.wait_ge(proj[1], g * PG + (GB + j + 1 if j else 1))
                    if j >= 2:
                        dve.wait_ge(scores_done, g * NU + 2 * (j - 1))
                    elif not (isinstance(g, int) and g == 0):
                        dve.wait_ge(scores_done, g * NU + 2 * (j - 1))
                    for h in range(2):
                        rows = slice(h * DH, (h + 1) * DH)
                        ins = dve.tensor_copy(kB[rows, j % 2, :, h, :],
                                              pj_ps[rows, 1, 0:N].rearrange("p (b t) -> p b t", b=GB))
                    ins.then_inc(taken[1], 1)

                def shift(g, u):
                    dve.wait_ge(scores_done, g * NU + (u + 1))
                    s4 = s_ps[:, u % 2, 0:4 * TP].rearrange("p (i t) -> p i t", i=4)[:, :, 0:SL]
                    dve.tensor_reduce(mx[:, u % 2, :], s4, AX, ALU.max).then_inc(max_done, 1)
                    if u >= 4:
                        dve.wait_ge(turned, g * NU + (u - 3))
                    dve.wait_ge(max_done, g * NU + (u + 1))
                    dve.tensor_tensor(prob[:, u % 4, :, 0:SL], s4, mx[:, u % 2, :].unsqueeze(2).broadcast_to([TP, 4, SL]),
                                      ALU.subtract).then_inc(shifted, 1)

                def total(g, u):
                    dve.wait_ge(exp_done, g * NU + (u + 1))
                    if u >= 2:
                        dve.wait_ge(scaled, g * NU + (u - 1))
                    dve.tensor_reduce(sm[:, u % 2, :], prob[:, u % 4, :, 0:SL], AX, ALU.add).then_inc(sum_done, 1)
                    dve.wait_ge(sum_done, g * NU + (u + 1))
                    dve.reciprocal(rc[:, u % 2, :], sm[:, u % 2, :]).then_inc(recip_done, 1)

                def take_o(g, u):
                    j, half = divmod(u, 2)
                    dve.wait_ge(o_hi, g * NU + (u + 1))
                    o4 = o_ps[:, 0:4 * TP].rearrange("p (b h t) -> p b h t", b=2, h=2)
                    for h in range(2):
                        rows = slice(h * DH, (h + 1) * DH)
                        clips = slice(2 * half, 2 * half + 2)
                        ins = dve.tensor_tensor(oT[rows, j % 2, LO, clips, :], o4[rows, :, h, :],
                                                oT[rows, j % 2, HI, clips, :], ALU.subtract)
                    ins.then_inc(o_lo, 1)

                def group(g, last):
                    for b in range(GB):
                        dve.wait_ge(proj[1], g * PG + (b + 2))
                        dve.wait_ge(pv_done, g * NU)
                        dve.tensor_copy(v_rows[:, b, 512:1024], pj_ps[0:TP, 1, :]).then_inc(taken[1], 1)
                    for u in range(NU):
                        j, half = divmod(u, 2)
                        if u >= 1:
                            total(g, u - 1)
                        if j + 1 < NJ and half:
                            take_k(g, j + 1)
                        shift(g, u)
                        if u >= 3:
                            take_o(g, u - 3)
                    total(g, NU - 1)
                    if not last:
                        take_k(g + 1, 0)
                    take_o(g, NU - 3)
                    take_o(g, NU - 2)
                    take_o(g, NU - 1)
                    dve.wait_ge(wo_done, g * NJ + NJ)
                    for m in range(MC):
                        ins = dve.tensor_tensor(hT[:, m, gcols(g)], hT[:, m, gcols(g)], y_ps[:, m, 0:N], ALU.add)
                    ins.then_inc(wo_added, 1)

                dve.wait_ge(ring_zero, 2)
                take_k(0, 0)
                with dve.Fori(0, NG - 1) as g:
                    group(g, False)
                group(NG - 1, True)

            @block.gpsimd
            def _(pool):
                pool.memset(kB[:, :, :, :, :], 0.0).then_inc(ring_zero, 1)
                pool.memset(prob[:, :, :, :], 0.0).then_inc(ring_zero, 1)
                pool.memset(zeros[:, :], 0.0).then_inc(zeros_set, 1)
                pool.wait_ge(zeros_set, 1)
                whole = P * 8
                fills = 0
                for t in (slots_x, slots_y):
                    for r0 in range(0, SLOTS, whole):
                        a = min(whole, SLOTS - r0) // P
                        pool.dma_start(t[r0:r0 + a * P, :].rearrange("(p a) n -> p (a n)", p=P), zeros[:, 0:a * HD]
                                       ).then_inc(cleared, 16)
                        fills += 1

                with pool.Fori(0, NG) as g:
                    for u in range(NU):
                        pool.wait_ge(recip_done, g * NU + (u + 1))
                        p = prob[:, u % 4, :, 0:SL]
                        pool.tensor_tensor(p, p, rc[:, u % 2, :].unsqueeze(2).broadcast_to([TP, 4, SL]), ALU.mult
                                           ).then_inc(scaled, 1)
                pool.wait_ge(cleared, fills * 16)

        rout = ExitStack()
        x_rows = sb(rout, "x_rows", [TP, B, HD])
        logits = sb(rout, "logits", [TP, B, E])
        layernorm(True)

        with ExitStack() as c:
            small = [TP, B, E]
            ex = sb(c, "ex", small)
            top_i = sb(c, "top_i", small, U32)
            idx = sb(c, "idx", [TP, B, 2])
            mask = sb(c, "mask", [TP, 2, B, E])
            both = sb(c, "both", small)
            cum = sb(c, "cum", [TP, 2, B, E])
            rank = sb(c, "rank", small)
            pick = sb(c, "pick", [TP, 2, B, E])
            slot_f = sb(c, "slot_f", [TP, 2, B])
            row_mx = sb(c, "row_mx", [TP, B])
            row_sum = sb(c, "row_sum", [TP, B])
            numbers = sb(c, "numbers", [TP, E])
            limits = sb(c, "limits", [TP, MAXT - 1])
            over = sb(c, "over", [TP, E, MAXT - 1])
            tiles_f = sb(c, "tiles_f", [TP, 3, E])
            before_w = sb(c, "before_w", [SL, TP])
            ones_w = sb(c, "ones_w", [SL, TP])
            rank_ps = ps(c, "rank_ps", [TP, B * E])
            tot_ps = ps(c, "tot_ps", [TP, B * E])
            ones_set = sem(c, "ones_set")
            tri_set = sem(c, "tri_set")
            shifted = sem(c, "r_shifted")
            exp_done = sem(c, "r_exp")
            masks_done = sem(c, "masks_done")
            ranks_done = sem(c, "ranks_done")
            v_chain = sem(c, "r_chain")
            block = c.enter_context(nc.Block())

            @block.gpsimd
            def _(pool):
                pool.memset(before_w[:, :], 1.0).then_inc(ones_set, 1)
                pool.memset(ones_w[:, :], 1.0).then_inc(tri_set, 1)
                pool.wait_ge(ones_set, 1)
                pool.affine_select(out=before_w[:, :], in_=before_w[:, :], compare_op=ALU.is_gt, fill=0.0, base=0,
                                   pattern=[[1, TP]], channel_multiplier=-1).then_inc(tri_set, 1)

            @block.scalar
            def _(act):
                act.wait_ge(shifted, 1)
                act.activation(ex[:, :, :], ex[:, :, :], ACT.Exp).then_inc(exp_done, 1)

            @block.tensor
            def _(pe):
                pe.wait_ge(tri_set, 2)
                pe.wait_ge(masks_done, 1)
                m2 = both[0:SL, :, :].rearrange("p b e -> p (b e)")
                pe.matmul(rank_ps[:, :], before_w[:, :], m2, start=True, stop=True)
                pe.matmul(tot_ps[:, :], ones_w[:, :], m2, start=True, stop=True).then_inc(ranks_done, 1)

            @block.vector
            def _(dve):
                ch = Chain(dve, v_chain)
                for e in range(E):
                    dve.memset(numbers[:, e:e + 1], float(e))
                for k in range(MAXT - 1):
                    ins = dve.memset(limits[:, k:k + 1], float(ET * (k + 1)))
                ch.then(ins)
                wide = lambda a: a.unsqueeze(2).broadcast_to(small)
                ch.then(dve.tensor_reduce(row_mx[:, :], logits[:, :, :], AX, ALU.max))
                dve.tensor_tensor(ex[:, :, :], logits[:, :, :], wide(row_mx[:, :]), ALU.subtract).then_inc(shifted, 1)
                dve.wait_ge(exp_done, 1)
                ch.then(dve.tensor_reduce(row_sum[:, :], ex[:, :, :], AX, ALU.add))
                ch.then(dve.reciprocal(row_sum[:, :], row_sum[:, :]))
                ch.then(dve.tensor_tensor(ex[:, :, :], ex[:, :, :], wide(row_sum[:, :]), ALU.mult))
                for b in range(B):
                    ins = dve.max(out=top_p[:, b, :], in_=ex[:, b, :])
                ch.then(ins)
                for b in range(B):
                    ins = dve.max_index(out=top_i[:, b, :], in_max=top_p[:, b, :], in_values=ex[:, b, :])
                ch.then(ins)
                ch.then(dve.tensor_copy(idx[:, :, :], top_i[:, :, 0:2]))
                every = numbers[:, :].unsqueeze(1).broadcast_to(small)
                for k in range(2):
                    ins = dve.tensor_tensor(mask[:, k, :, :], idx[:, :, k:k + 1].broadcast_to(small), every, ALU.is_equal)
                ch.then(ins)
                dve.tensor_tensor(both[:, :, :], mask[:, 0, :, :], mask[:, 1, :, :], ALU.add).then_inc(masks_done, 1)
                dve.wait_ge(ranks_done, 1)
                tot = tot_ps[:, :].rearrange("p (b e) -> p b e", e=E)
                ch.then(dve.tensor_copy(cum[:, 0, :, :], tot))
                step, at = 1, 0
                while step < B:
                    dve.tensor_copy(cum[:, 1 - at, 0:step, :], cum[:, at, 0:step, :])
                    ch.then(dve.tensor_tensor(cum[:, 1 - at, step:B, :], cum[:, at, step:B, :], cum[:, at, 0:B - step, :],
                                              ALU.add))
                    step, at = 2 * step, 1 - at
                full = cum[:, at, :, :]
                count = cum[:, at, B - 1, :]
                ch.then(dve.tensor_tensor(over[:, :, :], count.unsqueeze(2).broadcast_to([TP, E, MAXT - 1]),
                                          limits[:, :].unsqueeze(1).broadcast_to([TP, E, MAXT - 1]), ALU.is_gt))
                ch.then(dve.tensor_reduce(tiles_f[:, 0, :], over[:, :, :], AX, ALU.add))
                ch.then(dve.tensor_scalar(tiles_f[:, 0, :], tiles_f[:, 0, :], 1.0, None, ALU.add))
                ch.then(dve.memset(tiles_f[:, 1, :], 0.0))
                for e in range(1, E):
                    ch.then(dve.tensor_tensor(tiles_f[:, 1, e:e + 1], tiles_f[:, 1, e - 1:e], tiles_f[:, 0, e - 1:e], ALU.add))
                ch.then(dve.tensor_scalar(tiles_f[:, 2, :], tiles_f[:, 1, :], float(ET), None, ALU.mult))
                ch.then(dve.tensor_copy(tiles_i[:, :, :], tiles_f[:, 0:2, :]))
                ch.then(dve.tensor_tensor(rank[:, :, :], full, tot, ALU.subtract))
                ch.then(dve.tensor_tensor(rank[:, :, :], rank[:, :, :], rank_ps[:, :].rearrange("p (b e) -> p b e", e=E),
                                          ALU.add))
                ch.then(dve.tensor_tensor(rank[:, :, :], rank[:, :, :], tiles_f[:, 2, :].unsqueeze(1).broadcast_to(small),
                                          ALU.add))
                for k in range(2):
                    ins = dve.tensor_tensor(pick[:, k, :, :], mask[:, k, :, :], rank[:, :, :], ALU.mult)
                ch.then(ins)
                ch.then(dve.tensor_reduce(slot_f[:, :, :], pick[:, :, :, :], AX, ALU.add))
                ch.then(dve.tensor_copy(slot[:, :, :], slot_f[:, :, :]))

        with ExitStack() as c:
            xg = sb(c, "sx", [P, 2, MC, N], F32R)
            act_f = sb(c, "act_f", [P, 2, N])
            act_s = sb(c, "act_s", [P, 2, FC, N], F32R)
            bg = sb(c, "bg", [P, MC, N])
            b_rows = sb(c, "b_rows", [TP, GB, HD])
            up_ps = ps(c, "up_ps", [P, 4, 512])
            dn_ps = ps(c, "dn_ps", [P, MC, 512])
            bt_ps = ps(c, "bt_ps", [TP, 2, 2, HD])
            xg_in = sem(c, "sx_in")
            up_done = sem(c, "up_done")
            gelu_done = sem(c, "gelu_done")
            act_hi = sem(c, "act_hi")
            act_lo = sem(c, "act_lo")
            dn_done = sem(c, "dn_done")
            summed = sem(c, "summed")
            bt_done = sem(c, "bt_done")
            bt_out = sem(c, "bt_out")
            stored = sem(c, "b_stored")
            scattered = sem(c, "scattered")
            block = c.enter_context(nc.Block())

            @block.gpsimd
            def _(pool):
                for b in range(B):
                    for k in range(2):
                        pool.indirect_dma_start(
                            out=slots_x, out_offset=bass.IndirectOffsetOnAxis(ap=slot[0:SL, k, b:b + 1], axis=0),
                            in_=x_rows[0:SL, b, :], in_offset=None).then_inc(scattered, 16)
                pool.wait_ge(scattered, 2 * B * 16)

            @block.sync
            def _(sp):
                def load(g):
                    sp.dma_start(xg[:, :, :, :].rearrange("p s m n -> p s (m n)").bitcast(F32),
                                 ln_out[bass.ds(g, 1)].rearrange("o p s n -> p (o s) n")).then_inc(xg_in, 16)

                def store(g):
                    sp.wait_ge(bt_out, g * 2 + 2)
                    sp.dma_start(base[bass.ds(g, 1)].rearrange("o p n -> p (o n)"),
                                 b_rows[:, :, :].rearrange("p b n -> p (b n)")).then_inc(stored, 16)

                load(0)
                with sp.Fori(0, NG - 1) as g:
                    sp.wait_ge(up_done, g * FC + FC)
                    load(g + 1)
                    store(g)
                store(NG - 1)
                sp.wait_ge(stored, NG * 16)

            @block.tensor
            def _(pe):
                def turn(g):
                    pe.wait_ge(summed, g + 1)
                    pe.wait_ge(bt_out, g * 2)
                    for r in range(2):
                        for q in range(2):
                            for m in range(MC):
                                b = 2 * r + q
                                ins = pe.transpose(bt_ps[:, r, q, m * P:(m + 1) * P], bg[:, m, b * TP:(b + 1) * TP],
                                                   ident[:, :])
                        ins.then_inc(bt_done, 1)

                def up(g):
                    pe.wait_ge(xg_in, (g + 1) * 16)
                    for f in range(FC):
                        if f >= 4 or not (isinstance(g, int) and g == 0):
                            pe.wait_ge(gelu_done, g * FC + (f - 3))
                        k = 0
                        for m in range(MC):
                            for wp, dp in PASSES:
                                at = m * F + f * P
                                ins = pe.matmul(up_ps[:, f % 4, 0:N], wB[:, wp, at:at + P], xg[:, dp, m, :],
                                                start=(k == 0), stop=(k == 5))
                                k += 1
                        ins.then_inc(up_done, 1)

                def down(g):
                    pe.wait_ge(summed, g)
                    for f in range(FC):
                        pe.wait_ge(act_lo, g * FC + (f + 1))
                        for m in range(MC):
                            for k, (wp, dp) in enumerate(PASSES):
                                at = 2048 + f * HD + m * P
                                ins = pe.matmul(dn_ps[:, m, 0:N], wB[:, wp, at:at + P], act_s[:, dp, f, :],
                                                start=(f == 0 and k == 0), stop=(f == FC - 1 and k == 2))
                    ins.then_inc(dn_done, 1)

                up(0)
                down(0)
                with pe.Fori(1, NG) as g:
                    up(g)
                    turn(g - 1)
                    down(g)
                turn(NG - 1)

            @block.scalar
            def _(act):
                def gelus(g):
                    for f in range(FC):
                        act.wait_ge(up_done, g * FC + (f + 1))
                        if f >= 2 or not (isinstance(g, int) and g == 0):
                            act.wait_ge(act_lo, g * FC + (f - 1))
                        act.activation(act_f[:, f % 2, :], up_ps[:, f % 4, 0:N], ACT.Gelu).then_inc(gelu_done, 1)

                def take_rows(g):
                    act.wait_ge(stored, g * 16)
                    for r in range(2):
                        act.wait_ge(bt_done, g * 2 + (r + 1))
                        act.activation(b_rows[:, 2 * r:2 * r + 2, :], bt_ps[:, r, :, :], ACT.Copy).then_inc(bt_out, 1)

                gelus(0)
                with act.Fori(1, NG) as g:
                    gelus(g)
                    take_rows(g - 1)
                take_rows(NG - 1)

            @block.vector
            def _(dve):
                def splits(g):
                    if not (isinstance(g, int) and g == 0):
                        dve.wait_ge(dn_done, g)
                    for f in range(FC):
                        dve.wait_ge(gelu_done, g * FC + (f + 1))
                        dve.tensor_copy(act_s[:, HI, f, :], act_f[:, f % 2, :]).then_inc(act_hi, 1)
                        dve.wait_ge(act_hi, g * FC + (f + 1))
                        dve.tensor_tensor(act_s[:, LO, f, :], act_f[:, f % 2, :], act_s[:, HI, f, :], ALU.subtract
                                          ).then_inc(act_lo, 1)

                with dve.Fori(0, NG) as g:
                    splits(g)
                    dve.wait_ge(dn_done, g + 1)
                    dve.wait_ge(bt_done, g * 2)
                    for m in range(MC):
                        ins = dve.tensor_tensor(bg[:, m, :], hT[:, m, gcols(g)], dn_ps[:, m, 0:N], ALU.add)
                    ins.then_inc(summed, 1)
        rout.close()

        with ExitStack() as c:
            raw = sb(c, "raw", [P, 4096])
            rows_in = sb(c, "rows_in", [P, 2, HD])
            xs = sb(c, "xs", [P, 2, MC, ET], F32R)
            act_f = sb(c, "ract_f", [P, 2, ET])
            act_s = sb(c, "ract_s", [P, 2, FC, ET], F32R)
            rows_out = sb(c, "rows_out", [P, 2, HD])
            xt_ps = ps(c, "rxt_ps", [P, MC, 2, P])
            up_ps = ps(c, "rup_ps", [P, 4, 512])
            dn_ps = ps(c, "rdn_ps", [P, 2, HD])
            w_in = sem(c, "w_in")
            w_hi = sem(c, "w_hi")
            w_split = sem(c, "w_split")
            w_used = [sem(c, "w_used_a"), sem(c, "w_used_b")]
            rows_loaded = sem(c, "rows_loaded")
            xt_done = sem(c, "rxt_done")
            x_hi = sem(c, "rx_hi")
            x_lo = sem(c, "rx_lo")
            up_done = sem(c, "rup_done")
            gelu_done = sem(c, "rgelu_done")
            act_hi = sem(c, "ract_hi")
            act_lo = sem(c, "ract_lo")
            dn_done = sem(c, "rdn_done")
            y_out = sem(c, "y_out")
            y_stored = sem(c, "y_stored")
            block = c.enter_context(nc.Block())
            weights = (wA, wB)

            def tiles_of(eng, e):
                n = eng.value_load(tiles_i[0:1, 0, bass.ds(e, 1)], min_val=1, max_val=MAXT)
                t0 = eng.value_load(tiles_i[0:1, 1, bass.ds(e, 1)], min_val=0, max_val=E * MAXT)
                return n, t0

            def first_row(n0):
                return nc.s_assert_within(n0 * ET, 0, SLOTS - ET,
                                          skip_runtime_bounds_check_because="the slots hold every expert's tiles")

            @block.gpsimd
            def _(pool):
                with pool.Fori(0, E // 2) as i:
                    for par in range(2):
                        e = i * 2 + par
                        w = weights[par]
                        pool.dma_start(raw[:, 0:2048].rearrange("p (c n) -> p c n", c=MC),
                                       rt_up[bass.ds(e, 1)].rearrange("o (c p) n -> p (o c) n", p=P)).then_inc(w_in, 16)
                        pool.dma_start(raw[:, 2048:4096].rearrange("p (c n) -> p c n", c=FC),
                                       rt_down[bass.ds(e, 1)].rearrange("o (c p) n -> p (o c) n", p=P)).then_inc(w_in, 16)
                        pool.wait_ge(w_in, e * 32 + 32)
                        pool.wait_ge(w_used[par], i)
                        for q in range(4):
                            cols = slice(q * 1024, (q + 1) * 1024)
                            pool.tensor_tensor(w[:, HI, cols], raw[:, cols], zero_c[:, 0:1].broadcast_to([P, 1024]), ALU.add).then_inc(w_hi, 1)
                            pool.wait_ge(w_hi, e * 4 + (q + 1))
                            ins = pool.tensor_tensor(w[:, LO, cols], raw[:, cols], w[:, HI, cols], ALU.subtract)
                        ins.then_inc(w_split, 1)
                        pool.wait_ge(w_split, e + 1)

            @block.sync
            def _(sp):
                with sp.Fori(0, E) as e:
                    n, t0 = tiles_of(sp, e)
                    with sp.Fori(0, n) as t:
                        sp.wait_ge(xt_done, t0 + t)
                        sp.dma_start(rows_in[:, :, :],
                                     slots_x[bass.ds(first_row(t0 + t), ET), :].rearrange("(p a) n -> p a n", a=2)
                                     ).then_inc(rows_loaded, 16)

            @block.tensor
            def _(pe):
                def tile(w, e, n0):
                    pe.wait_ge(rows_loaded, n0 * 16 + 16)
                    pe.wait_ge(x_lo, n0)
                    for a in range(2):
                        for m in range(MC):
                            ins = pe.transpose(xt_ps[:, m, a, :], rows_in[:, a, m * P:(m + 1) * P], ident[:, :])
                    ins.then_inc(xt_done, 1)
                    pe.wait_ge(w_split, e + 1)
                    pe.wait_ge(x_lo, n0 + 1)
                    for f in range(FC):
                        pe.wait_ge(gelu_done, n0 * FC + (f - 3) if f >= 3 else n0 * FC)
                        k = 0
                        for m in range(MC):
                            for wp, dp in PASSES:
                                at = m * F + f * P
                                ins = pe.matmul(up_ps[:, f % 4, 0:ET], w[:, wp, at:at + P], xs[:, dp, m, :],
                                                start=(k == 0), stop=(k == 5))
                                k += 1
                        ins.then_inc(up_done, 1)
                    pe.wait_ge(y_out, n0)
                    for a in range(2):
                        k = 0
                        for f in range(FC):
                            if a == 0:
                                pe.wait_ge(act_lo, n0 * FC + (f + 1))
                            for dp, wp in PASSES:
                                at = 2048 + f * HD
                                ins = pe.matmul(dn_ps[:, a, :], act_s[:, dp, f, a * P:(a + 1) * P], w[:, wp, at:at + HD],
                                                start=(k == 0), stop=(k == 3 * FC - 1))
                                k += 1
                    ins.then_inc(dn_done, 1)

                with pe.Fori(0, E // 2) as i:
                    for par in range(2):
                        e = i * 2 + par
                        n, t0 = tiles_of(pe, e)
                        with pe.Fori(0, n) as t:
                            tile(weights[par], e, t0 + t)
                        pe.wait_ge(dn_done, t0 + n)
                        pe.sem_inc(w_used[par], 1)

            @block.scalar
            def _(act):
                with act.Fori(0, E) as e:
                    n, t0 = tiles_of(act, e)
                    with act.Fori(0, n) as t:
                        n0 = t0 + t
                        act.wait_ge(xt_done, n0 + 1)
                        act.wait_ge(up_done, n0 * FC)
                        act.activation(xs[:, HI, :, :], xt_ps[:, :, :, :].rearrange("p m a t -> p m (a t)"), ACT.Copy
                                       ).then_inc(x_hi, 1)
                        for f in range(FC):
                            act.wait_ge(up_done, n0 * FC + (f + 1))
                            act.wait_ge(act_lo, n0 * FC + (f - 1) if f >= 1 else n0 * FC)
                            act.activation(act_f[:, f % 2, :], up_ps[:, f % 4, 0:ET], ACT.Gelu).then_inc(gelu_done, 1)
                        act.wait_ge(dn_done, n0 + 1)
                        act.wait_ge(y_stored, n0 * 16)
                        act.activation(rows_out[:, :, :], dn_ps[:, :, :], ACT.Copy).then_inc(y_out, 1)
                        act.wait_ge(y_out, n0 + 1)
                        act.dma_start(slots_y[bass.ds(first_row(t0 + t), ET), :].rearrange("(p a) n -> p a n", a=2),
                                      rows_out[:, :, :]).then_inc(y_stored, 16)
                    act.wait_ge(y_stored, (t0 + n) * 16)

            @block.vector
            def _(dve):
                with dve.Fori(0, E) as e:
                    n, t0 = tiles_of(dve, e)
                    with dve.Fori(0, n) as t:
                        n0 = t0 + t
                        dve.wait_ge(x_hi, n0 + 1)
                        dve.tensor_tensor(xs[:, LO, :, :], xt_ps[:, :, :, :].rearrange("p m a t -> p m (a t)"),
                                          xs[:, HI, :, :], ALU.subtract).then_inc(x_lo, 1)
                        dve.wait_ge(dn_done, n0)
                        for f in range(FC):
                            dve.wait_ge(gelu_done, n0 * FC + (f + 1))
                            dve.tensor_copy(act_s[:, HI, f, :], act_f[:, f % 2, :]).then_inc(act_hi, 1)
                            dve.wait_ge(act_hi, n0 * FC + (f + 1))
                            dve.tensor_tensor(act_s[:, LO, f, :], act_f[:, f % 2, :], act_s[:, HI, f, :], ALU.subtract
                                              ).then_inc(act_lo, 1)

        with ExitStack() as c:
            b_all = sb(c, "b_all", [TP, B, HD])
            y = sb(c, "y", [TP, 2, B, HD])
            b_in = sem(c, "b_in")
            gathered = [sem(c, "gathered_%d" % b) for b in range(B)]
            first = sem(c, "first")
            second = sem(c, "second")
            out_done = sem(c, "out_done")
            block = c.enter_context(nc.Block())

            @block.gpsimd
            def _(pool):
                for b in range(B):
                    for k in range(2):
                        pool.indirect_dma_start(
                            out=y[0:SL, k, b, :], out_offset=None, in_=slots_y,
                            in_offset=bass.IndirectOffsetOnAxis(ap=slot[0:SL, k, b:b + 1], axis=0)
                            ).then_inc(gathered[b], 16)

            @block.vector
            def _(dve):
                dve.wait_ge(b_in, 16)
                for b in range(B):
                    dve.wait_ge(gathered[b], 32)
                    acc = b_all[0:SL, b, :]
                    dve.scalar_tensor_tensor(out=acc, in0=y[0:SL, 0, b, :], scalar=top_p[0:SL, b, 0:1], in1=acc,
                                             op0=ALU.mult, op1=ALU.add).then_inc(first, 1)
                    dve.wait_ge(first, b + 1)
                    dve.scalar_tensor_tensor(out=acc, in0=y[0:SL, 1, b, :], scalar=top_p[0:SL, b, 1:2], in1=acc,
                                             op0=ALU.mult, op1=ALU.add).then_inc(second, 1)

            @block.sync
            def _(sp):
                sp.dma_start(b_all[:, :, :].rearrange("p (g b) n -> p g (b n)", g=NG), base.rearrange("g p n -> p g n")
                             ).then_inc(b_in, 16)
                for g in range(NG):
                    sp.wait_ge(second, GB * (g + 1))
                    sp.dma_start(out[GB * g:GB * (g + 1)].rearrange("b s n -> s b n"), b_all[0:SL, GB * g:GB * (g + 1), :]
                                 ).then_inc(out_done, 16)
                sp.wait_ge(out_done, NG * 16)


_INS = ["x", "L0_tok_W1", "L0_tok_b1", "L0_tok_W2", "L0_tok_b2", "L0_tok_gamma", "L0_tok_beta", "L0_attn_kernel",
        "L0_attn_WO", "L0_ffn_shared_up", "L0_ffn_shared_down", "L0_ffn_routed_up", "L0_ffn_routed_down",
        "L0_ffn_router_w"]


def kernel(**inputs):
    import numpy as np
    import concourse.bacc as bacc
    from concourse.bass_utils import run_bass_kernel_spmd

    nc = bacc.Bacc("TRN2", target_bir_lowering=False, num_devices=1)
    arrays, args = {}, []
    for name in _INS:
        a = np.ascontiguousarray(inputs[name])
        arrays[f"in_{name}"] = a
        args.append(nc.dram_tensor(f"in_{name}", a.shape, mybir.dt.from_np(a.dtype), kind="ExternalInput").ap())
    shape = (inputs["x"].shape[0], 93, inputs["L0_tok_W2"].shape[1])
    args.append(nc.dram_tensor("out_0", shape, F32, kind="ExternalOutput").ap())
    audio_tower_kernel(nc, *args)
    r = run_bass_kernel_spmd(nc, [arrays], core_ids=[0])
    return r.results[0]["out_0"]
```

```python
from contextlib import ExitStack

import concourse.bass as bass
from concourse import mybir

ALU = mybir.AluOpType
ACT = mybir.ActivationFunctionType
F32 = mybir.dt.float32
F32R = mybir.dt.float32r
I32 = mybir.dt.int32
U32 = mybir.dt.uint32
AX = mybir.AxisListType.X

P = 128
EPS = 1e-5

HI, LO = 0, 1
PASSES = ((HI, HI), (HI, LO), (LO, HI))


class Chain:

    def __init__(self, eng, sem, start=0):
        self.eng, self.sem, self.start, self.n = eng, sem, start, 0

    def then(self, ins):
        self.n += 1
        ins.then_inc(self.sem, 1)
        self.eng.wait_ge(self.sem, self.start + self.n)


def audio_tower_kernel(nc, x, W1, b1, W2, b2, gamma, beta, qkv_w, WO, sh_up, sh_down, rt_up, rt_down, router_w, out):
    B, L, D = x.shape
    STRIDE, FRAMES = 4, 8
    KF = STRIDE * D
    SL = 1 + (L + STRIDE - (L - FRAMES) % STRIDE - FRAMES) // STRIDE
    FG = SL + 1
    TP = 96
    GPITCH = TP + 2
    HD = W2.shape[1]
    MC = HD // P
    GB = 4
    NG = B // GB
    N = GB * TP
    NT = B * TP
    _, H, _, DH = qkv_w.shape
    NJ = H // 2
    SCALE = 1.0 / (DH * DH * H)
    F = sh_up.shape[2]
    FC = F // P
    E = rt_up.shape[0]
    ET = 256
    SLOTS = (2 * B * SL // ET + E) * ET
    MAXT = -(-B * SL // ET)
    KC = (112, 112, 96)
    KO = (0, 112, 224)

    ln_out = nc.dram_tensor("ln_out", (NG, P, 2, MC * N), F32).ap()
    slots_x = nc.dram_tensor("slots_x", (SLOTS, HD), F32).ap()
    slots_y = nc.dram_tensor("slots_y", (SLOTS, HD), F32).ap()
    base = nc.dram_tensor("base", (NG, TP, GB * HD), F32).ap()

    with ExitStack() as ctx:
        def sb(c, name, shape, dt=F32):
            return c.enter_context(nc.sbuf_tensor(name, shape, dt))

        def ps(c, name, shape, dt=F32):
            return c.enter_context(nc.psum_tensor(name, shape, dt))

        def sem(c, name):
            return c.enter_context(nc.semaphore(name))

        hT = sb(ctx, "hT", [P, MC, NT])
        wA = sb(ctx, "wA", [P, 2, 4096], F32R)
        wB = sb(ctx, "wB", [P, 2, 4096], F32R)
        ident = sb(ctx, "ident", [P, P])
        mean_w = sb(ctx, "mean_w", [P, P])
        eps_c = sb(ctx, "eps_c", [P, 1])
        zero_c = sb(ctx, "zero_c", [P, 1])
        half3_c = sb(ctx, "half3_c", [P, 1])
        bn_scale = sb(ctx, "bn_scale", [P, MC])
        bn_shift = sb(ctx, "bn_shift", [P, MC])
        top_p = sb(ctx, "top_p", [TP, B, 8])
        slot = sb(ctx, "slot", [TP, 2, B], U32)
        tiles_i = sb(ctx, "tiles_i", [TP, 2, E], I32)

        gcols = lambda g: bass.ds(g * N, N)

        with ExitStack() as c:
            raw_s = sb(c, "raw_s", [P, 2048])
            raw_w = sb(c, "raw_w", [P, 4096])
            w1 = sb(c, "w1", [P, 2, 6, HD], F32R)
            w2 = sb(c, "w2", [P, 2, MC, HD], F32R)
            b1c = sb(c, "b1c", [P, MC])
            b2c = sb(c, "b2c", [P, MC])
            gam = sb(c, "gam", [P, MC])
            bet = sb(c, "bet", [P, MC])
            frames = sb(c, "frames", [FG, GB, KF])
            grp = [sb(c, "grp%d" % i, [112, 2, 3, GB, GPITCH], F32R) for i in range(2)]
            t1 = sb(c, "t1", [P, MC, N])
            t1s = sb(c, "t1s", [P, 2, MC, N], F32R)
            stats = sb(c, "stats", [P, MC, NG, 6])
            mv = sb(c, "mv", [P, MC, 2])
            std = sb(c, "std", [P, MC])
            tr_ps = ps(c, "tr_ps", [112, 2, 4, P])
            l1_ps = ps(c, "l1_ps", [P, MC, 512])
            l2_ps = ps(c, "l2_ps", [P, MC, 512])

            ident_zero = sem(c, "ident_zero")
            consts = sem(c, "consts")
            pads = sem(c, "pads")
            w12_in = sem(c, "w12_in")
            vec_in = sem(c, "vec_in")
            w12_split = sem(c, "w12_split")
            attn_raw = sem(c, "attn_raw")
            attn_hi = sem(c, "attn_hi")
            attn_split = sem(c, "attn_split")
            x_in = sem(c, "x_in")
            turned = sem(c, "turned")
            grp_hi = sem(c, "grp_hi")
            grp_lo = sem(c, "grp_lo")
            l1_done = sem(c, "l1_done")
            l1_relu = sem(c, "l1_relu")
            l1_hi = sem(c, "l1_hi")
            l1_split = sem(c, "l1_split")
            l2_done = sem(c, "l2_done")
            l2_relu = sem(c, "l2_relu")
            bn_seen = sem(c, "bn_seen")
            bn_var = sem(c, "bn_var")
            bn_std = sem(c, "bn_std")
            v_chain = sem(c, "v_chain")

            block = c.enter_context(nc.Block())

            def in_pairs(eng, step):
                with eng.Fori(0, NG // 2 - 1) as i:
                    step(i * 2, 0)
                    step(i * 2 + 1, 1)
                step(NG - 2, 0)
                step(NG - 1, 1, more=False)

            @block.sync
            def _(sp):
                def load_frames(g):
                    sp.dma_start(frames[0:SL, :, :],
                                 x[bass.ds(g * GB, GB), 0:SL * STRIDE, :].rearrange("b (s f) d -> s b (f d)", f=STRIDE)
                                 ).then_inc(x_in, 16)
                    rest = L - SL * STRIDE
                    sp.dma_start(frames[SL:FG, :, 0:rest * D],
                                 x[bass.ds(g * GB, GB), SL * STRIDE:L, :].rearrange("b f d -> b (f d)").unsqueeze(0)
                                 ).then_inc(x_in, 16)

                sp.wait_ge(pads, 1)
                load_frames(0)
                for s in range(2):
                    for q in range(3):
                        sp.dma_start(raw_s[0:KC[q], (3 * s + q) * HD:(3 * s + q + 1) * HD],
                                     W1[s * KF + KO[q]:s * KF + KO[q] + KC[q], :]).then_inc(w12_in, 16)
                sp.dma_start(raw_s[:, 6 * HD:8 * HD].rearrange("p (c n) -> p c n", c=MC),
                             W2.rearrange("(c p) n -> p c n", p=P)).then_inc(w12_in, 16)
                for v, t in ((b1, b1c), (b2, b2c), (gamma, gam), (beta, bet)):
                    sp.dma_start(t[:, :].unsqueeze(2), v.rearrange("(c p o) -> p c o", p=P, o=1),
                                 allow_slow_non_contiguous=True).then_inc(vec_in, 16)
                for t in range(2):
                    for m in range(MC):
                        sp.dma_start(raw_w[:, m * 2048 + t * 1024:m * 2048 + (t + 1) * 1024].rearrange("p (h d) -> p h d", h=H),
                                     qkv_w[t, :, m * P:(m + 1) * P, :].rearrange("h p d -> p h d")).then_inc(attn_raw, 16)
                for g in range(1, 4):
                    sp.wait_ge(turned, GB * g)
                    load_frames(g)
                sp.wait_ge(attn_split, 1)
                for m in range(MC):
                    sp.dma_start(raw_w[:, m * 1024:(m + 1) * 1024].rearrange("p (h d) -> p h d", h=H),
                                 qkv_w[2, :, m * P:(m + 1) * P, :].rearrange("h p d -> p h d")).then_inc(attn_raw, 16)
                for hh in range(2):
                    sp.dma_start(raw_w[hh * DH:(hh + 1) * DH, 2048:4096].rearrange("p (j n) -> p j n", j=NJ),
                                 WO[0].rearrange("(d j hh) n -> hh d j n", hh=2, j=NJ)[hh]).then_inc(attn_raw, 16)
                with sp.Fori(4, NG) as g:
                    sp.wait_ge(turned, g * GB)
                    load_frames(g)

            @block.gpsimd
            def _(pool):
                pool.memset(frames[:, :, (STRIDE - 1) * D:KF], 0.0).then_inc(pads, 1)
                for t in grp:
                    pool.memset(t[:, :, :, :, :].bitcast(F32), 0.0).then_inc(pads, 1)
                pool.memset(ident[:, :], 0.0).then_inc(ident_zero, 1)
                pool.wait_ge(ident_zero, 1)
                pool.affine_select(out=ident[:, :], in_=ident[:, :], compare_op=ALU.not_equal, fill=1.0, base=0,
                                   pattern=[[-1, P]], channel_multiplier=1).then_inc(consts, 1)
                pool.memset(mean_w[:, :], 1.0 / HD).then_inc(consts, 1)
                pool.memset(eps_c[:, :], EPS).then_inc(consts, 1)
                pool.memset(zero_c[:, :], 0.0).then_inc(consts, 1)
                pool.memset(half3_c[:, :], 1.5).then_inc(consts, 1)
                pool.wait_ge(consts, 5)
                for t, w in ((0, wA), (1, wB)):
                    pool.wait_ge(attn_raw, 64 * (t + 1))
                    for q in range(4):
                        cols = slice(q * 1024, (q + 1) * 1024)
                        pool.tensor_tensor(w[:, HI, cols], raw_w[:, cols], zero_c[:, 0:1].broadcast_to([P, 1024]), ALU.add).then_inc(attn_hi, 1)
                        pool.wait_ge(attn_hi, 4 * t + q + 1)
                        ins = pool.tensor_tensor(w[:, LO, cols], raw_w[:, cols], w[:, HI, cols], ALU.subtract)
                    ins.then_inc(attn_split, 1)
                pool.wait_ge(attn_split, 2)

            @block.tensor
            def _(pe):
                def turn(g, b):
                    if b == 0:
                        pe.wait_ge(x_in, (g + 1) * 32)
                    if b >= 2 or not (isinstance(g, int) and g == 0):
                        pe.wait_ge(grp_lo, g * GB + (b - 1))
                    for q in range(3):
                        ins = pe.transpose(tr_ps[0:KC[q], b % 2, q, 0:FG], frames[:, b, KO[q]:KO[q] + KC[q]],
                                           ident[0:FG, 0:FG])
                    ins.then_inc(turned, 1)

                def layer1(g, par, m):
                    pe.wait_ge(grp_lo, g * GB + GB)
                    pe.wait_ge(l1_relu, g * MC)
                    k = 0
                    for s in range(2):
                        for q in range(3):
                            for wp, dp in PASSES:
                                ins = pe.matmul(l1_ps[:, m, 0:N], w1[0:KC[q], wp, 3 * s + q, m * P:(m + 1) * P],
                                                grp[par][0:KC[q], dp, q, :, s:s + TP], start=(k == 0), stop=(k == 17))
                                k += 1
                    ins.then_inc(l1_done, 1)

                def layer2(g):
                    pe.wait_ge(l2_relu, g * MC)
                    for q in range(MC):
                        pe.wait_ge(l1_split, g * MC + (q + 1))
                        for m in range(MC):
                            for k, (wp, dp) in enumerate(PASSES):
                                ins = pe.matmul(l2_ps[:, m, 0:N], w2[:, wp, q, m * P:(m + 1) * P], t1s[:, dp, q, :],
                                                start=(q == 0 and k == 0), stop=(q == MC - 1 and k == 2))
                            if q == MC - 1:
                                ins.then_inc(l2_done, 1)

                def step(g, par, more=True):
                    for m in range(MC):
                        layer1(g, par, m)
                        for b in range(2 * m, 2 * m + 2):
                            if more:
                                turn(g + 1, b)
                    layer2(g)

                pe.wait_ge(consts, 5)
                for b in range(GB):
                    turn(0, b)
                pe.wait_ge(w12_split, 1)
                in_pairs(pe, step)

            @block.scalar
            def _(act):
                def turned_hi(g, par, b):
                    act.wait_ge(turned, g * GB + (b + 1))
                    act.activation(grp[par][0:112, HI, 0:2, b, 0:FG], tr_ps[0:112, b % 2, 0:2, 0:FG], ACT.Copy)
                    act.activation(grp[par][0:96, HI, 2, b, 0:FG], tr_ps[0:96, b % 2, 2, 0:FG], ACT.Copy
                                   ).then_inc(grp_hi, 1)

                def relu1(g, m):
                    act.wait_ge(l1_split, g * MC)
                    act.wait_ge(l1_done, g * MC + (m + 1))
                    act.activation(t1[:, m, :], l1_ps[:, m, 0:N], ACT.Relu, bias=b1c[:, m:m + 1]).then_inc(l1_relu, 1)

                def relu2(g):
                    for m in range(MC):
                        act.wait_ge(l2_done, g * MC + (m + 1))
                        act.activation(hT[:, m, gcols(g)], l2_ps[:, m, 0:N], ACT.Relu, bias=b2c[:, m:m + 1]
                                       ).then_inc(l2_relu, 1)

                def step(g, par, more=True):
                    for m in range(MC):
                        relu1(g, m)
                        for b in range(2 * m, 2 * m + 2):
                            if more:
                                turned_hi(g + 1, 1 - par, b)
                    relu2(g)

                act.wait_ge(pads, 3)
                for b in range(GB):
                    turned_hi(0, 0, b)
                act.wait_ge(vec_in, 64)
                in_pairs(act, step)
                act.wait_ge(bn_var, 1)
                act.activation(std[:, :], mv[:, :, 1], ACT.Sqrt, bias=eps_c[:, :]).then_inc(bn_std, 1)

            @block.vector
            def _(dve):
                def turned_lo(g, par, b):
                    dve.wait_ge(grp_hi, g * GB + (b + 1))
                    dve.tensor_tensor(grp[par][0:112, LO, 0:2, b, 0:FG], tr_ps[0:112, b % 2, 0:2, 0:FG],
                                      grp[par][0:112, HI, 0:2, b, 0:FG], ALU.subtract)
                    dve.tensor_tensor(grp[par][0:96, LO, 2, b, 0:FG], tr_ps[0:96, b % 2, 2, 0:FG],
                                      grp[par][0:96, HI, 2, b, 0:FG], ALU.subtract).then_inc(grp_lo, 1)

                def split1(g, m):
                    dve.wait_ge(l2_done, g * MC)
                    dve.wait_ge(l1_relu, g * MC + (m + 1))
                    dve.tensor_copy(t1s[:, HI, m, :], t1[:, m, :]).then_inc(l1_hi, 1)
                    dve.wait_ge(l1_hi, g * MC + (m + 1))
                    dve.tensor_tensor(t1s[:, LO, m, :], t1[:, m, :], t1s[:, HI, m, :], ALU.subtract
                                      ).then_inc(l1_split, 1)

                def count(g):
                    for m in range(MC):
                        dve.wait_ge(l2_relu, g * MC + (m + 1))
                        dve.bn_stats(stats[:, m, bass.ds(g, 1), :].rearrange("p o s -> p (o s)"),
                                     hT[:, m, gcols(g)].rearrange("p (b t) -> p b t", b=GB)[:, :, 0:SL]
                                     ).then_inc(bn_seen, 1)

                def step(g, par, more=True):
                    for m in range(MC):
                        split1(g, m)
                        for b in range(2 * m, 2 * m + 2):
                            if more:
                                turned_lo(g + 1, 1 - par, b)
                    count(g)

                dve.wait_ge(pads, 3)
                for b in range(GB):
                    turned_lo(0, 0, b)
                dve.wait_ge(w12_in, 7 * 16)
                chain = Chain(dve, v_chain)
                for q in range(6):
                    dve.tensor_copy(w1[0:KC[q % 3], HI, q, :], raw_s[0:KC[q % 3], q * HD:(q + 1) * HD])
                w2raw = raw_s[:, 6 * HD:8 * HD].rearrange("p (c n) -> p c n", c=MC)
                chain.then(dve.tensor_copy(w2[:, HI, :, :], w2raw))
                for q in range(6):
                    dve.tensor_tensor(w1[0:KC[q % 3], LO, q, :], raw_s[0:KC[q % 3], q * HD:(q + 1) * HD],
                                      w1[0:KC[q % 3], HI, q, :], ALU.subtract)
                dve.tensor_tensor(w2[:, LO, :, :], w2raw, w2[:, HI, :, :], ALU.subtract).then_inc(w12_split, 1)
                in_pairs(dve, step)
                dve.wait_ge(bn_seen, NG * MC)
                for m in range(MC):
                    ins = dve.bn_aggr(mv[:, m, :], stats[:, m, :, :].rearrange("p g s -> p (g s)"))
                ins.then_inc(bn_var, 1)
                dve.wait_ge(bn_std, 1)
                chain.then(dve.reciprocal(bn_scale[:, :], std[:, :]))
                dve.wait_ge(vec_in, 64)
                chain.then(dve.tensor_tensor(bn_scale[:, :], bn_scale[:, :], gam[:, :], ALU.mult))
                chain.then(dve.tensor_tensor(bn_shift[:, :], mv[:, :, 0], bn_scale[:, :], ALU.mult))
                chain.then(dve.tensor_tensor(bn_shift[:, :], bet[:, :], bn_shift[:, :], ALU.subtract))

        x_rows = sb(ctx, "x_rows", [TP, B, HD])
        logits = sb(ctx, "logits", [TP, B, E])
        raw_sh = ExitStack()
        raw2 = sb(raw_sh, "raw2", [P, 4096])
        raw2_in = sem(ctx, "raw2_in")
        with ExitStack() as c:
            NU = 2 * NJ
            VW = 2 * P
            xg = sb(c, "xg", [P, 2, MC, N], F32R)
            qT = sb(c, "qT", [P, 2, N])
            kB = sb(c, "kB", [P, 2, GB, 2, TP])
            v_rows = sb(c, "v_rows", [TP, 2, GB, VW])
            prob = sb(c, "prob", [TP, 4, 4, TP])
            probT = sb(c, "probT", [TP, 2, 4 * TP])
            mx = sb(c, "mx", [TP, 2, 4])
            sm = sb(c, "sm", [TP, 2, 4])
            rc = sb(c, "rc", [TP, 2, 4])
            oT = sb(c, "oT", [P, 2, 2, GB, TP], F32R)
            dev = [sb(c, "dev%d" % i, [P, MC, N]) for i in range(2)]
            sq = [sb(c, "sq%d" % i, [P, MC, N]) for i in range(2)]
            var = [sb(c, "var%d" % i, [P, N]) for i in range(2)]
            rstd = [sb(c, "rstd%d" % i, [P, N]) for i in range(2)]
            split2 = sb(c, "split2", [P, 2, MC, N], F32R)
            rw = sb(c, "rw", [P, MC, P])
            lgT = sb(c, "lgT", [P, N])
            zeros = sb(c, "zeros", [P, 2 * HD])
            pj_ps = ps(c, "pj_ps", [P, 2, 512])
            s_ps = ps(c, "s_ps", [TP, 2, 512])
            t_ps = ps(c, "t_ps", [TP, 512])
            o_ps = ps(c, "o_ps", [P, 512])
            y_ps = ps(c, "y_ps", [P, MC, 512])

            ring_zero = sem(c, "ring_zero")
            rw_in = sem(c, "rw_in")
            cleared = sem(c, "cleared")
            filled = [sem(c, "filled_act"), sem(c, "filled_dve")]
            taken = [sem(c, "taken_act"), sem(c, "taken_dve")]
            scores_done = sem(c, "scores_done")
            max_done = sem(c, "max_done")
            shifted = sem(c, "shifted")
            exp_done = sem(c, "exp_done")
            sum_done = sem(c, "sum_done")
            recip_done = sem(c, "recip_done")
            scaled = sem(c, "scaled")
            turned = sem(c, "p_turned")
            turned_out = sem(c, "p_turned_out")
            pv_done = sem(c, "pv_done")
            o_hi = sem(c, "o_hi")
            o_lo = sem(c, "o_lo")
            wo_done = sem(c, "wo_done")
            h_added = sem(c, "h_added")
            affine = sem(c, "affine")
            ln = [{k: sem(c, "ln%d_%s" % (i + 1, k)) for k in
                   ("sq", "log", "root", "square", "scaled", "halved", "rstd", "out", "hi", "lo")} for i in range(2)]
            stored = sem(c, "stored")
            kept = sem(c, "kept")
            block = c.enter_context(nc.Block())

            def tiles(kind):
                ahead, behind = kind != "last", kind != "first"
                t = ["q1", "k1", "v00", "v01", "v02", "v03"] + ["mean1"] * ahead + ["q2", "k2", "v10", "v11", "q3", "k3"]
                t += ["var1"] * ahead + ["v12", "v13", "q4", "k4"] + ["mean2"] * behind + ["v20", "v21", "q5", "k5", "v22", "v23"]
                t += ["var2"] * behind + ["q6", "k6", "v30", "v31", "q7", "k7", "v32", "v33"]
                t += ["router", "xt0", "xt1", "logits"] * behind + ["q0", "k0"] * ahead
                return t

            def bank_of(tile):
                if tile[0] == "v" and tile[1].isdigit():
                    return int(tile[2]) % 2
                return 1 if tile[0] == "k" or tile in ("mean1", "mean2", "router", "logits") else 0

            SERIES = {"start": ["mean1", "var1", "q0", "k0"], "drain": ["mean2", "var2", "router", "xt0", "xt1", "logits"]}
            SERIES.update({kind: tiles(kind) for kind in ("first", "middle", "last")})

            def number(g, tile, back=0):
                bank = bank_of(tile)
                series = {kind: [t for t in ts if bank_of(t) == bank] for kind, ts in SERIES.items()}
                size = {kind: len(ts) for kind, ts in series.items()}
                before = size["start"] + size["first"]
                if not isinstance(g, int):
                    return (g - 1) * size["middle"] + (before + series["middle"].index(tile) + 1 - back * size["middle"])
                g -= back
                if g < 0:
                    return series["start"].index(tile) + 1
                if g == 0:
                    return size["start"] + series["first"].index(tile) + 1
                if g < NG - 1:
                    return before + (g - 1) * size["middle"] + series["middle"].index(tile) + 1
                before += (NG - 2) * size["middle"]
                if g == NG - 1:
                    return before + series["last"].index(tile) + 1
                return before + size["last"] + series["drain"].index(tile) + 1

            def ge(eng, s, value):
                if not (isinstance(value, int) and value <= 0):
                    eng.wait_ge(s, value)

            def run(eng, start, group, drain):
                start()
                group(0, False, True)
                with eng.Fori(1, NG - 1) as g:
                    group(g, True, True)
                group(NG - 1, True, False)
                drain()

            @block.sync
            def _(sp):
                sp.wait_ge(ring_zero, 4)
                sp.dma_start(rw[:, :, 0:E], router_w.rearrange("(c p) e -> p c e", p=P)).then_inc(rw_in, 16)
                sp.dma_start(raw2[:, 0:2048].rearrange("p (c n) -> p c n", c=MC),
                             sh_up[0].rearrange("(c p) n -> p c n", p=P)).then_inc(raw2_in, 16)
                sp.dma_start(raw2[:, 2048:4096].rearrange("p (c n) -> p c n", c=FC),
                             sh_down[0].rearrange("(c p) n -> p c n", p=P)).then_inc(raw2_in, 16)
                fills = [t[r0:r0 + ET, :] for t in (slots_x, slots_y) for r0 in range(0, SLOTS, ET)]
                for rows in fills:
                    sp.dma_start(rows.rearrange("(p a) n -> p (a n)", p=P), zeros[:, :]).then_inc(cleared, 16)
                with sp.Fori(0, NG) as g:
                    sp.wait_ge(ln[1]["lo"], g + 1)
                    sp.dma_start(ln_out[bass.ds(g, 1)].rearrange("o p s n -> p (o s) n"),
                                 split2[:, :, :, :].rearrange("p s m n -> p s (m n)").bitcast(F32)).then_inc(stored, 16)
                sp.wait_ge(stored, NG * 16)
                sp.wait_ge(cleared, len(fills) * 16)

            @block.tensor
            def _(pe):
                def begin(g, tile):
                    ge(pe, taken[bank_of(tile)], number(g, tile) - 1)

                def v_tile(g, tile):
                    jj, b = int(tile[1]), int(tile[2])
                    begin(g, tile)
                    k = 0
                    for m in range(MC):
                        for dp, wp in PASSES:
                            at = m * 1024 + jj * VW
                            ins = pe.matmul(pj_ps[0:TP, b % 2, 0:VW], xg[:, dp, m, b * TP:(b + 1) * TP],
                                            wB[:, wp, at:at + VW], start=(k == 0), stop=(k == 5))
                            k += 1
                    ins.then_inc(filled[b % 2], 1)

                def qk_tile(g, tile):
                    t, j = (0, 1)[tile[0] == "k"], int(tile[1])
                    begin(g, tile)
                    k = 0
                    for m in range(MC):
                        for wp, dp in PASSES:
                            at = m * 2048 + t * 1024 + j * P
                            ins = pe.matmul(pj_ps[:, t, 0:N], wA[:, wp, at:at + P], xg[:, dp, m, :],
                                            start=(k == 0), stop=(k == 5))
                            k += 1
                    ins.then_inc(filled[t], 1)

                def mean_tile(g, i, n):
                    tile = "mean%d" % (i + 1)
                    pe.wait_ge(*((affine, n + 1) if i == 0 else (h_added, n + 1)))
                    begin(g, tile)
                    for m in range(MC):
                        ins = pe.matmul(pj_ps[:, 1, 0:N], mean_w[:, :], hT[:, m, gcols(n)], start=(m == 0), stop=(m == 1))
                    ins.then_inc(filled[1], 1)

                def var_tile(g, i, n):
                    tile = "var%d" % (i + 1)
                    pe.wait_ge(ln[i]["sq"], n + 1)
                    begin(g, tile)
                    for m in range(MC):
                        ins = pe.matmul(pj_ps[:, 0, 0:N], mean_w[:, :], sq[i][:, m, :], start=(m == 0), stop=(m == 1))
                    ins.then_inc(filled[0], 1)

                def router_tile(g, n):
                    pe.wait_ge(ln[1]["out"], n + 1)
                    begin(g, "router")
                    for m in range(MC):
                        ins = pe.matmul(pj_ps[:, 1, 0:N], rw[:, m, :], dev[1][:, m, :], start=(m == 0), stop=(m == 1))
                    ins.then_inc(filled[1], 1)

                def rows_tile(g, r, n):
                    begin(g, "xt%d" % r)
                    for q in range(2):
                        for m in range(MC):
                            b = 2 * r + q
                            ins = pe.transpose(pj_ps[0:TP, 0, q * HD + m * P:q * HD + (m + 1) * P],
                                               dev[1][:, m, b * TP:(b + 1) * TP], ident[:, :])
                    ins.then_inc(filled[0], 1)

                def logits_tile(g, n):
                    pe.wait_ge(taken[1], number(g, "router"))
                    begin(g, "logits")
                    for b in range(GB):
                        ins = pe.transpose(pj_ps[0:TP, 1, b * P:(b + 1) * P], lgT[:, b * TP:(b + 1) * TP], ident[:, :])
                    ins.then_inc(filled[1], 1)

                def scores(g, u):
                    j, half = divmod(u, 2)
                    if not half:
                        for t in range(2):
                            pe.wait_ge(taken[t], number(g, "qk"[t] + str(j), back=0 if j else 1))
                    ge(pe, shifted, g * NU + (u - 1))
                    for i in range(2):
                        b = 2 * half + i
                        ins = pe.matmul(s_ps[:, u % 2, i * 2 * TP:(i + 1) * 2 * TP], qT[:, j % 2, b * TP:(b + 1) * TP],
                                        kB[:, j % 2, b, :, :].rearrange("p h t -> p (h t)"), start=True, stop=True)
                    ins.then_inc(scores_done, 1)

                def turn(g, u):
                    ge(pe, turned_out, g * NU + u)
                    pe.wait_ge(scaled, g * NU + (u + 1))
                    for i in range(4):
                        ins = pe.transpose(t_ps[:, i * TP:(i + 1) * TP], prob[:, u % 4, i, :], ident[0:TP, 0:TP])
                    ins.then_inc(turned, 1)

                def values(g, u):
                    j, half = divmod(u, 2)
                    if u % 4 == 0:
                        for b in range(2, 4):
                            pe.wait_ge(taken[b % 2], number(g, "v%d%d" % (j // 2, b)))
                    pe.wait_ge(turned_out, g * NU + (u + 1))
                    ge(pe, o_lo, g * NU + u)
                    for i in range(2):
                        b = 2 * half + i
                        at = (j % 2) * P
                        ins = pe.matmul(o_ps[:, i * 2 * TP:(i + 1) * 2 * TP], v_rows[:, (j // 2) % 2, b, at:at + P],
                                        probT[:, u % 2, i * 2 * TP:(i + 1) * 2 * TP], start=True, stop=True)
                    ins.then_inc(pv_done, 1)

                def output(g, j):
                    pe.wait_ge(o_lo, g * NU + 2 * (j + 1))
                    if j == 0:
                        ge(pe, h_added, g)
                    for m in range(MC):
                        for k, (wp, dp) in enumerate(PASSES):
                            at = 2048 + j * HD + m * P
                            ins = pe.matmul(y_ps[:, m, 0:N], wB[:, wp, at:at + P],
                                            oT[:, j % 2, dp, :, :].rearrange("p b t -> p (b t)"),
                                            start=(j == 0 and k == 0), stop=(j == NJ - 1 and k == 2))
                    ins.then_inc(wo_done, 1)

                def group(g, behind, ahead):
                    V = {0: "00 01", 1: "02 03", 3: "10 11", 5: "12 13", 7: "20 21", 9: "22 23", 11: "30 31", 12: "32 33"}
                    for s in range(NU):
                        scores(g, s)
                        if s % 2 == 0 and s // 2 + 1 < NJ:
                            qk_tile(g, "q%d" % (s // 2 + 1))
                            qk_tile(g, "k%d" % (s // 2 + 1))
                        if s == NU - 1 and behind:
                            logits_tile(g, g - 1)
                        if s == NU - 1 and ahead:
                            pe.wait_ge(ln[0]["lo"], g + 2)
                            qk_tile(g, "q0")
                            qk_tile(g, "k0")
                        for v in V.get(s, "").split():
                            v_tile(g, "v" + v)
                        for lag, what in ((2, turn), (3, values)):
                            if s >= lag:
                                what(g, s - lag)
                            elif behind:
                                what(g - 1, NU + s - lag)
                        if s % 2 and s >= 5:
                            output(g, (s - 5) // 2)
                        elif s in (1, 3) and behind:
                            output(g - 1, NJ - 2 + s // 2)
                        if s == 1 and ahead:
                            mean_tile(g, 0, g + 1)
                        if s == 4 and ahead:
                            var_tile(g, 0, g + 1)
                        if behind:
                            if s == 6:
                                mean_tile(g, 1, g - 1)
                            if s == 9:
                                var_tile(g, 1, g - 1)
                            if s == 13:
                                router_tile(g, g - 1)
                            if s == 14:
                                rows_tile(g, 0, g - 1)
                                rows_tile(g, 1, g - 1)

                def start():
                    pe.wait_ge(rw_in, 16)
                    mean_tile(-1, 0, 0)
                    var_tile(-1, 0, 0)
                    pe.wait_ge(ln[0]["lo"], 1)
                    qk_tile(-1, "q0")
                    qk_tile(-1, "k0")

                def drain():
                    g = NG - 1
                    turn(g, NU - 2)
                    values(g, NU - 3)
                    turn(g, NU - 1)
                    values(g, NU - 2)
                    output(g, NJ - 2)
                    values(g, NU - 1)
                    output(g, NJ - 1)
                    mean_tile(NG, 1, g)
                    var_tile(NG, 1, g)
                    router_tile(NG, g)
                    rows_tile(NG, 0, g)
                    rows_tile(NG, 1, g)
                    logits_tile(NG, g)

                run(pe, start, group, drain)

            @block.scalar
            def _(act):
                def take(g, tile):
                    act.wait_ge(filled[0], number(g, tile))

                def take_q(g, j, n):
                    take(g, "q%d" % j)
                    ge(act, scores_done, n * NU + 2 * (j - 1))
                    act.activation(qT[:, j % 2, :], pj_ps[:, 0, 0:N], ACT.Copy).then_inc(taken[0], 1)

                def take_v(g, tile):
                    jj, b = int(tile[1]), int(tile[2])
                    take(g, tile)
                    ge(act, pv_done, g * NU + 4 * (jj - 1))
                    act.activation(v_rows[:, jj % 2, b, :], pj_ps[0:TP, 0, 0:VW], ACT.Copy).then_inc(taken[0], 1)

                def normalise_batch(n):
                    for m in range(MC):
                        ins = act.activation(hT[:, m, gcols(n)], hT[:, m, gcols(n)], ACT.Identity,
                                             bias=bn_shift[:, m:m + 1], scale=bn_scale[:, m:m + 1])
                    ins.then_inc(affine, 1)

                def square(g, i, n):
                    act.wait_ge(taken[1], number(g, "mean%d" % (i + 1)))
                    ge(act, ln[i]["rstd"], n)
                    act.activation(sq[i][:, :, :], dev[i][:, :, :], ACT.Square).then_inc(ln[i]["sq"], 1)

                def root(g, i, n):
                    take(g, "var%d" % (i + 1))
                    ge(act, ln[i]["scaled"], n)
                    act.activation(var[i][:, :], pj_ps[:, 0, 0:N], ACT.Identity, bias=eps_c[:, :]).then_inc(taken[0], 1)
                    act.wait_ge(taken[0], number(g, "var%d" % (i + 1)))
                    ge(act, ln[i]["out"], n)
                    act.activation(rstd[i][:, :], var[i][:, :], ACT.Ln).then_inc(ln[i]["log"], 1)
                    act.wait_ge(ln[i]["log"], n + 1)
                    act.activation(rstd[i][:, :], rstd[i][:, :], ACT.Exp, scale=-0.5).then_inc(ln[i]["root"], 1)

                def halve(i, n):
                    act.wait_ge(ln[i]["scaled"], n + 1)
                    t = sq[i][:, 0, :]
                    act.activation(t, t, ACT.Identity, bias=half3_c[:, :], scale=-0.5).then_inc(ln[i]["halved"], 1)

                def hi(g, i, n):
                    act.wait_ge(ln[i]["out"], n + 1)
                    if i == 0:
                        for b in range(2):
                            if not (isinstance(g, int) and g < 0):
                                act.wait_ge(filled[b], number(g, "v3%d" % (2 + b)))
                        act.activation(xg[:, HI, :, :], dev[0][:, :, :], ACT.Copy).then_inc(ln[0]["hi"], 1)
                    else:
                        ge(act, stored, n * 16)
                        act.activation(split2[:, HI, :, :], dev[1][:, :, :], ACT.Copy).then_inc(ln[1]["hi"], 1)

                def take_rows(g, r, n):
                    take(g, "xt%d" % r)
                    act.activation(x_rows[:, bass.ds(n * GB + 2 * r, 2), :], pj_ps[0:TP, 0, :].rearrange("p (b n) -> p b n", b=2),
                                   ACT.Copy).then_inc(taken[0], 1)

                def exps(g, u):
                    act.wait_ge(shifted, g * NU + (u + 1))
                    act.activation(prob[:, u % 4, :, 0:SL], prob[:, u % 4, :, 0:SL], ACT.Exp, scale=SCALE
                                   ).then_inc(exp_done, 1)

                def take_turned(g, u):
                    act.wait_ge(turned, g * NU + (u + 1))
                    ge(act, pv_done, g * NU + (u - 1))
                    act.activation(probT[:, u % 2, :], t_ps[:, 0:4 * TP], ACT.Copy).then_inc(turned_out, 1)

                def take_o(g, u):
                    j, half = divmod(u, 2)
                    act.wait_ge(pv_done, g * NU + (u + 1))
                    if not half:
                        ge(act, wo_done, g * NJ + (j - 1))
                    o4 = o_ps[:, 0:4 * TP].rearrange("p (b h t) -> p b h t", b=2, h=2)
                    for h in range(2):
                        rows = slice(h * DH, (h + 1) * DH)
                        ins = act.activation(oT[rows, j % 2, HI, 2 * half:2 * half + 2, :], o4[rows, :, h, :], ACT.Copy)
                    ins.then_inc(o_hi, 1)

                def group(g, behind, ahead):
                    V = {0: "00", 1: "02", 3: "10", 5: "12", 7: "20", 9: "22", 11: "30", 12: "32"}
                    for s in range(NU):
                        if s % 2 == 0 and s // 2 + 1 < NJ:
                            take_q(g, s // 2 + 1, g)
                        if s == NU - 1 and ahead:
                            take_q(g, 0, g + 1)
                        if s in V:
                            take_v(g, "v" + V[s])
                        if s >= 2:
                            take_turned(g, s - 2)
                        elif behind:
                            take_turned(g - 1, NU + s - 2)
                        exps(g, s)
                        if s >= 3:
                            take_o(g, s - 3)
                        elif behind:
                            take_o(g - 1, NU + s - 3)
                        if ahead:
                            if s == 0:
                                normalise_batch(g + 1)
                            if s == 2:
                                square(g, 0, g + 1)
                            if s == 4:
                                root(g, 0, g + 1)
                            if s == 6:
                                halve(0, g + 1)
                            if s == 12:
                                hi(g, 0, g + 1)
                        if behind:
                            if s == 7:
                                square(g, 1, g - 1)
                            if s == 9:
                                root(g, 1, g - 1)
                            if s == 11:
                                halve(1, g - 1)
                            if s == 13:
                                hi(g, 1, g - 1)
                            if s == 14:
                                take_rows(g, 0, g - 1)
                                take_rows(g, 1, g - 1)

                def start():
                    normalise_batch(0)
                    square(-1, 0, 0)
                    root(-1, 0, 0)
                    halve(0, 0)
                    hi(-1, 0, 0)
                    act.wait_ge(ring_zero, 4)
                    take_q(-1, 0, 0)

                def drain():
                    g = NG - 1
                    take_turned(g, NU - 2)
                    take_o(g, NU - 3)
                    take_turned(g, NU - 1)
                    take_o(g, NU - 2)
                    take_o(g, NU - 1)
                    square(NG, 1, g)
                    root(NG, 1, g)
                    halve(1, g)
                    hi(NG, 1, g)
                    take_rows(NG, 0, g)
                    take_rows(NG, 1, g)

                run(act, start, group, drain)

            @block.vector
            def _(dve):
                def take(g, tile):
                    dve.wait_ge(filled[1], number(g, tile))

                def take_k(g, j, n):
                    take(g, "k%d" % j)
                    ge(dve, scores_done, n * NU + 2 * (j - 1))
                    for h in range(2):
                        rows = slice(h * DH, (h + 1) * DH)
                        ins = dve.tensor_copy(kB[rows, j % 2, :, h, :],
                                              pj_ps[rows, 1, 0:N].rearrange("p (b t) -> p b t", b=GB))
                    ins.then_inc(taken[1], 1)

                def take_v(g, tile):
                    jj, b = int(tile[1]), int(tile[2])
                    take(g, tile)
                    ge(dve, pv_done, g * NU + 4 * (jj - 1))
                    dve.tensor_copy(v_rows[:, jj % 2, b, :], pj_ps[0:TP, 1, 0:VW]).then_inc(taken[1], 1)

                def deviation(g, i, n):
                    take(g, "mean%d" % (i + 1))
                    ge(dve, ln[i]["lo"], n)
                    if i == 1:
                        ge(dve, kept, n)
                        if not (isinstance(n, int) and n == 0):
                            dve.wait_ge(filled[0], number(g, "xt1", back=1))
                    for m in range(MC):
                        ins = dve.tensor_tensor(dev[i][:, m, :], hT[:, m, gcols(n)], pj_ps[:, 1, 0:N], ALU.subtract)
                    ins.then_inc(taken[1], 1)

                def normalise(i, n):
                    dve.wait_ge(ln[i]["rstd"], n + 1)
                    for m in range(MC):
                        ins = dve.tensor_tensor(dev[i][:, m, :], dev[i][:, m, :], rstd[i][:, :], ALU.mult)
                    ins.then_inc(ln[i]["out"], 1)

                def lo(i, n):
                    dve.wait_ge(ln[i]["hi"], n + 1)
                    to = (xg, split2)[i]
                    dve.tensor_tensor(to[:, LO, :, :], dev[i][:, :, :], to[:, HI, :, :], ALU.subtract
                                      ).then_inc(ln[i]["lo"], 1)

                def add(n):
                    dve.wait_ge(wo_done, n * NJ + NJ)
                    for m in range(MC):
                        ins = dve.tensor_tensor(hT[:, m, gcols(n)], hT[:, m, gcols(n)], y_ps[:, m, 0:N], ALU.add)
                    ins.then_inc(h_added, 1)

                def take_router(g):
                    take(g, "router")
                    dve.tensor_copy(lgT[:, :], pj_ps[:, 1, 0:N]).then_inc(taken[1], 1)

                def take_logits(g, n):
                    take(g, "logits")
                    dve.tensor_copy(logits[:, bass.ds(n * GB, GB), :],
                                    pj_ps[0:TP, 1, :].rearrange("p (b e) -> p b e", b=GB)[:, :, 0:E]).then_inc(taken[1], 1)

                def shift(g, u):
                    dve.wait_ge(scores_done, g * NU + (u + 1))
                    s4 = s_ps[:, u % 2, 0:4 * TP].rearrange("p (i t) -> p i t", i=4)[:, :, 0:SL]
                    dve.tensor_reduce(mx[:, u % 2, :], s4, AX, ALU.max).then_inc(max_done, 1)
                    ge(dve, turned, g * NU + (u - 3))
                    dve.wait_ge(max_done, g * NU + (u + 1))
                    dve.tensor_tensor(prob[:, u % 4, :, 0:SL], s4, mx[:, u % 2, :].unsqueeze(2).broadcast_to([TP, 4, SL]),
                                      ALU.subtract).then_inc(shifted, 1)

                def total(g, u):
                    dve.wait_ge(exp_done, g * NU + (u + 1))
                    ge(dve, scaled, g * NU + (u - 1))
                    dve.tensor_reduce(sm[:, u % 2, :], prob[:, u % 4, :, 0:SL], AX, ALU.add).then_inc(sum_done, 1)
                    dve.wait_ge(sum_done, g * NU + (u + 1))
                    dve.reciprocal(rc[:, u % 2, :], sm[:, u % 2, :]).then_inc(recip_done, 1)

                def take_o(g, u):
                    j, half = divmod(u, 2)
                    dve.wait_ge(o_hi, g * NU + (u + 1))
                    o4 = o_ps[:, 0:4 * TP].rearrange("p (b h t) -> p b h t", b=2, h=2)
                    for h in range(2):
                        rows = slice(h * DH, (h + 1) * DH)
                        clips = slice(2 * half, 2 * half + 2)
                        ins = dve.tensor_tensor(oT[rows, j % 2, LO, clips, :], o4[rows, :, h, :],
                                                oT[rows, j % 2, HI, clips, :], ALU.subtract)
                    ins.then_inc(o_lo, 1)

                def group(g, behind, ahead):
                    V = {0: "01", 1: "03", 3: "11", 5: "13", 7: "21", 9: "23", 11: "31", 12: "33"}
                    for s in range(NU):
                        shift(g, s)
                        if s % 2 == 0 and s // 2 + 1 < NJ:
                            take_k(g, s // 2 + 1, g)
                        if s >= 1:
                            total(g, s - 1)
                        elif behind:
                            total(g - 1, NU - 1)
                        if s == NU - 1 and behind:
                            take_logits(g, g - 1)
                        if s == NU - 1 and ahead:
                            take_k(g, 0, g + 1)
                        if s in V:
                            take_v(g, "v" + V[s])
                        if s >= 3:
                            take_o(g, s - 3)
                        elif behind:
                            take_o(g - 1, NU + s - 3)
                        if s == 3 and behind:
                            add(g - 1)
                        if ahead:
                            if s == 1:
                                deviation(g, 0, g + 1)
                            if s == 8:
                                normalise(0, g + 1)
                            if s == 12:
                                lo(0, g + 1)
                        if behind:
                            if s == 6:
                                deviation(g, 1, g - 1)
                            if s == 12:
                                normalise(1, g - 1)
                            if s == 13:
                                lo(1, g - 1)
                                take_router(g)

                def start():
                    deviation(-1, 0, 0)
                    normalise(0, 0)
                    lo(0, 0)
                    dve.wait_ge(ring_zero, 4)
                    take_k(-1, 0, 0)

                def drain():
                    g = NG - 1
                    total(g, NU - 1)
                    take_o(g, NU - 3)
                    take_o(g, NU - 2)
                    take_o(g, NU - 1)
                    add(g)
                    deviation(NG, 1, g)
                    normalise(1, g)
                    lo(1, g)
                    take_router(NG)
                    take_logits(NG, g)

                run(dve, start, group, drain)

            @block.gpsimd
            def _(pool):
                def newton(i, n, step):
                    t = sq[i][:, 0, :]
                    if step == 0:
                        pool.wait_ge(ln[i]["root"], n + 1)
                        pool.tensor_tensor(t, rstd[i][:, :], rstd[i][:, :], ALU.mult).then_inc(ln[i]["square"], 1)
                        pool.wait_ge(ln[i]["square"], n + 1)
                        pool.tensor_tensor(t, t, var[i][:, :], ALU.mult).then_inc(ln[i]["scaled"], 1)
                    else:
                        pool.wait_ge(ln[i]["halved"], n + 1)
                        pool.tensor_tensor(rstd[i][:, :], rstd[i][:, :], t, ALU.mult).then_inc(ln[i]["rstd"], 1)

                def keep(n):
                    pool.wait_ge(ln[1]["out"], n + 1)
                    pool.tensor_tensor(hT[:, :, gcols(n)], hT[:, :, gcols(n)], dev[1][:, :, :], ALU.add).then_inc(kept, 1)

                def group(g, behind, ahead):
                    for u in range(NU):
                        pool.wait_ge(recip_done, g * NU + (u + 1))
                        p = prob[:, u % 4, :, 0:SL]
                        pool.tensor_tensor(p, p, rc[:, u % 2, :].unsqueeze(2).broadcast_to([TP, 4, SL]), ALU.mult
                                           ).then_inc(scaled, 1)
                        if ahead:
                            if u == 4:
                                newton(0, g + 1, 0)
                            if u == 6:
                                newton(0, g + 1, 1)
                        if behind:
                            if u == 9:
                                newton(1, g - 1, 0)
                            if u == 11:
                                newton(1, g - 1, 1)
                            if u == 13:
                                keep(g - 1)

                def start():
                    pool.memset(kB[:, :, :, :, :], 0.0).then_inc(ring_zero, 1)
                    pool.memset(prob[:, :, :, :], 0.0).then_inc(ring_zero, 1)
                    pool.memset(rw[:, :, :], 0.0).then_inc(ring_zero, 1)
                    pool.memset(zeros[:, :], 0.0).then_inc(ring_zero, 1)
                    newton(0, 0, 0)
                    newton(0, 0, 1)

                def drain():
                    newton(1, NG - 1, 0)
                    newton(1, NG - 1, 1)
                    keep(NG - 1)

                run(pool, start, group, drain)

        with ExitStack() as c:
            small = [TP, B, E]
            ex = sb(c, "ex", small)
            top_i = sb(c, "top_i", small, U32)
            idx = sb(c, "idx", [TP, B, 2])
            mask = sb(c, "mask", [TP, 2, B, E])
            both = sb(c, "both", small)
            cum = sb(c, "cum", [TP, 2, B, E])
            rank = sb(c, "rank", small)
            pick = sb(c, "pick", [TP, 2, B, E])
            slot_f = sb(c, "slot_f", [TP, 2, B])
            row_mx = sb(c, "row_mx", [TP, B])
            row_sum = sb(c, "row_sum", [TP, B])
            numbers = sb(c, "numbers", [TP, E])
            limits = sb(c, "limits", [TP, MAXT - 1])
            over = sb(c, "over", [TP, E, MAXT - 1])
            tiles_f = sb(c, "tiles_f", [TP, 3, E])
            before_w = sb(c, "before_w", [SL, TP])
            ones_w = sb(c, "ones_w", [SL, TP])
            rank_ps = ps(c, "rank_ps", [TP, B * E])
            tot_ps = ps(c, "tot_ps", [TP, B * E])
            ones_set = sem(c, "ones_set")
            tri_set = sem(c, "tri_set")
            shifted = sem(c, "r_shifted")
            exp_done = sem(c, "r_exp")
            masks_done = sem(c, "masks_done")
            ranks_done = sem(c, "ranks_done")
            v_chain = sem(c, "r_chain")
            w_hi = sem(c, "w01_hi")
            block = c.enter_context(nc.Block())

            @block.gpsimd
            def _(pool):
                pool.memset(before_w[:, :], 1.0).then_inc(ones_set, 1)
                pool.memset(ones_w[:, :], 1.0).then_inc(tri_set, 1)
                pool.wait_ge(ones_set, 1)
                pool.affine_select(out=before_w[:, :], in_=before_w[:, :], compare_op=ALU.is_gt, fill=0.0, base=0,
                                   pattern=[[1, TP]], channel_multiplier=-1).then_inc(tri_set, 1)

            @block.scalar
            def _(act):
                act.wait_ge(raw2_in, 32)
                for q in range(4):
                    cols = slice(q * 1024, (q + 1) * 1024)
                    act.activation(wB[:, HI, cols], raw2[:, cols], ACT.Copy).then_inc(w_hi, 1)
                act.wait_ge(shifted, 1)
                act.activation(ex[:, :, :], ex[:, :, :], ACT.Exp).then_inc(exp_done, 1)

            @block.tensor
            def _(pe):
                pe.wait_ge(tri_set, 2)
                pe.wait_ge(masks_done, 1)
                m2 = both[0:SL, :, :].rearrange("p b e -> p (b e)")
                pe.matmul(rank_ps[:, :], before_w[:, :], m2, start=True, stop=True)
                pe.matmul(tot_ps[:, :], ones_w[:, :], m2, start=True, stop=True).then_inc(ranks_done, 1)

            @block.vector
            def _(dve):
                ch = Chain(dve, v_chain)
                for e in range(E):
                    dve.memset(numbers[:, e:e + 1], float(e))
                for k in range(MAXT - 1):
                    ins = dve.memset(limits[:, k:k + 1], float(ET * (k + 1)))
                ch.then(ins)
                wide = lambda a: a.unsqueeze(2).broadcast_to(small)
                ch.then(dve.tensor_reduce(row_mx[:, :], logits[:, :, :], AX, ALU.max))
                dve.tensor_tensor(ex[:, :, :], logits[:, :, :], wide(row_mx[:, :]), ALU.subtract).then_inc(shifted, 1)
                dve.wait_ge(exp_done, 1)
                ch.then(dve.tensor_reduce(row_sum[:, :], ex[:, :, :], AX, ALU.add))
                ch.then(dve.reciprocal(row_sum[:, :], row_sum[:, :]))
                ch.then(dve.tensor_tensor(ex[:, :, :], ex[:, :, :], wide(row_sum[:, :]), ALU.mult))
                for b in range(B):
                    ins = dve.max(out=top_p[:, b, :], in_=ex[:, b, :])
                ch.then(ins)
                for b in range(B):
                    ins = dve.max_index(out=top_i[:, b, :], in_max=top_p[:, b, :], in_values=ex[:, b, :])
                ch.then(ins)
                ch.then(dve.tensor_copy(idx[:, :, :], top_i[:, :, 0:2]))
                every = numbers[:, :].unsqueeze(1).broadcast_to(small)
                for k in range(2):
                    ins = dve.tensor_tensor(mask[:, k, :, :], idx[:, :, k:k + 1].broadcast_to(small), every, ALU.is_equal)
                ch.then(ins)
                dve.tensor_tensor(both[:, :, :], mask[:, 0, :, :], mask[:, 1, :, :], ALU.add).then_inc(masks_done, 1)
                for q in range(4):
                    cols = slice(q * 1024, (q + 1) * 1024)
                    dve.wait_ge(w_hi, q + 1)
                    dve.tensor_tensor(wB[:, LO, cols], raw2[:, cols], wB[:, HI, cols], ALU.subtract)
                dve.wait_ge(ranks_done, 1)
                tot = tot_ps[:, :].rearrange("p (b e) -> p b e", e=E)
                ch.then(dve.tensor_copy(cum[:, 0, :, :], tot))
                step, at = 1, 0
                while step < B:
                    dve.tensor_copy(cum[:, 1 - at, 0:step, :], cum[:, at, 0:step, :])
                    ch.then(dve.tensor_tensor(cum[:, 1 - at, step:B, :], cum[:, at, step:B, :], cum[:, at, 0:B - step, :],
                                              ALU.add))
                    step, at = 2 * step, 1 - at
                full = cum[:, at, :, :]
                count = cum[:, at, B - 1, :]
                ch.then(dve.tensor_tensor(over[:, :, :], count.unsqueeze(2).broadcast_to([TP, E, MAXT - 1]),
                                          limits[:, :].unsqueeze(1).broadcast_to([TP, E, MAXT - 1]), ALU.is_gt))
                ch.then(dve.tensor_reduce(tiles_f[:, 0, :], over[:, :, :], AX, ALU.add))
                ch.then(dve.tensor_scalar(tiles_f[:, 0, :], tiles_f[:, 0, :], 1.0, None, ALU.add))
                ch.then(dve.memset(tiles_f[:, 1, :], 0.0))
                for e in range(1, E):
                    ch.then(dve.tensor_tensor(tiles_f[:, 1, e:e + 1], tiles_f[:, 1, e - 1:e], tiles_f[:, 0, e - 1:e], ALU.add))
                ch.then(dve.tensor_scalar(tiles_f[:, 2, :], tiles_f[:, 1, :], float(ET), None, ALU.mult))
                ch.then(dve.tensor_copy(tiles_i[:, :, :], tiles_f[:, 0:2, :]))
                ch.then(dve.tensor_tensor(rank[:, :, :], full, tot, ALU.subtract))
                ch.then(dve.tensor_tensor(rank[:, :, :], rank[:, :, :], rank_ps[:, :].rearrange("p (b e) -> p b e", e=E),
                                          ALU.add))
                ch.then(dve.tensor_tensor(rank[:, :, :], rank[:, :, :], tiles_f[:, 2, :].unsqueeze(1).broadcast_to(small),
                                          ALU.add))
                for k in range(2):
                    ins = dve.tensor_tensor(pick[:, k, :, :], mask[:, k, :, :], rank[:, :, :], ALU.mult)
                ch.then(ins)
                ch.then(dve.tensor_reduce(slot_f[:, :, :], pick[:, :, :, :], AX, ALU.add))
                ch.then(dve.tensor_copy(slot[:, :, :], slot_f[:, :, :]))

        raw_sh.close()
        with ExitStack() as c:
            G1 = NG // 2
            YR = 8
            raw = sb(c, "raw", [P, 4096])
            sx = sb(c, "sx", [P, 2, MC, N], F32R)
            rows_in = sb(c, "rows_in", [P, 2, HD])
            rx = sb(c, "rx", [P, 2, MC, ET], F32R)
            act_f = sb(c, "act_f", [P, 2, N])
            act_s = sb(c, "act_s", [P, 2, FC, N], F32R)
            bg = sb(c, "bg", [P, MC, N])
            b_rows = sb(c, "b_rows", [TP, GB, HD])
            rows_out = sb(c, "rows_out", [P, 2, HD])
            fin = sb(c, "fin", [TP, YR, HD])
            up_ps = ps(c, "up_ps", [P, 4, 512])
            dn_ps = ps(c, "dn_ps", [P, MC, 512])
            tr_ps = ps(c, "ftr_ps", [P, 2, 512])

            scattered = sem(c, "scattered")
            sx_in = sem(c, "sx_in")
            up_done = sem(c, "up_done")
            gelu_done = sem(c, "gelu_done")
            act_hi = sem(c, "act_hi")
            act_lo = sem(c, "act_lo")
            dn_done = sem(c, "dn_done")
            summed = sem(c, "summed")
            bt_done = sem(c, "bt_done")
            bt_out = sem(c, "bt_out")
            base_stored = sem(c, "base_stored")
            w0_in = sem(c, "w0_in")
            w0_hi = sem(c, "w0_hi")
            w0_lo = sem(c, "w0_lo")
            w_in = sem(c, "w_in")
            w_hi = sem(c, "w_hi")
            w_split = sem(c, "w_split")
            w_used = [sem(c, "w_used_a"), sem(c, "w_used_b")]
            rows_loaded = sem(c, "rows_loaded")
            xt_done = sem(c, "rxt_done")
            x_hi = sem(c, "rx_hi")
            x_lo = sem(c, "rx_lo")
            rup_done = sem(c, "rup_done")
            rgelu_done = sem(c, "rgelu_done")
            ract_hi = sem(c, "ract_hi")
            ract_lo = sem(c, "ract_lo")
            rdn_done = sem(c, "rdn_done")
            y_out = sem(c, "y_out")
            y_stored = sem(c, "y_stored")
            rows_ready = sem(c, "rows_ready")
            gathered = [sem(c, "gathered_%d" % b) for b in range(YR)]
            base_in = [sem(c, "base_in_%d" % h) for h in range(2)]
            first = sem(c, "first")
            combined = sem(c, "combined")
            out_done = [sem(c, "out_done_%d" % h) for h in range(2)]
            block = c.enter_context(nc.Block())
            weights = (wA, wB)

            def tiles_of(eng, e):
                n = eng.value_load(tiles_i[0:1, 0, bass.ds(e, 1)], min_val=1, max_val=MAXT)
                t0 = eng.value_load(tiles_i[0:1, 1, bass.ds(e, 1)], min_val=0, max_val=SLOTS // ET - 1)
                return n, t0

            def first_row(n0):
                return nc.s_assert_within(n0 * ET, 0, SLOTS - ET,
                                          skip_runtime_bounds_check_because="the slots hold every expert's tiles")

            def y_ring(b, k):
                return x_rows[0:SL, 2 * (b % YR) + k, :]

            @block.gpsimd
            def _(pool):
                for b in range(B):
                    for k in range(2):
                        pool.indirect_dma_start(
                            out=slots_x, out_offset=bass.IndirectOffsetOnAxis(ap=slot[0:SL, k, b:b + 1], axis=0),
                            in_=x_rows[0:SL, b, :], in_offset=None).then_inc(scattered, 16)

                def fetch(n, par, up, down):
                    w = weights[par]
                    pool.dma_start(raw[:, 0:2048].rearrange("p (c n) -> p c n", c=MC), up).then_inc(w_in, 16)
                    pool.dma_start(raw[:, 2048:4096].rearrange("p (c n) -> p c n", c=FC), down).then_inc(w_in, 16)
                    pool.wait_ge(w_in, n * 32)
                    yield
                    for q in range(4):
                        cols = slice(q * 1024, (q + 1) * 1024)
                        pool.tensor_tensor(w[:, HI, cols], raw[:, cols], zero_c[:, 0:1].broadcast_to([P, 1024]), ALU.add
                                           ).then_inc(w_hi, 1)
                        pool.wait_ge(w_hi, (n - 1) * 4 + (q + 1))
                        ins = pool.tensor_tensor(w[:, LO, cols], raw[:, cols], w[:, HI, cols], ALU.subtract)
                    ins.then_inc(w_split, 1)
                    pool.wait_ge(w_split, n + 1)

                def expert_weights(e, par):
                    return (rt_up[bass.ds(e, 1)].rearrange("o (c p) n -> p (o c) n", p=P),
                            rt_down[bass.ds(e, 1)].rearrange("o (c p) n -> p (o c) n", p=P))

                pool.wait_ge(w0_lo, 4)
                pool.sem_inc(w_split, 1)
                with pool.Fori(0, E // 2 - 1) as i:
                    for k in range(2):
                        n = i * 2 + (k + 1)
                        steps = fetch(n, 1 - k, *expert_weights(n, 1 - k))
                        next(steps)
                        pool.wait_ge(w_used[1 - k], i + 1)
                        for _ in steps:
                            pass
                steps = fetch(E - 1, 1, *expert_weights(E - 1, 1))
                next(steps)
                pool.wait_ge(w_used[1], E // 2)
                for _ in steps:
                    pass
                steps = fetch(E, 0, sh_up[0].rearrange("(c p) n -> p c n", p=P), sh_down[0].rearrange("(c p) n -> p c n", p=P))
                next(steps)
                pool.wait_ge(w_used[0], E // 2)
                for _ in steps:
                    pass
                n, t0 = tiles_of(pool, E - 1)
                pool.wait_ge(y_stored, (t0 + n) * 16)
                pool.sem_inc(rows_ready, 1)
                pool.wait_ge(rows_ready, 1)
                pool.wait_ge(scattered, 2 * B * 16)
                for b in range(B):
                    if b >= YR:
                        pool.wait_ge(combined, b - YR + 1)
                    for k in range(2):
                        pool.indirect_dma_start(
                            out=y_ring(b, k), out_offset=None, in_=slots_y,
                            in_offset=bass.IndirectOffsetOnAxis(ap=slot[0:SL, k, b:b + 1], axis=0)
                            ).then_inc(gathered[b % YR], 16)

            @block.sync
            def _(sp):
                def load(g):
                    sp.dma_start(sx[:, :, :, :].rearrange("p s m n -> p s (m n)").bitcast(F32),
                                 ln_out[bass.ds(g, 1)].rearrange("o p s n -> p (o s) n")).then_inc(sx_in, 16)

                def store(g):
                    sp.wait_ge(bt_out, g * 2 + 2)
                    sp.dma_start(base[bass.ds(g, 1)].rearrange("o p n -> p (o n)"),
                                 b_rows[:, :, :].rearrange("p b n -> p (b n)")).then_inc(base_stored, 16)

                def load_base(q, h):
                    sp.dma_start(fin[:, h * GB:(h + 1) * GB, :].rearrange("p b n -> p (b n)"),
                                 base[bass.ds(q * 2 + h, 1)].rearrange("o p n -> p (o n)")).then_inc(base_in[h], 16)

                def store_out(q, h):
                    sp.wait_ge(combined, q * YR + (h + 1) * GB)
                    sp.dma_start(out[bass.ds(q * YR + h * GB, GB)].rearrange("b s n -> s b n"),
                                 fin[0:SL, h * GB:(h + 1) * GB, :]).then_inc(out_done[h], 16)

                load(0)
                sp.dma_start(raw[:, 0:2048].rearrange("p (c n) -> p c n", c=MC),
                             rt_up[0].rearrange("(c p) n -> p c n", p=P)).then_inc(w0_in, 16)
                sp.dma_start(raw[:, 2048:4096].rearrange("p (c n) -> p c n", c=FC),
                             rt_down[0].rearrange("(c p) n -> p c n", p=P)).then_inc(w0_in, 16)
                with sp.Fori(1, G1) as g:
                    sp.wait_ge(up_done, g * FC)
                    load(g)
                    store(g - 1)
                sp.wait_ge(up_done, G1 * FC)
                load(G1)
                store(G1 - 1)
                sp.wait_ge(scattered, 2 * B * 16)
                with sp.Fori(0, E) as e:
                    n, t0 = tiles_of(sp, e)
                    with sp.Fori(0, n) as t:
                        sp.wait_ge(xt_done, t0 + t)
                        sp.dma_start(rows_in[:, :, :], slots_x[bass.ds(first_row(t0 + t), ET), :].rearrange("(p a) n -> p a n", a=2)
                                     ).then_inc(rows_loaded, 16)
                n, t0 = tiles_of(sp, E - 1)
                sp.wait_ge(xt_done, t0 + n)
                sp.dma_start(rows_in[:, :, :], slots_x[0:ET, :].rearrange("(p a) n -> p a n", a=2)).then_inc(rows_loaded, 16)
                sp.wait_ge(base_stored, G1 * 16)
                load_base(0, 0)
                load_base(0, 1)
                sp.wait_ge(up_done, (G1 + 1) * FC)
                load(G1 + 1)
                for g in range(G1 + 1, NG):
                    q = g - (G1 + 1)
                    store(g - 1)
                    if g + 1 < NG:
                        sp.wait_ge(up_done, g * FC + FC)
                        load(g + 1)
                    for h in range(2):
                        store_out(q, h)
                    if g + 1 == NG:
                        store(g)
                    sp.wait_ge(base_stored, min(g + 2, NG) * 16 if g + 1 == NG else g * 16)
                    for h in range(2):
                        sp.wait_ge(out_done[h], q * 16 + 16)
                        load_base(q + 1, h)
                for h in range(2):
                    store_out(NG - (G1 + 1), h)
                for h in range(2):
                    sp.wait_ge(out_done[h], B // YR * 16)

            @block.tensor
            def _(pe):
                def turn(g):
                    pe.wait_ge(summed, g + 1)
                    pe.wait_ge(bt_out, g * 2)
                    for r in range(2):
                        for q in range(2):
                            for m in range(MC):
                                b = 2 * r + q
                                ins = pe.transpose(tr_ps[0:TP, r, q * HD + m * P:q * HD + (m + 1) * P],
                                                   bg[:, m, b * TP:(b + 1) * TP], ident[:, :])
                        ins.then_inc(bt_done, 1)

                def up(w, g):
                    pe.wait_ge(sx_in, (g + 1) * 16)
                    for f in range(FC):
                        if f >= 4 or not (isinstance(g, int) and g == 0):
                            pe.wait_ge(gelu_done, g * FC + (f - 3))
                        k = 0
                        for m in range(MC):
                            for wp, dp in PASSES:
                                at = m * F + f * P
                                ins = pe.matmul(up_ps[:, f % 4, 0:N], w[:, wp, at:at + P], sx[:, dp, m, :],
                                                start=(k == 0), stop=(k == 5))
                                k += 1
                        ins.then_inc(up_done, 1)

                def down(w, g):
                    if not (isinstance(g, int) and g == 0):
                        pe.wait_ge(summed, g)
                    for f in range(FC):
                        pe.wait_ge(act_lo, g * FC + (f + 1))
                        for m in range(MC):
                            for k, (wp, dp) in enumerate(PASSES):
                                at = 2048 + f * HD + m * P
                                ins = pe.matmul(dn_ps[:, m, 0:N], w[:, wp, at:at + P], act_s[:, dp, f, :],
                                                start=(f == 0 and k == 0), stop=(f == FC - 1 and k == 2))
                    ins.then_inc(dn_done, 1)

                def turn_rows(n0):
                    pe.wait_ge(rows_loaded, n0 * 16 + 16)
                    for m in range(MC):
                        for a in range(2):
                            ins = pe.transpose(tr_ps[:, 0, (2 * m + a) * P:(2 * m + a + 1) * P],
                                               rows_in[:, a, m * P:(m + 1) * P], ident[:, :])
                    ins.then_inc(xt_done, 1)

                def tile(w, e, n0):
                    pe.wait_ge(w_split, e + 1)
                    pe.wait_ge(x_lo, n0 + 1)
                    for f in range(FC):
                        pe.wait_ge(rgelu_done, n0 * FC + (f - 3) if f >= 3 else n0 * FC)
                        k = 0
                        for m in range(MC):
                            for wp, dp in PASSES:
                                at = m * F + f * P
                                ins = pe.matmul(up_ps[:, f % 4, 0:ET], w[:, wp, at:at + P], rx[:, dp, m, :],
                                                start=(k == 0), stop=(k == 5))
                                k += 1
                        ins.then_inc(rup_done, 1)
                    turn_rows(n0 + 1)
                    pe.wait_ge(y_out, n0)
                    for a in range(2):
                        k = 0
                        for f in range(FC):
                            if a == 0:
                                pe.wait_ge(ract_lo, n0 * FC + (f + 1))
                            for dp, wp in PASSES:
                                at = 2048 + f * HD
                                ins = pe.matmul(dn_ps[:, 0, a * HD:(a + 1) * HD], act_s[:, dp, f, a * P:(a + 1) * P],
                                                w[:, wp, at:at + HD], start=(k == 0), stop=(k == 3 * FC - 1))
                                k += 1
                    ins.then_inc(rdn_done, 1)

                up(wB, 0)
                down(wB, 0)
                with pe.Fori(1, G1) as g:
                    up(wB, g)
                    turn(g - 1)
                    down(wB, g)
                pe.wait_ge(dn_done, G1)
                pe.sem_inc(w_used[1], 1)
                turn(G1 - 1)

                pe.wait_ge(bt_out, G1 * 2)
                turn_rows(0)
                with pe.Fori(0, E // 2) as i:
                    for par in range(2):
                        e = i * 2 + par
                        n, t0 = tiles_of(pe, e)
                        with pe.Fori(0, n) as t:
                            tile(weights[par], e, t0 + t)
                        pe.wait_ge(rdn_done, t0 + n)
                        pe.sem_inc(w_used[par], 1)

                pe.wait_ge(w_split, E + 1)
                n, t0 = tiles_of(pe, E - 1)
                pe.wait_ge(x_lo, t0 + n + 1)
                pe.wait_ge(y_out, t0 + n)
                up(wA, G1)
                down(wA, G1)
                with pe.Fori(G1 + 1, NG) as g:
                    up(wA, g)
                    turn(g - 1)
                    down(wA, g)
                turn(NG - 1)

            @block.scalar
            def _(act):
                def gelus(g):
                    for f in range(FC):
                        act.wait_ge(up_done, g * FC + (f + 1))
                        if f >= 2 or not (isinstance(g, int) and g == 0):
                            act.wait_ge(act_lo, g * FC + (f - 1))
                        act.activation(act_f[:, f % 2, :], up_ps[:, f % 4, 0:N], ACT.Gelu).then_inc(gelu_done, 1)

                def take_rows(g):
                    act.wait_ge(base_stored, g * 16)
                    for r in range(2):
                        act.wait_ge(bt_done, g * 2 + (r + 1))
                        act.activation(b_rows[:, 2 * r:2 * r + 2, :].rearrange("p b n -> p (b n)"), tr_ps[0:TP, r, :], ACT.Copy
                                       ).then_inc(bt_out, 1)

                def take_x(n0):
                    act.wait_ge(xt_done, n0 + 1)
                    act.activation(rx[:, HI, :, :].rearrange("p m t -> p (m t)"), tr_ps[:, 0, :], ACT.Copy).then_inc(x_hi, 1)

                def w0_part(q):
                    cols = slice(q * 1024, (q + 1) * 1024)
                    act.activation(wA[:, HI, cols], raw[:, cols], ACT.Copy).then_inc(w0_hi, 1)

                gelus(0)
                act.wait_ge(w0_in, 32)
                w0_part(0)
                w0_part(1)
                with act.Fori(1, G1) as g:
                    gelus(g)
                    take_rows(g - 1)
                w0_part(2)
                w0_part(3)
                take_rows(G1 - 1)

                take_x(0)
                with act.Fori(0, E) as e:
                    n, t0 = tiles_of(act, e)
                    with act.Fori(0, n) as t:
                        n0 = t0 + t
                        for f in range(FC):
                            act.wait_ge(rup_done, n0 * FC + (f + 1))
                            act.wait_ge(ract_lo, n0 * FC + (f - 1) if f >= 1 else n0 * FC)
                            act.activation(act_f[:, f % 2, 0:ET], up_ps[:, f % 4, 0:ET], ACT.Gelu).then_inc(rgelu_done, 1)
                        take_x(n0 + 1)
                        act.wait_ge(rdn_done, n0 + 1)
                        act.wait_ge(y_stored, n0 * 16)
                        act.activation(rows_out[:, :, :].rearrange("p a n -> p (a n)"), dn_ps[:, 0, :], ACT.Copy
                                       ).then_inc(y_out, 1)
                        act.wait_ge(y_out, n0 + 1)
                        act.dma_start(slots_y[bass.ds(first_row(n0), ET), :].rearrange("(p a) n -> p a n", a=2),
                                      rows_out[:, :, :]).then_inc(y_stored, 16)

                gelus(G1)
                with act.Fori(G1 + 1, NG) as g:
                    gelus(g)
                    take_rows(g - 1)
                take_rows(NG - 1)

            @block.vector
            def _(dve):
                def split(g, f):
                    dve.wait_ge(gelu_done, g * FC + (f + 1))
                    dve.tensor_copy(act_s[:, HI, f, :], act_f[:, f % 2, :]).then_inc(act_hi, 1)
                    dve.wait_ge(act_hi, g * FC + (f + 1))
                    dve.tensor_tensor(act_s[:, LO, f, :], act_f[:, f % 2, :], act_s[:, HI, f, :], ALU.subtract
                                      ).then_inc(act_lo, 1)

                def add(g):
                    dve.wait_ge(dn_done, g + 1)
                    dve.wait_ge(bt_done, g * 2)
                    for m in range(MC):
                        ins = dve.tensor_tensor(bg[:, m, :], hT[:, m, gcols(g)], dn_ps[:, m, 0:N], ALU.add)
                    ins.then_inc(summed, 1)

                def combine(q, f):
                    b = q * YR + f
                    if f % GB == 0:
                        dve.wait_ge(base_in[f // GB], q * 16 + 16)
                    dve.wait_ge(gathered[f], q * 32 + 32)
                    acc = fin[0:SL, f, :]
                    for k, done in ((0, first), (1, combined)):
                        p = top_p[0:SL, bass.ds(b, 1), k:k + 1].rearrange("p o k -> p (o k)")
                        dve.scalar_tensor_tensor(out=acc, in0=y_ring(f, k), scalar=p, in1=acc,
                                                 op0=ALU.mult, op1=ALU.add).then_inc(done, 1)
                        if k == 0:
                            dve.wait_ge(first, b + 1)

                def take_x(n0):
                    dve.wait_ge(x_hi, n0 + 1)
                    dve.tensor_tensor(rx[:, LO, :, :].rearrange("p m t -> p (m t)"), tr_ps[:, 0, :],
                                      rx[:, HI, :, :].rearrange("p m t -> p (m t)"), ALU.subtract).then_inc(x_lo, 1)

                def w0_part(q):
                    cols = slice(q * 1024, (q + 1) * 1024)
                    dve.wait_ge(w0_hi, q + 1)
                    dve.tensor_tensor(wA[:, LO, cols], raw[:, cols], wA[:, HI, cols], ALU.subtract).then_inc(w0_lo, 1)

                for f in range(FC):
                    split(0, f)
                add(0)
                w0_part(0)
                w0_part(1)
                with dve.Fori(1, G1) as g:
                    for f in range(FC):
                        split(g, f)
                    add(g)
                w0_part(2)
                w0_part(3)
                take_x(0)
                with dve.Fori(0, E) as e:
                    n, t0 = tiles_of(dve, e)
                    with dve.Fori(0, n) as t:
                        n0 = t0 + t
                        for f in range(FC):
                            dve.wait_ge(rgelu_done, n0 * FC + (f + 1))
                            if f == 0:
                                dve.wait_ge(rdn_done, n0)
                            dve.tensor_copy(act_s[:, HI, f, 0:ET], act_f[:, f % 2, 0:ET]).then_inc(ract_hi, 1)
                            dve.wait_ge(ract_hi, n0 * FC + (f + 1))
                            dve.tensor_tensor(act_s[:, LO, f, 0:ET], act_f[:, f % 2, 0:ET], act_s[:, HI, f, 0:ET],
                                              ALU.subtract).then_inc(ract_lo, 1)
                        take_x(n0 + 1)
                n, t0 = tiles_of(dve, E - 1)
                dve.wait_ge(rdn_done, t0 + n)
                for f in range(FC):
                    split(G1, f)
                add(G1)
                with dve.Fori(G1 + 1, NG) as g:
                    for f in range(FC):
                        split(g, f)
                        combine(g - (G1 + 1), f)
                    add(g)
                for f in range(FC):
                    combine(NG - (G1 + 1), f)


_INS = ["x", "L0_tok_W1", "L0_tok_b1", "L0_tok_W2", "L0_tok_b2", "L0_tok_gamma", "L0_tok_beta", "L0_attn_kernel",
        "L0_attn_WO", "L0_ffn_shared_up", "L0_ffn_shared_down", "L0_ffn_routed_up", "L0_ffn_routed_down",
        "L0_ffn_router_w"]


def kernel(**inputs):
    import numpy as np
    import concourse.bacc as bacc
    from concourse.bass_utils import run_bass_kernel_spmd

    nc = bacc.Bacc("TRN2", target_bir_lowering=False, num_devices=1)
    arrays, args = {}, []
    for name in _INS:
        a = np.ascontiguousarray(inputs[name])
        arrays[f"in_{name}"] = a
        args.append(nc.dram_tensor(f"in_{name}", a.shape, mybir.dt.from_np(a.dtype), kind="ExternalInput").ap())
    shape = (inputs["x"].shape[0], 93, inputs["L0_tok_W2"].shape[1])
    args.append(nc.dram_tensor("out_0", shape, F32, kind="ExternalOutput").ap())
    audio_tower_kernel(nc, *args)
    r = run_bass_kernel_spmd(nc, [arrays], core_ids=[0])
    return r.results[0]["out_0"]
```

```python
from contextlib import ExitStack

import concourse.bass as bass
from concourse import mybir

ALU = mybir.AluOpType
ACT = mybir.ActivationFunctionType
F32 = mybir.dt.float32
F32R = mybir.dt.float32r
I32 = mybir.dt.int32
U32 = mybir.dt.uint32
AX = mybir.AxisListType.X

P = 128
EPS = 1e-5

HI, LO = 0, 1
PASSES = ((HI, HI), (HI, LO), (LO, HI))


class Chain:

    def __init__(self, eng, sem):
        self.eng, self.sem, self.n = eng, sem, 0

    def then(self, ins):
        self.n += 1
        ins.then_inc(self.sem, 1)
        self.eng.wait_ge(self.sem, self.n)


def ge(eng, s, value):
    if not (isinstance(value, int) and value <= 0):
        eng.wait_ge(s, value)


def audio_tower_kernel(nc, x, W1, b1, W2, b2, gamma, beta, qkv_w, WO, sh_up, sh_down, rt_up, rt_down, router_w, out):
    B, L, D = x.shape
    STRIDE, FRAMES = 4, 8
    KF = STRIDE * D
    SL = 1 + (L + STRIDE - (L - FRAMES) % STRIDE - FRAMES) // STRIDE
    FG = SL + 1
    TP = 96
    GPITCH = TP + 2
    HD = W2.shape[1]
    MC = HD // P
    GB = 4
    NG = B // GB
    N = GB * TP
    NT = B * TP
    _, H, _, DH = qkv_w.shape
    NJ = H // 2
    SCALE = 1.0 / (DH * DH * H)
    F = sh_up.shape[2]
    FC = F // P
    E = rt_up.shape[0]
    ET = 256
    MAXT = -(-B * SL // ET)
    CAP = MAXT * ET
    KC = (112, 112, 96)
    KO = (0, 112, 224)

    ln_out = nc.dram_tensor("ln_out", (NG, P, 2, MC * N), F32).ap()
    slots = nc.dram_tensor("slots", (E * CAP, HD), F32).ap()
    base = nc.dram_tensor("base", (NG, TP, GB * HD), F32).ap()

    with ExitStack() as ctx:
        def sb(c, name, shape, dt=F32):
            return c.enter_context(nc.sbuf_tensor(name, shape, dt))

        def ps(c, name, shape, dt=F32):
            return c.enter_context(nc.psum_tensor(name, shape, dt))

        def sem(c, name):
            return c.enter_context(nc.semaphore(name))

        hT = sb(ctx, "hT", [P, MC, NT])
        wA = sb(ctx, "wA", [P, 2, 4096], F32R)
        wB = sb(ctx, "wB", [P, 2, 4096], F32R)
        ident = sb(ctx, "ident", [P, P])
        mean_w = sb(ctx, "mean_w", [P, P])
        eps_c = sb(ctx, "eps_c", [P, 1])
        zero_c = sb(ctx, "zero_c", [P, 1])
        half3_c = sb(ctx, "half3_c", [P, 1])
        bn_scale = sb(ctx, "bn_scale", [P, MC])
        bn_shift = sb(ctx, "bn_shift", [P, MC])
        top_p = sb(ctx, "top_p", [TP, B, 2])
        slot = sb(ctx, "slot", [TP, 2, B], U32)
        tiles_i = sb(ctx, "tiles_i", [1, 2, E], I32)

        gcols = lambda g: bass.ds(g * N, N)

        with ExitStack() as c:
            raw_s = sb(c, "raw_s", [P, 2048])
            raw_w = sb(c, "raw_w", [P, 4096])
            w1 = sb(c, "w1", [P, 2, 6, HD], F32R)
            w2 = sb(c, "w2", [P, 2, MC, HD], F32R)
            b1c = sb(c, "b1c", [P, MC])
            b2c = sb(c, "b2c", [P, MC])
            gam = sb(c, "gam", [P, MC])
            bet = sb(c, "bet", [P, MC])
            frames = sb(c, "frames", [FG, GB, KF])
            grp = [sb(c, "grp%d" % i, [112, 2, 3, GB, GPITCH], F32R) for i in range(2)]
            t1 = sb(c, "t1", [P, MC, N])
            t1s = sb(c, "t1s", [P, 2, MC, N], F32R)
            stats = sb(c, "stats", [P, MC, NG, 6])
            mv = sb(c, "mv", [P, MC, 2])
            std = sb(c, "std", [P, MC])
            tr_ps = ps(c, "tr_ps", [112, 2, 4, P])
            l1_ps = ps(c, "l1_ps", [P, MC, 512])
            l2_ps = ps(c, "l2_ps", [P, MC, 512])

            ident_zero = sem(c, "ident_zero")
            consts = sem(c, "consts")
            pads = sem(c, "pads")
            w12_in = sem(c, "w12_in")
            vec_in = sem(c, "vec_in")
            w12_split = sem(c, "w12_split")
            attn_raw = sem(c, "attn_raw")
            attn_hi = sem(c, "attn_hi")
            attn_split = sem(c, "attn_split")
            x_in = sem(c, "x_in")
            turned = sem(c, "turned")
            grp_hi = sem(c, "grp_hi")
            grp_lo = sem(c, "grp_lo")
            l1_done = sem(c, "l1_done")
            l1_relu = sem(c, "l1_relu")
            l1_hi = sem(c, "l1_hi")
            l1_split = sem(c, "l1_split")
            l2_done = sem(c, "l2_done")
            l2_relu = sem(c, "l2_relu")
            bn_seen = sem(c, "bn_seen")
            bn_var = sem(c, "bn_var")
            bn_std = sem(c, "bn_std")
            v_chain = sem(c, "v_chain")

            block = c.enter_context(nc.Block())

            def in_pairs(eng, step):
                step(0, 0)
                step(1, 1)
                with eng.Fori(1, NG // 2 - 1) as i:
                    step(i * 2, 0)
                    step(i * 2 + 1, 1)
                step(NG - 2, 0)
                step(NG - 1, 1, more=False)

            @block.sync
            def _(sp):
                def load_frames(g):
                    sp.dma_start(frames[0:SL, :, :],
                                 x[bass.ds(g * GB, GB), 0:SL * STRIDE, :].rearrange("b (s f) d -> s b (f d)", f=STRIDE)
                                 ).then_inc(x_in, 16)
                    rest = L - SL * STRIDE
                    sp.dma_start(frames[SL:FG, :, 0:rest * D],
                                 x[bass.ds(g * GB, GB), SL * STRIDE:L, :].rearrange("b f d -> b (f d)").unsqueeze(0)
                                 ).then_inc(x_in, 16)

                sp.wait_ge(pads, 1)
                load_frames(0)
                for s in range(2):
                    for q in range(3):
                        sp.dma_start(raw_s[0:KC[q], (3 * s + q) * HD:(3 * s + q + 1) * HD],
                                     W1[s * KF + KO[q]:s * KF + KO[q] + KC[q], :]).then_inc(w12_in, 16)
                sp.dma_start(raw_s[:, 6 * HD:8 * HD].rearrange("p (c n) -> p c n", c=MC),
                             W2.rearrange("(c p) n -> p c n", p=P)).then_inc(w12_in, 16)
                for v, t in ((b1, b1c), (b2, b2c), (gamma, gam), (beta, bet)):
                    sp.dma_start(t[:, :].unsqueeze(2), v.rearrange("(c p o) -> p c o", p=P, o=1),
                                 allow_slow_non_contiguous=True).then_inc(vec_in, 16)
                for t in range(2):
                    for m in range(MC):
                        sp.dma_start(raw_w[:, m * 2048 + t * 1024:m * 2048 + (t + 1) * 1024].rearrange("p (h d) -> p h d", h=H),
                                     qkv_w[t, :, m * P:(m + 1) * P, :].rearrange("h p d -> p h d")).then_inc(attn_raw, 16)
                for g in range(1, 4):
                    sp.wait_ge(turned, GB * g)
                    load_frames(g)
                sp.wait_ge(attn_split, 1)
                for m in range(MC):
                    sp.dma_start(raw_w[:, m * 1024:(m + 1) * 1024].rearrange("p (h d) -> p h d", h=H),
                                 qkv_w[2, :, m * P:(m + 1) * P, :].rearrange("h p d -> p h d")).then_inc(attn_raw, 16)
                for hh in range(2):
                    sp.dma_start(raw_w[hh * DH:(hh + 1) * DH, 2048:4096].rearrange("p (j n) -> p j n", j=NJ),
                                 WO[0].rearrange("(d j hh) n -> hh d j n", hh=2, j=NJ)[hh]).then_inc(attn_raw, 16)
                with sp.Fori(4, NG) as g:
                    sp.wait_ge(turned, g * GB)
                    load_frames(g)

            @block.gpsimd
            def _(pool):
                pool.memset(frames[:, :, (STRIDE - 1) * D:KF], 0.0).then_inc(pads, 1)
                for t in grp:
                    pool.memset(t[:, :, :, :, :].bitcast(F32), 0.0).then_inc(pads, 1)
                pool.memset(ident[:, :], 0.0).then_inc(ident_zero, 1)
                pool.wait_ge(ident_zero, 1)
                pool.affine_select(out=ident[:, :], in_=ident[:, :], compare_op=ALU.not_equal, fill=1.0, base=0,
                                   pattern=[[-1, P]], channel_multiplier=1).then_inc(consts, 1)
                pool.memset(mean_w[:, :], 1.0 / HD).then_inc(consts, 1)
                pool.memset(eps_c[:, :], EPS).then_inc(consts, 1)
                pool.memset(zero_c[:, :], 0.0).then_inc(consts, 1)
                pool.memset(half3_c[:, :], 1.5).then_inc(consts, 1)
                pool.wait_ge(consts, 5)
                for t, w in ((0, wA), (1, wB)):
                    pool.wait_ge(attn_raw, 64 * (t + 1))
                    for q in range(4):
                        cols = slice(q * 1024, (q + 1) * 1024)
                        pool.tensor_tensor(w[:, HI, cols], raw_w[:, cols], zero_c[:, 0:1].broadcast_to([P, 1024]), ALU.add).then_inc(attn_hi, 1)
                        pool.wait_ge(attn_hi, 4 * t + q + 1)
                        ins = pool.tensor_tensor(w[:, LO, cols], raw_w[:, cols], w[:, HI, cols], ALU.subtract)
                    ins.then_inc(attn_split, 1)
                pool.wait_ge(attn_split, 2)

            @block.tensor
            def _(pe):
                def turn(g, b):
                    if b == 0:
                        pe.wait_ge(x_in, (g + 1) * 32)
                    if b >= 2 or not (isinstance(g, int) and g == 0):
                        pe.wait_ge(grp_lo, g * GB + (b - 1))
                    for q in range(3):
                        ins = pe.transpose(tr_ps[0:KC[q], b % 2, q, 0:FG], frames[:, b, KO[q]:KO[q] + KC[q]],
                                           ident[0:FG, 0:FG])
                    ins.then_inc(turned, 1)

                def layer1(g, par, m):
                    pe.wait_ge(grp_lo, g * GB + GB)
                    ge(pe, l1_relu, g * MC)
                    k = 0
                    for s in range(2):
                        for q in range(3):
                            for wp, dp in PASSES:
                                ins = pe.matmul(l1_ps[:, m, 0:N], w1[0:KC[q], wp, 3 * s + q, m * P:(m + 1) * P],
                                                grp[par][0:KC[q], dp, q, :, s:s + TP], start=(k == 0), stop=(k == 17))
                                k += 1
                    ins.then_inc(l1_done, 1)

                def layer2(g):
                    ge(pe, l2_relu, g * MC)
                    for q in range(MC):
                        pe.wait_ge(l1_split, g * MC + (q + 1))
                        for m in range(MC):
                            for k, (wp, dp) in enumerate(PASSES):
                                ins = pe.matmul(l2_ps[:, m, 0:N], w2[:, wp, q, m * P:(m + 1) * P], t1s[:, dp, q, :],
                                                start=(q == 0 and k == 0), stop=(q == MC - 1 and k == 2))
                            if q == MC - 1:
                                ins.then_inc(l2_done, 1)

                def step(g, par, more=True):
                    for m in range(MC):
                        layer1(g, par, m)
                        for b in range(2 * m, 2 * m + 2):
                            if more:
                                turn(g + 1, b)
                    layer2(g)

                pe.wait_ge(consts, 5)
                for b in range(GB):
                    turn(0, b)
                pe.wait_ge(w12_split, 1)
                in_pairs(pe, step)

            @block.scalar
            def _(act):
                def turned_hi(g, par, b):
                    act.wait_ge(turned, g * GB + (b + 1))
                    act.activation(grp[par][0:112, HI, 0:2, b, 0:FG], tr_ps[0:112, b % 2, 0:2, 0:FG], ACT.Copy)
                    act.activation(grp[par][0:96, HI, 2, b, 0:FG], tr_ps[0:96, b % 2, 2, 0:FG], ACT.Copy
                                   ).then_inc(grp_hi, 1)

                def relu1(g, m):
                    ge(act, l1_split, g * MC)
                    act.wait_ge(l1_done, g * MC + (m + 1))
                    act.activation(t1[:, m, :], l1_ps[:, m, 0:N], ACT.Relu, bias=b1c[:, m:m + 1]).then_inc(l1_relu, 1)

                def relu2(g):
                    for m in range(MC):
                        act.wait_ge(l2_done, g * MC + (m + 1))
                        act.activation(hT[:, m, gcols(g)], l2_ps[:, m, 0:N], ACT.Relu, bias=b2c[:, m:m + 1]
                                       ).then_inc(l2_relu, 1)

                def step(g, par, more=True):
                    for m in range(MC):
                        relu1(g, m)
                        for b in range(2 * m, 2 * m + 2):
                            if more:
                                turned_hi(g + 1, 1 - par, b)
                    relu2(g)

                act.wait_ge(pads, 3)
                for b in range(GB):
                    turned_hi(0, 0, b)
                act.wait_ge(vec_in, 64)
                in_pairs(act, step)
                act.wait_ge(bn_var, 1)
                act.activation(std[:, :], mv[:, :, 1], ACT.Sqrt, bias=eps_c[:, :]).then_inc(bn_std, 1)

            @block.vector
            def _(dve):
                def turned_lo(g, par, b):
                    dve.wait_ge(grp_hi, g * GB + (b + 1))
                    dve.tensor_tensor(grp[par][0:112, LO, 0:2, b, 0:FG], tr_ps[0:112, b % 2, 0:2, 0:FG],
                                      grp[par][0:112, HI, 0:2, b, 0:FG], ALU.subtract)
                    dve.tensor_tensor(grp[par][0:96, LO, 2, b, 0:FG], tr_ps[0:96, b % 2, 2, 0:FG],
                                      grp[par][0:96, HI, 2, b, 0:FG], ALU.subtract).then_inc(grp_lo, 1)

                def split1(g, m):
                    ge(dve, l2_done, g * MC)
                    dve.wait_ge(l1_relu, g * MC + (m + 1))
                    dve.tensor_copy(t1s[:, HI, m, :], t1[:, m, :]).then_inc(l1_hi, 1)
                    dve.wait_ge(l1_hi, g * MC + (m + 1))
                    dve.tensor_tensor(t1s[:, LO, m, :], t1[:, m, :], t1s[:, HI, m, :], ALU.subtract
                                      ).then_inc(l1_split, 1)

                def count(g):
                    for m in range(MC):
                        dve.wait_ge(l2_relu, g * MC + (m + 1))
                        dve.bn_stats(stats[:, m, bass.ds(g, 1), :].rearrange("p o s -> p (o s)"),
                                     hT[:, m, gcols(g)].rearrange("p (b t) -> p b t", b=GB)[:, :, 0:SL]
                                     ).then_inc(bn_seen, 1)

                def step(g, par, more=True):
                    for m in range(MC):
                        split1(g, m)
                        for b in range(2 * m, 2 * m + 2):
                            if more:
                                turned_lo(g + 1, 1 - par, b)
                    count(g)

                dve.wait_ge(pads, 3)
                for b in range(GB):
                    turned_lo(0, 0, b)
                dve.wait_ge(w12_in, 7 * 16)
                chain = Chain(dve, v_chain)
                for q in range(6):
                    dve.tensor_copy(w1[0:KC[q % 3], HI, q, :], raw_s[0:KC[q % 3], q * HD:(q + 1) * HD])
                w2raw = raw_s[:, 6 * HD:8 * HD].rearrange("p (c n) -> p c n", c=MC)
                chain.then(dve.tensor_copy(w2[:, HI, :, :], w2raw))
                for q in range(6):
                    dve.tensor_tensor(w1[0:KC[q % 3], LO, q, :], raw_s[0:KC[q % 3], q * HD:(q + 1) * HD],
                                      w1[0:KC[q % 3], HI, q, :], ALU.subtract)
                dve.tensor_tensor(w2[:, LO, :, :], w2raw, w2[:, HI, :, :], ALU.subtract).then_inc(w12_split, 1)
                in_pairs(dve, step)
                dve.wait_ge(bn_seen, NG * MC)
                for m in range(MC):
                    ins = dve.bn_aggr(mv[:, m, :], stats[:, m, :, :].rearrange("p g s -> p (g s)"))
                ins.then_inc(bn_var, 1)
                dve.wait_ge(bn_std, 1)
                chain.then(dve.reciprocal(bn_scale[:, :], std[:, :]))
                dve.wait_ge(vec_in, 64)
                chain.then(dve.tensor_tensor(bn_scale[:, :], bn_scale[:, :], gam[:, :], ALU.mult))
                chain.then(dve.tensor_tensor(bn_shift[:, :], mv[:, :, 0], bn_scale[:, :], ALU.mult))
                chain.then(dve.tensor_tensor(bn_shift[:, :], bet[:, :], bn_shift[:, :], ALU.subtract))

        x_rows = sb(ctx, "x_rows", [TP, GB, HD])
        sx = sb(ctx, "sx", [P, 2, MC, N], F32R)
        sq2 = sb(ctx, "sq2", [P, MC, N])
        dev2 = sb(ctx, "dev2", [P, MC, N])
        var2 = sb(ctx, "var2", [P, N])
        rstd2 = sb(ctx, "rstd2", [P, N])
        split2 = sb(ctx, "split2", [P, 2, MC, N], F32R)
        rw = sb(ctx, "rw", [P, MC, P])
        lgT = sb(ctx, "lgT", [P, N])
        small = [TP, GB, E]
        ex = sb(ctx, "ex", small)
        tops = sb(ctx, "tops", small)
        top_i = sb(ctx, "top_i", small, U32)
        idx = sb(ctx, "idx", [TP, GB, 2])
        mask = sb(ctx, "mask", [TP, 2, GB, E])
        both = sb(ctx, "both", small)
        rank = sb(ctx, "rank", small)
        pick = sb(ctx, "pick", [TP, 2, GB, E])
        slot_f = sb(ctx, "slot_f", [TP, 2, GB])
        slot_now = sb(ctx, "slot_now", [TP, 2, GB], U32)
        row_mx = sb(ctx, "row_mx", [TP, GB])
        row_sum = sb(ctx, "row_sum", [TP, GB])
        next_row = sb(ctx, "next_row", [TP, E])
        numbers = sb(ctx, "numbers", [TP, E])
        before_w = sb(ctx, "before_w", [SL, TP])
        ones_w = sb(ctx, "ones_w", [SL, TP])
        pj_ps = ps(ctx, "pj_ps", [P, 2, 512])
        ones_set = sem(ctx, "ones_set")
        tri_set = sem(ctx, "tri_set")
        numbers_set = sem(ctx, "numbers_set")
        filled = [sem(ctx, "filled_act"), sem(ctx, "filled_dve")]
        taken = [sem(ctx, "taken_act"), sem(ctx, "taken_dve")]
        h_added = sem(ctx, "h_added")
        affine = sem(ctx, "affine")
        ln = [{k: sem(ctx, "ln%d_%s" % (i + 1, k)) for k in
               ("sq", "log", "root", "square", "scaled", "halved", "rstd", "out", "hi", "lo")} for i in range(2)]
        stored = sem(ctx, "stored")
        kept = sem(ctx, "kept")
        logits_shifted = sem(ctx, "logits_shifted")
        logits_exp = sem(ctx, "logits_exp")
        masks_done = sem(ctx, "masks_done")
        slots_set = sem(ctx, "slots_set")
        scattered = sem(ctx, "scattered")
        cleared = sem(ctx, "cleared")
        slots_known = sem(ctx, "slots_known")
        probs_there = sem(ctx, "probs_there")
        sending = sem(ctx, "sending")
        r_chain = sem(ctx, "r_chain")
        sh_hi = sem(ctx, "sh_hi")
        sx_in = sem(ctx, "sx_in")
        raw_sh = ExitStack()
        raw2 = sb(raw_sh, "raw2", [P, 4096])
        raw2_in = sem(ctx, "raw2_in")
        with ExitStack() as c:
            NU = 2 * NJ
            VW = 2 * P
            xg = sb(c, "xg", [P, 2, MC, N], F32R)
            qT = sb(c, "qT", [P, 2, N])
            kB = sb(c, "kB", [P, 2, GB, 2, TP])
            v_rows = sb(c, "v_rows", [TP, 2, GB, VW])
            prob = sb(c, "prob", [TP, 4, 4, TP])
            probT = sb(c, "probT", [TP, 2, 4 * TP])
            mx = sb(c, "mx", [TP, 2, 4])
            sm = sb(c, "sm", [TP, 2, 4])
            rc = sb(c, "rc", [TP, 2, 4])
            oT = sb(c, "oT", [P, 2, 2, GB, TP], F32R)
            dev = [sb(c, "dev1", [P, MC, N]), dev2]
            sq = [sb(c, "sq1", [P, MC, N]), sq2]
            var = [sb(c, "var1", [P, N]), var2]
            rstd = [sb(c, "rstd1", [P, N]), rstd2]
            zeros = sb(c, "zeros", [P, HD])
            s_ps = ps(c, "s_ps", [TP, 2, 512])
            t_ps = ps(c, "t_ps", [TP, 512])
            o_ps = ps(c, "o_ps", [P, 512])
            y_ps = ps(c, "y_ps", [P, MC, 512])

            ring_zero = sem(c, "ring_zero")
            rw_in = sem(c, "rw_in")
            scores_done = sem(c, "scores_done")
            max_done = sem(c, "max_done")
            shifted = sem(c, "shifted")
            exp_done = sem(c, "exp_done")
            sum_done = sem(c, "sum_done")
            recip_done = sem(c, "recip_done")
            scaled = sem(c, "scaled")
            turned = sem(c, "p_turned")
            turned_out = sem(c, "p_turned_out")
            pv_done = sem(c, "pv_done")
            o_hi = sem(c, "o_hi")
            o_lo = sem(c, "o_lo")
            wo_done = sem(c, "wo_done")
            block = c.enter_context(nc.Block())

            def tiles(kind):
                ahead, behind = kind != "last", kind != "first"
                t = ["q1", "k1", "v00", "v01", "v02", "v03"] + ["mean1"] * ahead + ["q2", "k2", "v10", "v11", "q3", "k3"]
                t += ["var1"] * ahead + ["v12", "v13"] + ["mean2"] * behind + ["q4", "k4"] + ["var2"] * behind
                t += ["v20", "v21", "q5", "k5", "v22", "v23", "q6", "k6"] + ["router", "xt0", "xt1"] * behind
                t += ["v30", "v31"] + ["logits"] * behind + ["q7", "k7", "v32", "v33"]
                t += ["rank"] * behind + ["q0", "k0"] * ahead
                return t

            def bank_of(tile):
                if tile[0] == "v" and tile[1].isdigit():
                    return int(tile[2]) % 2
                return 1 if tile[0] == "k" or tile in ("mean1", "mean2", "router", "logits", "rank") else 0

            SERIES = {"start": ["mean1", "var1", "q0", "k0"], "drain": ["mean2", "var2", "router", "xt0", "xt1", "logits", "rank"]}
            SERIES.update({kind: tiles(kind) for kind in ("first", "middle", "last")})

            def number(g, tile, back=0):
                bank = bank_of(tile)
                series = {kind: [t for t in ts if bank_of(t) == bank] for kind, ts in SERIES.items()}
                size = {kind: len(ts) for kind, ts in series.items()}
                before = size["start"] + size["first"]
                if not isinstance(g, int):
                    return (g - 1) * size["middle"] + (before + series["middle"].index(tile) + 1 - back * size["middle"])
                g -= back
                if g < 0:
                    return series["start"].index(tile) + 1
                if g == 0:
                    return size["start"] + series["first"].index(tile) + 1
                if g < NG - 1:
                    return before + (g - 1) * size["middle"] + series["middle"].index(tile) + 1
                before += (NG - 2) * size["middle"]
                if g == NG - 1:
                    return before + series["last"].index(tile) + 1
                return before + size["last"] + series["drain"].index(tile) + 1

            def begin(pe, g, tile):
                ge(pe, taken[bank_of(tile)], number(g, tile) - 1)

            def mean_tile(pe, g, i, n):
                tile = "mean%d" % (i + 1)
                pe.wait_ge(*((affine, n + 1) if i == 0 else (h_added, n + 1)))
                begin(pe, g, tile)
                for m in range(MC):
                    ins = pe.matmul(pj_ps[:, 1, 0:N], mean_w[:, :], hT[:, m, gcols(n)], start=(m == 0), stop=(m == 1))
                ins.then_inc(filled[1], 1)

            def var_tile(pe, g, i, n):
                tile = "var%d" % (i + 1)
                pe.wait_ge(ln[i]["sq"], n + 1)
                begin(pe, g, tile)
                for m in range(MC):
                    ins = pe.matmul(pj_ps[:, 0, 0:N], mean_w[:, :], sq[i][:, m, :], start=(m == 0), stop=(m == 1))
                ins.then_inc(filled[0], 1)

            def router_tile(pe, g, n):
                pe.wait_ge(ln[1]["out"], n + 1)
                begin(pe, g, "router")
                for m in range(MC):
                    ins = pe.matmul(pj_ps[:, 1, 0:N], rw[:, m, :], dev[1][:, m, :], start=(m == 0), stop=(m == 1))
                ins.then_inc(filled[1], 1)

            def rows_tile(pe, g, r, n):
                begin(pe, g, "xt%d" % r)
                for q in range(2):
                    for m in range(MC):
                        b = 2 * r + q
                        ins = pe.transpose(pj_ps[0:TP, 0, q * HD + m * P:q * HD + (m + 1) * P],
                                           dev[1][:, m, b * TP:(b + 1) * TP], ident[:, :])
                ins.then_inc(filled[0], 1)

            def logits_tile(pe, g, n):
                pe.wait_ge(taken[1], number(g, "router"))
                begin(pe, g, "logits")
                for b in range(GB):
                    ins = pe.transpose(pj_ps[0:TP, 1, b * P:(b + 1) * P], lgT[:, b * TP:(b + 1) * TP], ident[:, :])
                ins.then_inc(filled[1], 1)

            def rank_tile(pe, g, n):
                pe.wait_ge(masks_done, n + 1)
                begin(pe, g, "rank")
                to = pj_ps[0:TP, 1, 0:(GB + 1) * E]
                pe.matmul(to[:, 0:GB * E], before_w[:, :], both[0:SL, :, :].rearrange("p b e -> p (b e)"),
                          start=True, stop=False)
                for k in range(1, GB):
                    pe.matmul(to[:, k * E:GB * E], ones_w[:, :],
                              both[0:SL, 0:GB - k, :].rearrange("p b e -> p (b e)"), start=False, stop=(k == GB - 1))
                for b in range(GB):
                    ins = pe.matmul(to[:, GB * E:(GB + 1) * E], ones_w[:, :], both[0:SL, b, :],
                                    start=(b == 0), stop=(b == GB - 1))
                ins.then_inc(filled[1], 1)

            def square(act, g, i, n):
                act.wait_ge(taken[1], number(g, "mean%d" % (i + 1)))
                ge(act, ln[i]["rstd"], n)
                act.activation(sq[i][:, :, :], dev[i][:, :, :], ACT.Square).then_inc(ln[i]["sq"], 1)

            def root(act, g, i, n):
                act.wait_ge(filled[0], number(g, "var%d" % (i + 1)))
                ge(act, ln[i]["scaled"], n)
                act.activation(var[i][:, :], pj_ps[:, 0, 0:N], ACT.Identity, bias=eps_c[:, :]).then_inc(taken[0], 1)
                act.wait_ge(taken[0], number(g, "var%d" % (i + 1)))
                ge(act, ln[i]["out"], n)
                act.activation(rstd[i][:, :], var[i][:, :], ACT.Ln).then_inc(ln[i]["log"], 1)
                act.wait_ge(ln[i]["log"], n + 1)
                act.activation(rstd[i][:, :], rstd[i][:, :], ACT.Exp, scale=-0.5).then_inc(ln[i]["root"], 1)

            def halve(act, i, n):
                act.wait_ge(ln[i]["scaled"], n + 1)
                t = sq[i][:, 0, :]
                act.activation(t, t, ACT.Identity, bias=half3_c[:, :], scale=-0.5).then_inc(ln[i]["halved"], 1)

            def hi(act, g, i, n):
                act.wait_ge(ln[i]["out"], n + 1)
                if i == 0:
                    for b in range(2):
                        if not (isinstance(g, int) and g < 0):
                            act.wait_ge(filled[b], number(g, "v3%d" % (2 + b)))
                    act.activation(xg[:, HI, :, :], dev[0][:, :, :], ACT.Copy).then_inc(ln[0]["hi"], 1)
                else:
                    ge(act, stored, n * 16)
                    act.activation(split2[:, HI, :, :], dev[1][:, :, :], ACT.Copy).then_inc(ln[1]["hi"], 1)

            def take_rows(act, g, r, n):
                act.wait_ge(filled[0], number(g, "xt%d" % r))
                if r == 0:
                    ge(act, scattered, n * (2 * GB * 16))
                act.activation(x_rows[:, 2 * r:2 * r + 2, :], pj_ps[0:TP, 0, :].rearrange("p (b n) -> p b n", b=2),
                               ACT.Copy).then_inc(taken[0], 1)

            def exp_logits(act, n):
                act.wait_ge(logits_shifted, n + 1)
                act.activation(ex[:, :, :], ex[:, :, :], ACT.Exp).then_inc(logits_exp, 1)

            def deviation(dve, g, i, n):
                dve.wait_ge(filled[1], number(g, "mean%d" % (i + 1)))
                ge(dve, ln[i]["lo"], n)
                if i == 1:
                    ge(dve, kept, n)
                    if not (isinstance(n, int) and n == 0):
                        dve.wait_ge(filled[0], number(g, "xt1", back=1))
                for m in range(MC):
                    ins = dve.tensor_tensor(dev[i][:, m, :], hT[:, m, gcols(n)], pj_ps[:, 1, 0:N], ALU.subtract)
                ins.then_inc(taken[1], 1)

            def normalise(dve, i, n):
                dve.wait_ge(ln[i]["rstd"], n + 1)
                for m in range(MC):
                    ins = dve.tensor_tensor(dev[i][:, m, :], dev[i][:, m, :], rstd[i][:, :], ALU.mult)
                ins.then_inc(ln[i]["out"], 1)

            def lo(dve, i, n):
                dve.wait_ge(ln[i]["hi"], n + 1)
                to = (xg, split2)[i]
                dve.tensor_tensor(to[:, LO, :, :], dev[i][:, :, :], to[:, HI, :, :], ALU.subtract
                                  ).then_inc(ln[i]["lo"], 1)

            def take_router(dve, g):
                dve.wait_ge(filled[1], number(g, "router"))
                dve.tensor_copy(lgT[:, :], pj_ps[:, 1, 0:N]).then_inc(taken[1], 1)

            R_STEPS = 11
            R_AFTER = {"max": 1, "shift": 2, "recip": 3, "scale": 4, "top": 5, "index": 6, "expert": 7, "masks": 8,
                       "both": 9, "pick": 10, "slots": 11}
            wide = lambda a: a.unsqueeze(2).broadcast_to(small)

            def route(dve, n, step, at=None):
                done = lambda ins: ins.then_inc(r_chain, 1)
                if step in R_AFTER:
                    dve.wait_ge(r_chain, n * R_STEPS + R_AFTER[step])
                if step == "copy":
                    done(dve.tensor_copy(ex[:, :, :], at))
                elif step == "max":
                    done(dve.tensor_reduce(row_mx[:, :], ex[:, :, :], AX, ALU.max))
                elif step == "shift":
                    dve.tensor_tensor(ex[:, :, :], ex[:, :, :], wide(row_mx[:, :]), ALU.subtract
                                      ).then_inc(logits_shifted, 1)
                elif step == "sum":
                    dve.wait_ge(logits_exp, n + 1)
                    done(dve.tensor_reduce(row_sum[:, :], ex[:, :, :], AX, ALU.add))
                elif step == "recip":
                    done(dve.reciprocal(row_sum[:, :], row_sum[:, :]))
                elif step == "scale":
                    done(dve.tensor_tensor(ex[:, :, :], ex[:, :, :], wide(row_sum[:, :]), ALU.mult))
                elif step == "top":
                    dve.sem_inc(probs_there, 1)
                    for b in range(GB):
                        ins = dve.max(out=tops[:, b, :], in_=ex[:, b, :])
                    done(ins)
                elif step == "index":
                    dve.tensor_copy(top_p[:, bass.ds(n * GB, GB), :], tops[:, :, 0:2])
                    for b in range(GB):
                        ins = dve.max_index(out=top_i[:, b, :], in_max=tops[:, b, :], in_values=ex[:, b, :])
                    done(ins)
                elif step == "expert":
                    done(dve.tensor_copy(idx[:, :, :], top_i[:, :, 0:2]))
                elif step == "masks":
                    every = numbers[:, :].unsqueeze(1).broadcast_to(small)
                    for k in range(2):
                        ins = dve.tensor_tensor(mask[:, k, :, :], idx[:, :, k:k + 1].broadcast_to(small), every, ALU.is_equal)
                    done(ins)
                elif step == "both":
                    dve.tensor_tensor(both[:, :, :], mask[:, 0, :, :], mask[:, 1, :, :], ALU.add).then_inc(masks_done, 1)
                elif step == "rank":
                    ranks = at[:, 0:GB * E].rearrange("p (b e) -> p b e", e=E)
                    done(dve.tensor_tensor(rank[:, :, :], ranks, next_row[:, :].unsqueeze(1).broadcast_to(small), ALU.add))
                elif step == "pick":
                    for k in range(2):
                        ins = dve.tensor_tensor(pick[:, k, :, :], mask[:, k, :, :], rank[:, :, :], ALU.mult)
                    done(ins)
                elif step == "slots":
                    dve.tensor_reduce(slot_f[:, :, :], pick[:, :, :, :], AX, ALU.add).then_inc(slots_known, 1)
                    ge(dve, scattered, n * (2 * GB * 16))
                    dve.wait_ge(slots_known, n + 1)
                    dve.tensor_copy(slot[:, :, bass.ds(n * GB, GB)], slot_f[:, :, :])
                    dve.tensor_copy(slot_now[:, :, :], slot_f[:, :, :]).then_inc(slots_set, 1)

            def take_ranks(dve, g, n):
                dve.wait_ge(filled[1], number(g, "rank"))
                route(dve, n, "rank", pj_ps[0:TP, 1, 0:(GB + 1) * E])
                dve.wait_ge(r_chain, n * R_STEPS + 10)
                dve.tensor_tensor(next_row[:, :], next_row[:, :], pj_ps[0:TP, 1, GB * E:(GB + 1) * E], ALU.add
                                  ).then_inc(taken[1], 1)

            def take_logits(dve, g, n):
                dve.wait_ge(filled[1], number(g, "logits"))
                route(dve, n, "copy", pj_ps[0:TP, 1, :].rearrange("p (b e) -> p b e", b=GB)[:, :, 0:E])
                dve.wait_ge(r_chain, n * R_STEPS + 1)
                dve.sem_inc(taken[1], 1)

            def newton(eng, i, n, step):
                t = sq[i][:, 0, :]
                if step == 0:
                    eng.wait_ge(ln[i]["root"], n + 1)
                    eng.tensor_tensor(t, rstd[i][:, :], rstd[i][:, :], ALU.mult).then_inc(ln[i]["square"], 1)
                    eng.wait_ge(ln[i]["square"], n + 1)
                    eng.tensor_tensor(t, t, var[i][:, :], ALU.mult).then_inc(ln[i]["scaled"], 1)
                else:
                    eng.wait_ge(ln[i]["halved"], n + 1)
                    eng.tensor_tensor(rstd[i][:, :], rstd[i][:, :], t, ALU.mult).then_inc(ln[i]["rstd"], 1)

            def keep(pool, n):
                pool.wait_ge(ln[1]["out"], n + 1)
                pool.tensor_tensor(hT[:, :, gcols(n)], hT[:, :, gcols(n)], dev[1][:, :, :], ALU.add).then_inc(kept, 1)

            def scatter(pool, n, i, rows_at):
                if i == 0:
                    pool.wait_ge(slots_set, n + 1)
                    pool.wait_ge(taken[0], rows_at)
                    pool.wait_ge(cleared, E * 16)
                    pool.sem_inc(sending, 1)
                b, k = divmod(i, 2)
                pool.indirect_dma_start(
                    out=slots, out_offset=bass.IndirectOffsetOnAxis(ap=slot_now[0:SL, k, b:b + 1], axis=0),
                    in_=x_rows[0:SL, b, :], in_offset=None).then_inc(scattered, 16)

            def load_split(sp, g):
                sp.dma_start(sx[:, :, :, :].rearrange("p s m n -> p s (m n)").bitcast(F32),
                             ln_out[bass.ds(g, 1)].rearrange("o p s n -> p (o s) n")).then_inc(sx_in, 16)

            def store_split(sp, n):
                sp.wait_ge(ln[1]["lo"], n + 1)
                sp.dma_start(ln_out[bass.ds(n, 1)].rearrange("o p s n -> p (o s) n"),
                             split2[:, :, :, :].rearrange("p s m n -> p s (m n)").bitcast(F32)).then_inc(stored, 16)

            def run(eng, start, group, drain):
                start()
                group(0, False, True)
                group(1, True, True)
                with eng.Fori(2, NG - 1) as g:
                    group(g, True, True)
                group(NG - 1, True, False)
                drain()

            @block.sync
            def _(sp):
                sp.wait_ge(ring_zero, 4)
                sp.dma_start(rw[:, :, 0:E], router_w.rearrange("(c p) e -> p c e", p=P)).then_inc(rw_in, 16)
                sp.dma_start(raw2[:, 0:2048].rearrange("p (c n) -> p c n", c=MC),
                             sh_up[0].rearrange("(c p) n -> p c n", p=P)).then_inc(raw2_in, 16)
                sp.dma_start(raw2[:, 2048:4096].rearrange("p (c n) -> p c n", c=FC),
                             sh_down[0].rearrange("(c p) n -> p c n", p=P)).then_inc(raw2_in, 16)
                for e in range(E):
                    sp.dma_start(slots[e * CAP:(e + 1) * CAP, :].rearrange("(a p) n -> p a n", p=P),
                                 zeros[:, :].unsqueeze(1).broadcast_to([P, CAP // P, HD])).then_inc(cleared, 16)
                with sp.Fori(0, NG - 1) as g:
                    store_split(sp, g)
                sp.wait_ge(cleared, E * 16)
                sp.wait_ge(stored, (NG - 1) * 16)
                load_split(sp, 0)

            @block.tensor
            def _(pe):
                def v_tile(g, tile):
                    jj, b = int(tile[1]), int(tile[2])
                    begin(pe, g, tile)
                    k = 0
                    for m in range(MC):
                        for dp, wp in PASSES:
                            at = m * 1024 + jj * VW
                            ins = pe.matmul(pj_ps[0:TP, b % 2, 0:VW], xg[:, dp, m, b * TP:(b + 1) * TP],
                                            wB[:, wp, at:at + VW], start=(k == 0), stop=(k == 5))
                            k += 1
                    ins.then_inc(filled[b % 2], 1)

                def qk_tile(g, tile):
                    t, j = (0, 1)[tile[0] == "k"], int(tile[1])
                    begin(pe, g, tile)
                    k = 0
                    for m in range(MC):
                        for wp, dp in PASSES:
                            at = m * 2048 + t * 1024 + j * P
                            ins = pe.matmul(pj_ps[:, t, 0:N], wA[:, wp, at:at + P], xg[:, dp, m, :],
                                            start=(k == 0), stop=(k == 5))
                            k += 1
                    ins.then_inc(filled[t], 1)

                def scores(g, u):
                    j, half = divmod(u, 2)
                    if not half:
                        for t in range(2):
                            pe.wait_ge(taken[t], number(g, "qk"[t] + str(j), back=0 if j else 1))
                    ge(pe, shifted, g * NU + (u - 1))
                    for i in range(2):
                        b = 2 * half + i
                        ins = pe.matmul(s_ps[:, u % 2, i * 2 * TP:(i + 1) * 2 * TP], qT[:, j % 2, b * TP:(b + 1) * TP],
                                        kB[:, j % 2, b, :, :].rearrange("p h t -> p (h t)"), start=True, stop=True)
                    ins.then_inc(scores_done, 1)

                def turn(g, u):
                    ge(pe, turned_out, g * NU + u)
                    pe.wait_ge(scaled, g * NU + (u + 1))
                    for i in range(4):
                        ins = pe.transpose(t_ps[:, i * TP:(i + 1) * TP], prob[:, u % 4, i, :], ident[0:TP, 0:TP])
                    ins.then_inc(turned, 1)

                def values(g, u):
                    j, half = divmod(u, 2)
                    if u % 4 == 0:
                        for b in range(2, 4):
                            pe.wait_ge(taken[b % 2], number(g, "v%d%d" % (j // 2, b)))
                    pe.wait_ge(turned_out, g * NU + (u + 1))
                    ge(pe, o_lo, g * NU + u)
                    for i in range(2):
                        b = 2 * half + i
                        at = (j % 2) * P
                        ins = pe.matmul(o_ps[:, i * 2 * TP:(i + 1) * 2 * TP], v_rows[:, (j // 2) % 2, b, at:at + P],
                                        probT[:, u % 2, i * 2 * TP:(i + 1) * 2 * TP], start=True, stop=True)
                    ins.then_inc(pv_done, 1)

                def output(g, j, ms=range(MC)):
                    pe.wait_ge(o_lo, g * NU + 2 * (j + 1))
                    if j == 0:
                        ge(pe, h_added, g)
                    for m in ms:
                        for k, (wp, dp) in enumerate(PASSES):
                            at = 2048 + j * HD + m * P
                            ins = pe.matmul(y_ps[:, m, 0:N], wB[:, wp, at:at + P],
                                            oT[:, j % 2, dp, :, :].rearrange("p b t -> p (b t)"),
                                            start=(j == 0 and k == 0), stop=(j == NJ - 1 and k == 2))
                    if ms[-1] == MC - 1:
                        ins.then_inc(wo_done, 1)

                def group(g, behind, ahead):
                    V = {0: "00 01", 1: "02 03", 3: "10 11", 5: "12 13", 7: "20 21", 9: "22 23", 11: "30 31", 12: "32 33"}
                    for s in range(NU):
                        if s > 0:
                            scores(g, s)
                        if s % 2 == 0 and s // 2 + 1 < NJ:
                            qk_tile(g, "q%d" % (s // 2 + 1))
                            if s == 0:
                                scores(g, 0)
                            qk_tile(g, "k%d" % (s // 2 + 1))
                        for v in V.get(s, "").split():
                            v_tile(g, "v" + v)
                        for lag, what in ((2, turn), (3, values)):
                            if s >= lag:
                                what(g, s - lag)
                            elif behind:
                                what(g - 1, NU + s - lag)
                            if s == NU - 1 and lag == 2 and ahead:
                                pe.wait_ge(ln[0]["lo"], g + 2)
                                qk_tile(g, "q0")
                        if s in (13, 14):
                            output(g, 4, range(s - 13, s - 12))
                        elif s % 2 and s >= 5:
                            output(g, (s - 5) // 2)
                        elif s in (1, 3) and behind:
                            output(g - 1, NJ - 2 + s // 2)
                        if s == NU - 1 and behind:
                            rank_tile(pe, g, g - 1)
                        if s == NU - 1 and ahead:
                            qk_tile(g, "k0")
                        if s == 1 and ahead:
                            mean_tile(pe, g, 0, g + 1)
                        if s == 4 and ahead:
                            var_tile(pe, g, 0, g + 1)
                        if behind:
                            if s == 5:
                                mean_tile(pe, g, 1, g - 1)
                            if s == 6:
                                var_tile(pe, g, 1, g - 1)
                            if s == 10:
                                router_tile(pe, g, g - 1)
                                rows_tile(pe, g, 0, g - 1)
                                rows_tile(pe, g, 1, g - 1)
                            if s == 11:
                                logits_tile(pe, g, g - 1)

                def start():
                    mean_tile(pe, -1, 0, 0)
                    var_tile(pe, -1, 0, 0)
                    pe.wait_ge(rw_in, 16)
                    pe.wait_ge(tri_set, 2)
                    pe.wait_ge(ln[0]["lo"], 1)
                    qk_tile(-1, "q0")
                    qk_tile(-1, "k0")

                def drain():
                    g = NG - 1
                    turn(g, NU - 2)
                    values(g, NU - 3)
                    turn(g, NU - 1)
                    values(g, NU - 2)
                    output(g, NJ - 2)
                    values(g, NU - 1)
                    output(g, NJ - 1)

                run(pe, start, group, drain)

            @block.scalar
            def _(act):
                def take(g, tile):
                    act.wait_ge(filled[0], number(g, tile))

                def take_q(g, j, n):
                    take(g, "q%d" % j)
                    ge(act, scores_done, n * NU + 2 * (j - 1))
                    act.activation(qT[:, j % 2, :], pj_ps[:, 0, 0:N], ACT.Copy).then_inc(taken[0], 1)

                def take_v(g, tile):
                    jj, b = int(tile[1]), int(tile[2])
                    take(g, tile)
                    ge(act, pv_done, g * NU + 4 * (jj - 1))
                    act.activation(v_rows[:, jj % 2, b, :], pj_ps[0:TP, 0, 0:VW], ACT.Copy).then_inc(taken[0], 1)

                def normalise_batch(n):
                    for m in range(MC):
                        ins = act.activation(hT[:, m, gcols(n)], hT[:, m, gcols(n)], ACT.Identity,
                                             bias=bn_shift[:, m:m + 1], scale=bn_scale[:, m:m + 1])
                    ins.then_inc(affine, 1)

                def exps(g, u):
                    act.wait_ge(shifted, g * NU + (u + 1))
                    act.activation(prob[:, u % 4, :, 0:SL], prob[:, u % 4, :, 0:SL], ACT.Exp, scale=SCALE
                                   ).then_inc(exp_done, 1)

                def take_turned(g, u):
                    act.wait_ge(turned, g * NU + (u + 1))
                    ge(act, pv_done, g * NU + (u - 1))
                    act.activation(probT[:, u % 2, :], t_ps[:, 0:4 * TP], ACT.Copy).then_inc(turned_out, 1)

                def take_o(g, u):
                    j, half = divmod(u, 2)
                    act.wait_ge(pv_done, g * NU + (u + 1))
                    if not half:
                        ge(act, wo_done, g * NJ + (j - 1))
                    o4 = o_ps[:, 0:4 * TP].rearrange("p (b h t) -> p b h t", b=2, h=2)
                    for h in range(2):
                        rows = slice(h * DH, (h + 1) * DH)
                        ins = act.activation(oT[rows, j % 2, HI, 2 * half:2 * half + 2, :], o4[rows, :, h, :], ACT.Copy)
                    ins.then_inc(o_hi, 1)

                def group(g, behind, ahead):
                    V = {0: "00", 1: "02", 3: "10", 5: "12", 7: "20", 9: "22", 11: "30", 12: "32"}
                    for s in range(NU):
                        if s == 6 and behind:
                            square(act, g, 1, g - 1)
                        if s == 7 and behind:
                            root(act, g, 1, g - 1)
                        if s % 2 == 0 and s // 2 + 1 < NJ:
                            take_q(g, s // 2 + 1, g)
                        if s == NU - 1 and ahead:
                            take_q(g, 0, g + 1)
                        if s in V:
                            take_v(g, "v" + V[s])
                        if s >= 2:
                            take_turned(g, s - 2)
                        elif behind:
                            take_turned(g - 1, NU + s - 2)
                        exps(g, s)
                        if s >= 3:
                            take_o(g, s - 3)
                        elif behind:
                            take_o(g - 1, NU + s - 3)
                        if ahead:
                            if s == 0:
                                normalise_batch(g + 1)
                            if s == 2:
                                square(act, g, 0, g + 1)
                            if s == 4:
                                root(act, g, 0, g + 1)
                            if s == 6:
                                halve(act, 0, g + 1)
                            if s == 12:
                                hi(act, g, 0, g + 1)
                        if behind:
                            if s == 7:
                                halve(act, 1, g - 1)
                            if s == 10:
                                hi(act, g, 1, g - 1)
                                take_rows(act, g, 0, g - 1)
                                take_rows(act, g, 1, g - 1)
                            if s == 12:
                                exp_logits(act, g - 1)
                        if not ahead and s >= 13:
                            shared_hi(s - 13)

                def shared_hi(q):
                    act.wait_ge(filled[1], number(NG - 1, "k7"))
                    act.wait_ge(raw2_in, 32)
                    cols = slice(q * 1024, (q + 1) * 1024)
                    act.activation(wA[:, HI, cols], raw2[:, cols], ACT.Copy).then_inc(sh_hi, 1)

                def start():
                    normalise_batch(0)
                    square(act, -1, 0, 0)
                    root(act, -1, 0, 0)
                    halve(act, 0, 0)
                    hi(act, -1, 0, 0)
                    act.wait_ge(ring_zero, 4)
                    take_q(-1, 0, 0)

                def drain():
                    g = NG - 1
                    take_turned(g, NU - 2)
                    take_o(g, NU - 3)
                    shared_hi(3)
                    take_turned(g, NU - 1)
                    take_o(g, NU - 2)
                    take_o(g, NU - 1)

                run(act, start, group, drain)

            @block.vector
            def _(dve):
                def take(g, tile):
                    dve.wait_ge(filled[1], number(g, tile))

                def take_k(g, j, n):
                    take(g, "k%d" % j)
                    ge(dve, scores_done, n * NU + 2 * (j - 1))
                    for h in range(2):
                        rows = slice(h * DH, (h + 1) * DH)
                        ins = dve.tensor_copy(kB[rows, j % 2, :, h, :],
                                              pj_ps[rows, 1, 0:N].rearrange("p (b t) -> p b t", b=GB))
                    ins.then_inc(taken[1], 1)

                def take_v(g, tile):
                    jj, b = int(tile[1]), int(tile[2])
                    take(g, tile)
                    ge(dve, pv_done, g * NU + 4 * (jj - 1))
                    dve.tensor_copy(v_rows[:, jj % 2, b, :], pj_ps[0:TP, 1, 0:VW]).then_inc(taken[1], 1)

                def add(n):
                    dve.wait_ge(wo_done, n * NJ + NJ)
                    for m in range(MC):
                        ins = dve.tensor_tensor(hT[:, m, gcols(n)], hT[:, m, gcols(n)], y_ps[:, m, 0:N], ALU.add)
                    ins.then_inc(h_added, 1)

                def shift(g, u):
                    dve.wait_ge(scores_done, g * NU + (u + 1))
                    s4 = s_ps[:, u % 2, 0:4 * TP].rearrange("p (i t) -> p i t", i=4)[:, :, 0:SL]
                    dve.tensor_reduce(mx[:, u % 2, :], s4, AX, ALU.max).then_inc(max_done, 1)
                    ge(dve, turned, g * NU + (u - 3))
                    dve.wait_ge(max_done, g * NU + (u + 1))
                    dve.tensor_tensor(prob[:, u % 4, :, 0:SL], s4, mx[:, u % 2, :].unsqueeze(2).broadcast_to([TP, 4, SL]),
                                      ALU.subtract).then_inc(shifted, 1)

                def total(g, u):
                    dve.wait_ge(exp_done, g * NU + (u + 1))
                    ge(dve, scaled, g * NU + (u - 1))
                    dve.tensor_reduce(sm[:, u % 2, :], prob[:, u % 4, :, 0:SL], AX, ALU.add).then_inc(sum_done, 1)
                    dve.wait_ge(sum_done, g * NU + (u + 1))
                    dve.reciprocal(rc[:, u % 2, :], sm[:, u % 2, :]).then_inc(recip_done, 1)

                def take_o(g, u):
                    j, half = divmod(u, 2)
                    dve.wait_ge(o_hi, g * NU + (u + 1))
                    o4 = o_ps[:, 0:4 * TP].rearrange("p (b h t) -> p b h t", b=2, h=2)
                    for h in range(2):
                        rows = slice(h * DH, (h + 1) * DH)
                        clips = slice(2 * half, 2 * half + 2)
                        ins = dve.tensor_tensor(oT[rows, j % 2, LO, clips, :], o4[rows, :, h, :],
                                                oT[rows, j % 2, HI, clips, :], ALU.subtract)
                    ins.then_inc(o_lo, 1)

                def routing(s, place, n):
                    plan = {12: ("max", "shift", ""), 13: ("sum", "recip", "scale top"), 14: ("", "", "index expert"),
                            15: ("", "masks both", "pick slots")}
                    for step in plan.get(s, ("", "", ""))[place].split():
                        route(dve, n, step)

                def group(g, behind, ahead):
                    V = {0: "01", 1: "03", 3: "11", 5: "13", 7: "21", 9: "23", 11: "31", 12: "33"}
                    for s in range(NU):
                        shift(g, s)
                        if behind:
                            routing(s, 0, g - 1)
                        if s % 2 == 0 and s // 2 + 1 < NJ:
                            take_k(g, s // 2 + 1, g)
                        if s >= 1:
                            total(g, s - 1)
                        elif behind:
                            total(g - 1, NU - 1)
                        if behind:
                            routing(s, 1, g - 1)
                        if s == 13 and ahead:
                            lo(dve, 0, g + 1)
                        if s in V:
                            take_v(g, "v" + V[s])
                        if s >= 3:
                            take_o(g, s - 3)
                        elif behind:
                            take_o(g - 1, NU + s - 3)
                        if s == NU - 1 and behind:
                            take_ranks(dve, g, g - 1)
                        if s == NU - 1 and ahead:
                            take_k(g, 0, g + 1)
                        if s == 3 and behind:
                            add(g - 1)
                        if ahead:
                            if s == 1:
                                deviation(dve, g, 0, g + 1)
                            if s == 10:
                                normalise(dve, 0, g + 1)
                        if behind:
                            if s == 5:
                                deviation(dve, g, 1, g - 1)
                            if s == 9:
                                normalise(dve, 1, g - 1)
                            if s == 10:
                                lo(dve, 1, g - 1)
                                take_router(dve, g)
                            if s == 11:
                                take_logits(dve, g, g - 1)
                            routing(s, 2, g - 1)
                        if not ahead and s >= 14:
                            shared_lo(s - 14)

                def shared_lo(q):
                    dve.wait_ge(sh_hi, q + 1)
                    cols = slice(q * 1024, (q + 1) * 1024)
                    dve.tensor_tensor(wA[:, LO, cols], raw2[:, cols], wA[:, HI, cols], ALU.subtract)

                def start():
                    for e in range(E):
                        dve.memset(next_row[:, e:e + 1], float(e * CAP))
                        ins = dve.memset(numbers[:, e:e + 1], float(e))
                    ins.then_inc(numbers_set, 1)
                    dve.wait_ge(numbers_set, 1)
                    deviation(dve, -1, 0, 0)
                    newton(dve, 0, 0, 0)
                    newton(dve, 0, 0, 1)
                    normalise(dve, 0, 0)
                    lo(dve, 0, 0)
                    dve.wait_ge(ring_zero, 4)
                    take_k(-1, 0, 0)

                def drain():
                    g = NG - 1
                    total(g, NU - 1)
                    take_o(g, NU - 3)
                    shared_lo(2)
                    shared_lo(3)
                    take_o(g, NU - 2)
                    take_o(g, NU - 1)
                    add(g)

                run(dve, start, group, drain)

            @block.gpsimd
            def _(pool):
                def group(g, behind, ahead, scattering=True):
                    for u in range(NU):
                        pool.wait_ge(recip_done, g * NU + (u + 1))
                        p = prob[:, u % 4, :, 0:SL]
                        pool.tensor_tensor(p, p, rc[:, u % 2, :].unsqueeze(2).broadcast_to([TP, 4, SL]), ALU.mult
                                           ).then_inc(scaled, 1)
                        if ahead:
                            if u == 4:
                                newton(pool, 0, g + 1, 0)
                            if u == 8:
                                newton(pool, 0, g + 1, 1)
                        if behind:
                            if u == 6:
                                newton(pool, 1, g - 1, 0)
                            if u == 7:
                                newton(pool, 1, g - 1, 1)
                            if u == 10:
                                keep(pool, g - 1)
                        if scattering and u < 2 * GB:
                            scatter(pool, g - 2, u, number(g, "xt1", back=1))

                def start():
                    pool.memset(kB[:, :, :, :, :], 0.0).then_inc(ring_zero, 1)
                    pool.memset(prob[:, :, :, :], 0.0).then_inc(ring_zero, 1)
                    pool.memset(rw[:, :, :], 0.0).then_inc(ring_zero, 1)
                    pool.memset(zeros[:, :], 0.0).then_inc(ring_zero, 1)
                    pool.memset(before_w[:, :], 1.0).then_inc(ones_set, 1)
                    pool.memset(ones_w[:, :], 1.0).then_inc(tri_set, 1)
                    pool.wait_ge(ones_set, 1)
                    pool.affine_select(out=before_w[:, :], in_=before_w[:, :], compare_op=ALU.is_gt, fill=0.0, base=0,
                                       pattern=[[1, TP]], channel_multiplier=-1).then_inc(tri_set, 1)

                start()
                group(0, False, True, False)
                group(1, True, True, False)
                with pool.Fori(2, NG - 1) as g:
                    group(g, True, True)
                group(NG - 1, True, False)

        raw_sh.close()
        with ExitStack() as c:
            G1 = 3
            YR = 8
            raw = sb(c, "raw", [P, 4096])
            limits = sb(c, "limits", [1, MAXT - 1])
            over = sb(c, "over", [1, E, MAXT - 1])
            tiles_f = sb(c, "tiles_f", [1, 2, E])
            rows_in = sb(c, "rows_in", [P, 2, HD])
            rx = sb(c, "rx", [P, 2, MC, ET], F32R)
            act_f = sb(c, "act_f", [P, 2, N])
            act_s = sb(c, "act_s", [P, 2, FC, N], F32R)
            bg = sb(c, "bg", [P, MC, N])
            b_rows = sb(c, "b_rows", [TP, GB, HD])
            rows_out = sb(c, "rows_out", [P, 2, HD])
            fin = sb(c, "fin", [TP, YR, HD])
            up_ps = ps(c, "up_ps", [P, 4, 512])
            dn_ps = ps(c, "dn_ps", [P, MC, 512])
            tr_ps = pj_ps

            tiles_set = sem(c, "tiles_set")
            v_chain = sem(c, "t_chain")
            up_done = sem(c, "up_done")
            gelu_done = sem(c, "gelu_done")
            act_hi = sem(c, "act_hi")
            act_lo = sem(c, "act_lo")
            dn_done = sem(c, "dn_done")
            summed = sem(c, "summed")
            bt_done = sem(c, "bt_done")
            bt_out = sem(c, "bt_out")
            base_stored = sem(c, "base_stored")
            w0_in = sem(c, "w0_in")
            w0_hi = sem(c, "w0_hi")
            w0_lo = sem(c, "w0_lo")
            w_in = sem(c, "w_in")
            w_hi = sem(c, "w_hi")
            w_split = sem(c, "w_split")
            rows_loaded = sem(c, "rows_loaded")
            xt_done = sem(c, "rxt_done")
            x_hi = sem(c, "rx_hi")
            x_lo = sem(c, "rx_lo")
            rup_done = sem(c, "rup_done")
            rgelu_done = sem(c, "rgelu_done")
            ract_hi = sem(c, "ract_hi")
            ract_lo = sem(c, "ract_lo")
            rdn_done = sem(c, "rdn_done")
            y_out = sem(c, "y_out")
            y_stored = sem(c, "y_stored")
            rows_ready = sem(c, "rows_ready")
            gathered = [sem(c, "gathered_%d" % b) for b in range(YR)]
            base_in = [sem(c, "base_in_%d" % h) for h in range(2)]
            first = sem(c, "first")
            combined = sem(c, "combined")
            out_done = [sem(c, "out_done_%d" % h) for h in range(2)]
            block = c.enter_context(nc.Block())
            weights = (wB, wA)
            LN, LG = NG - 1, NG

            def tiles_before(eng, e):
                return eng.value_load(tiles_i[0:1, 1, bass.ds(e, 1)], min_val=0, max_val=2 * B * SL // ET + E)

            def tiles_of(eng, e):
                return eng.value_load(tiles_i[0:1, 0, bass.ds(e, 1)], min_val=1, max_val=MAXT), tiles_before(eng, e)

            def first_row(e, t):
                return nc.s_assert_within(e * CAP + t * ET, 0, E * CAP - ET,
                                          skip_runtime_bounds_check_because="an expert's tiles are among its slots")

            def y_ring(b, k):
                at = (2 * (b % YR) + k) * HD
                return raw[0:SL, at:at + HD]

            @block.gpsimd
            def _(pool):
                for s in (rgelu_done, y_out, ract_lo, y_stored, rdn_done, xt_done):
                    pool.sem_inc(s, 1)
                for i in range(2 * GB - 2):
                    scatter(pool, LN - 1, i, number(LN, "xt1"))
                newton(pool, 1, LN, 0)
                newton(pool, 1, LN, 1)
                for i in range(2 * GB - 2, 2 * GB):
                    scatter(pool, LN - 1, i, number(LN, "xt1"))
                keep(pool, LN)
                for i in range(2 * GB):
                    scatter(pool, LN, i, number(LG, "xt1"))

                def fetch(n, par, up, down):
                    w = weights[par]
                    pool.dma_start(raw[:, 0:2048].rearrange("p (c n) -> p c n", c=MC), up).then_inc(w_in, 16)
                    pool.dma_start(raw[:, 2048:4096].rearrange("p (c n) -> p c n", c=FC), down).then_inc(w_in, 16)
                    pool.wait_ge(w_in, n * 32)
                    if isinstance(n, int) and n == 1:
                        pool.wait_ge(dn_done, G1)
                    else:
                        pool.wait_ge(rdn_done, 1 + tiles_before(pool, n - 1))
                    for q in range(4):
                        cols = slice(q * 1024, (q + 1) * 1024)
                        pool.tensor_tensor(w[:, HI, cols], raw[:, cols], zero_c[:, 0:1].broadcast_to([P, 1024]), ALU.add
                                           ).then_inc(w_hi, 1)
                        pool.wait_ge(w_hi, (n - 1) * 4 + (q + 1))
                        ins = pool.tensor_tensor(w[:, LO, cols], raw[:, cols], w[:, HI, cols], ALU.subtract)
                    ins.then_inc(w_split, 1)
                    pool.wait_ge(w_split, n + 1)

                def fetch_expert(e, par):
                    fetch(e, par, rt_up[bass.ds(e, 1)].rearrange("o (c p) n -> p (o c) n", p=P),
                          rt_down[bass.ds(e, 1)].rearrange("o (c p) n -> p (o c) n", p=P))

                pool.wait_ge(w0_lo, 4)
                pool.sem_inc(w_split, 1)
                fetch_expert(1, 1)
                pool.wait_ge(tiles_set, 1)
                with pool.Fori(1, E // 2) as i:
                    for par in range(2):
                        fetch_expert(i * 2 + par, par)
                fetch(E, 0, sh_up[0].rearrange("(c p) n -> p c n", p=P), sh_down[0].rearrange("(c p) n -> p c n", p=P))
                n, t0 = tiles_of(pool, E - 1)
                pool.wait_ge(y_stored, 1 + (t0 + n) * 16)
                pool.sem_inc(rows_ready, 1)
                pool.wait_ge(rows_ready, 1)
                for b in range(B):
                    if b >= YR:
                        pool.wait_ge(combined, b - YR + 1)
                    for k in range(2):
                        pool.indirect_dma_start(
                            out=y_ring(b, k), out_offset=None, in_=slots,
                            in_offset=bass.IndirectOffsetOnAxis(ap=slot[0:SL, k, b:b + 1], axis=0)
                            ).then_inc(gathered[b % YR], 16)

            @block.sync
            def _(sp):
                def store(g):
                    sp.wait_ge(bt_out, g * 2 + 2)
                    sp.dma_start(base[bass.ds(g, 1)].rearrange("o p n -> p (o n)"),
                                 b_rows[:, :, :].rearrange("p b n -> p (b n)")).then_inc(base_stored, 16)

                def load_base(g):
                    h = g % 2
                    sp.wait_ge(base_stored, (g + 1) * 16)
                    if g >= 2:
                        sp.wait_ge(out_done[h], g // 2 * 16)
                    sp.dma_start(fin[:, h * GB:(h + 1) * GB, :].rearrange("p b n -> p (b n)"),
                                 base[g]).then_inc(base_in[h], 16)

                def store_out(g):
                    h = g % 2
                    sp.wait_ge(combined, (g + 1) * GB)
                    rows = fin[0:SL, h * GB:(h + 1) * GB, :] if g + 1 < NG else b_rows[0:SL, :, :]
                    sp.dma_start(out[g * GB:(g + 1) * GB].rearrange("b s n -> s b n"), rows).then_inc(out_done[h], 16)

                sp.dma_start(raw[:, 0:2048].rearrange("p (c n) -> p c n", c=MC),
                             rt_up[0].rearrange("(c p) n -> p c n", p=P)).then_inc(w0_in, 16)
                sp.dma_start(raw[:, 2048:4096].rearrange("p (c n) -> p c n", c=FC),
                             rt_down[0].rearrange("(c p) n -> p c n", p=P)).then_inc(w0_in, 16)
                sp.wait_ge(up_done, FC)
                load_split(sp, 1)
                store_split(sp, LN)
                for g in range(2, G1 + 1):
                    sp.wait_ge(up_done, g * FC)
                    load_split(sp, g)
                    store(g - 2)
                sp.wait_ge(stored, NG * 16)
                sp.wait_ge(tiles_set, 1)
                sp.wait_ge(scattered, 2 * B * 16)
                with sp.Fori(0, E) as e:
                    n, t0 = tiles_of(sp, e)
                    with sp.Fori(0, n) as t:
                        sp.wait_ge(xt_done, 1 + t0 + t)
                        sp.dma_start(rows_in[:, :, :], slots[bass.ds(first_row(e, t), ET), :].rearrange("(p a) n -> p a n", a=2)
                                     ).then_inc(rows_loaded, 16)
                n, t0 = tiles_of(sp, E - 1)
                sp.wait_ge(xt_done, 1 + t0 + n)
                sp.wait_ge(y_stored, 1 + 16)
                sp.dma_start(rows_in[:, :, :], slots[0:ET, :].rearrange("(p a) n -> p a n", a=2)).then_inc(rows_loaded, 16)
                store(G1 - 1)
                load_base(0)
                load_base(1)
                sp.wait_ge(up_done, (G1 + 1) * FC)
                load_split(sp, G1 + 1)
                store(G1)
                for g in range(G1 + 1, NG):
                    if g + 1 < NG:
                        sp.wait_ge(up_done, (g + 1) * FC)
                        load_split(sp, g + 1)
                    if g == G1 + 1:
                        store_out(0)
                        load_base(2)
                        store_out(1)
                        load_base(3)
                    elif g == G1 + 2:
                        store_out(2)
                        load_base(4)
                        store_out(3)
                    elif g == G1 + 3:
                        load_base(5)
                        store_out(4)
                    else:
                        load_base(6)
                        store_out(5)
                    if g + 1 < NG:
                        store(g)
                store_out(6)
                store_out(7)
                for h in range(2):
                    sp.wait_ge(out_done[h], NG // 2 * 16)

            @block.tensor
            def _(pe):
                def turn(g):
                    pe.wait_ge(summed, g + 1)
                    ge(pe, bt_out, g * 2)
                    for r in range(2):
                        for q in range(2):
                            for m in range(MC):
                                b = 2 * r + q
                                ins = pe.transpose(tr_ps[0:TP, r, q * HD + m * P:q * HD + (m + 1) * P],
                                                   bg[:, m, b * TP:(b + 1) * TP], ident[:, :])
                        ins.then_inc(bt_done, 1)

                def up(w, g, fs=range(FC)):
                    if fs[0] == 0:
                        pe.wait_ge(sx_in, (g + 1) * 16)
                    for f in fs:
                        if f >= 4 or not (isinstance(g, int) and g == 0):
                            pe.wait_ge(gelu_done, g * FC + (f - 3))
                        k = 0
                        for m in range(MC):
                            for wp, dp in PASSES:
                                at = m * F + f * P
                                ins = pe.matmul(up_ps[:, f % 4, 0:N], w[:, wp, at:at + P], sx[:, dp, m, :],
                                                start=(k == 0), stop=(k == 5))
                                k += 1
                        ins.then_inc(up_done, 1)

                def down(w, g, fs=range(FC)):
                    if fs[0] == 0 and not (isinstance(g, int) and g == 0):
                        pe.wait_ge(summed, g)
                    for f in fs:
                        pe.wait_ge(act_lo, g * FC + (f + 1))
                        for m in range(MC):
                            for k, (wp, dp) in enumerate(PASSES):
                                at = 2048 + f * HD + m * P
                                ins = pe.matmul(dn_ps[:, m, 0:N], w[:, wp, at:at + P], act_s[:, dp, f, :],
                                                start=(f == 0 and k == 0), stop=(f == FC - 1 and k == 2))
                    if fs[-1] == FC - 1:
                        ins.then_inc(dn_done, 1)

                def turn_rows(n0):
                    pe.wait_ge(rows_loaded, n0 * 16 + 16)
                    for m in range(MC):
                        for a in range(2):
                            ins = pe.transpose(tr_ps[:, 0, (2 * m + a) * P:(2 * m + a + 1) * P],
                                               rows_in[:, a, m * P:(m + 1) * P], ident[:, :])
                    ins.then_inc(xt_done, 1)

                def tile(w, e, n0):
                    pe.wait_ge(w_split, e + 1)
                    pe.wait_ge(x_lo, n0 + 1)
                    for f in range(FC):
                        pe.wait_ge(rgelu_done, 1 + n0 * FC + max(f - 3, 0))
                        k = 0
                        for m in range(MC):
                            for wp, dp in PASSES:
                                at = m * F + f * P
                                ins = pe.matmul(up_ps[:, f % 4, 0:ET], w[:, wp, at:at + P], rx[:, dp, m, :],
                                                start=(k == 0), stop=(k == 5))
                                k += 1
                        ins.then_inc(rup_done, 1)
                    pe.wait_ge(bt_out, G1 * 2)
                    turn_rows(n0 + 1)
                    pe.wait_ge(y_out, 1 + n0)
                    for a in range(2):
                        k = 0
                        for f in range(FC):
                            if a == 0:
                                pe.wait_ge(ract_lo, 1 + n0 * FC + (f + 1))
                            for dp, wp in PASSES:
                                at = 2048 + f * HD
                                ins = pe.matmul(dn_ps[:, 0, a * HD:(a + 1) * HD], act_s[:, dp, f, a * P:(a + 1) * P],
                                                w[:, wp, at:at + HD], start=(k == 0), stop=(k == 3 * FC - 1))
                                k += 1
                    ins.then_inc(rdn_done, 1)

                mean_tile(pe, LG, 1, LN)
                up(wA, 0, range(0, 3))
                var_tile(pe, LG, 1, LN)
                up(wA, 0, range(3, FC))
                down(wA, 0, range(0, 5))
                router_tile(pe, LG, LN)
                rows_tile(pe, LG, 0, LN)
                rows_tile(pe, LG, 1, LN)
                down(wA, 0, range(5, FC))
                logits_tile(pe, LG, LN)
                up(wA, 1, range(0, 6))
                rank_tile(pe, LG, LN)
                up(wA, 1, range(6, FC))
                pe.wait_ge(taken[0], number(LG, "xt1"))
                pe.wait_ge(taken[1], number(LG, "rank"))
                turn(0)
                down(wA, 1)
                up(wA, 2)
                turn(1)
                down(wA, 2, range(0, 6))
                pe.wait_ge(bt_out, 2 * 2)
                turn_rows(0)
                down(wA, 2, range(6, FC))
                pe.wait_ge(x_lo, 1)
                turn(G1 - 1)

                pe.wait_ge(tiles_set, 1)
                with pe.Fori(0, E // 2) as i:
                    for par in range(2):
                        e = i * 2 + par
                        n, t0 = tiles_of(pe, e)
                        with pe.Fori(0, n) as t:
                            tile(weights[par], e, t0 + t)

                pe.wait_ge(w_split, E + 1)
                n, t0 = tiles_of(pe, E - 1)
                pe.wait_ge(x_lo, t0 + n + 1)
                pe.wait_ge(y_out, 1 + t0 + n)
                up(wB, G1)
                down(wB, G1)
                with pe.Fori(G1 + 1, NG) as g:
                    up(wB, g)
                    turn(g - 1)
                    down(wB, g)
                turn(NG - 1)

            @block.scalar
            def _(act):
                def gelus(g, fs=range(FC)):
                    for f in fs:
                        act.wait_ge(up_done, g * FC + (f + 1))
                        if f >= 2 or not (isinstance(g, int) and g == 0):
                            act.wait_ge(act_lo, g * FC + (f - 1))
                        act.activation(act_f[:, f % 2, :], up_ps[:, f % 4, 0:N], ACT.Gelu).then_inc(gelu_done, 1)

                def take_rows_out(g):
                    ge(act, base_stored, g * 16)
                    for r in range(2):
                        act.wait_ge(bt_done, g * 2 + (r + 1))
                        act.activation(b_rows[:, 2 * r:2 * r + 2, :].rearrange("p b n -> p (b n)"), tr_ps[0:TP, r, :], ACT.Copy
                                       ).then_inc(bt_out, 1)

                def take_x(n0):
                    act.wait_ge(xt_done, 1 + n0 + 1)
                    act.activation(rx[:, HI, :, :].rearrange("p m t -> p (m t)"), tr_ps[:, 0, :], ACT.Copy).then_inc(x_hi, 1)

                def w0_part(q):
                    cols = slice(q * 1024, (q + 1) * 1024)
                    act.activation(wB[:, HI, cols], raw[:, cols], ACT.Copy).then_inc(w0_hi, 1)

                square(act, LG, 1, LN)
                gelus(0, range(0, 3))
                root(act, LG, 1, LN)
                gelus(0, range(3, 5))
                halve(act, 1, LN)
                gelus(0, range(5, 6))
                hi(act, LG, 1, LN)
                gelus(0, range(6, FC))
                take_rows(act, LG, 0, LN)
                take_rows(act, LG, 1, LN)
                exp_logits(act, LN)
                gelus(1)
                take_rows_out(0)
                act.wait_ge(w0_in, 32)
                w0_part(0)
                w0_part(1)
                gelus(2)
                take_rows_out(1)
                take_x(0)
                w0_part(2)
                w0_part(3)
                take_rows_out(2)
                act.wait_ge(tiles_set, 1)

                with act.Fori(0, E) as e:
                    n, t0 = tiles_of(act, e)
                    with act.Fori(0, n) as t:
                        n0 = t0 + t
                        for f in range(FC):
                            act.wait_ge(rup_done, n0 * FC + (f + 1))
                            act.wait_ge(ract_lo, 1 + n0 * FC + max(f - 1, 0))
                            act.activation(act_f[:, f % 2, 0:ET], up_ps[:, f % 4, 0:ET], ACT.Gelu).then_inc(rgelu_done, 1)
                        take_x(n0 + 1)
                        act.wait_ge(rdn_done, 1 + n0 + 1)
                        act.wait_ge(y_stored, 1 + n0 * 16)
                        act.activation(rows_out[:, :, :].rearrange("p a n -> p (a n)"), dn_ps[:, 0, :], ACT.Copy
                                       ).then_inc(y_out, 1)
                        act.wait_ge(y_out, 1 + n0 + 1)
                        act.dma_start(slots[bass.ds(first_row(e, t), ET), :].rearrange("(p a) n -> p a n", a=2),
                                      rows_out[:, :, :]).then_inc(y_stored, 16)

                gelus(G1)
                with act.Fori(G1 + 1, NG) as g:
                    gelus(g)
                    take_rows_out(g - 1)
                take_rows_out(NG - 1)

            @block.vector
            def _(dve):
                def split(g, f):
                    dve.wait_ge(gelu_done, g * FC + (f + 1))
                    dve.tensor_copy(act_s[:, HI, f, :], act_f[:, f % 2, :]).then_inc(act_hi, 1)
                    dve.wait_ge(act_hi, g * FC + (f + 1))
                    dve.tensor_tensor(act_s[:, LO, f, :], act_f[:, f % 2, :], act_s[:, HI, f, :], ALU.subtract
                                      ).then_inc(act_lo, 1)

                def add(g):
                    dve.wait_ge(dn_done, g + 1)
                    ge(dve, bt_done, g * 2)
                    for m in range(MC):
                        ins = dve.tensor_tensor(bg[:, m, :], hT[:, m, gcols(g)], dn_ps[:, m, 0:N], ALU.add)
                    ins.then_inc(summed, 1)

                def combine(b):
                    q, f = divmod(b, YR)
                    if b // GB == NG - 1:
                        dve.wait_ge(bt_out, (NG - 1) * 2 + (b % GB) // 2 + 1)
                        acc = b_rows[0:SL, b % GB, :]
                    else:
                        if f % GB == 0:
                            dve.wait_ge(base_in[f // GB], q * 16 + 16)
                        acc = fin[0:SL, f, :]
                    dve.wait_ge(gathered[f], q * 32 + 32)
                    for k, done in ((0, first), (1, combined)):
                        p = top_p[0:SL, b, k:k + 1]
                        dve.scalar_tensor_tensor(out=acc, in0=y_ring(f, k), scalar=p, in1=acc,
                                                 op0=ALU.mult, op1=ALU.add).then_inc(done, 1)
                        if k == 0:
                            dve.wait_ge(first, b + 1)

                def take_x(n0):
                    dve.wait_ge(x_hi, n0 + 1)
                    dve.tensor_tensor(rx[:, LO, :, :].rearrange("p m t -> p (m t)"), tr_ps[:, 0, :],
                                      rx[:, HI, :, :].rearrange("p m t -> p (m t)"), ALU.subtract).then_inc(x_lo, 1)

                def w0_part(q):
                    cols = slice(q * 1024, (q + 1) * 1024)
                    dve.wait_ge(w0_hi, q + 1)
                    dve.tensor_tensor(wB[:, LO, cols], raw[:, cols], wB[:, HI, cols], ALU.subtract).then_inc(w0_lo, 1)

                def splits(g, fs=range(FC)):
                    for f in fs:
                        split(g, f)

                def count_tiles():
                    ch = Chain(dve, v_chain)
                    for k in range(MAXT - 1):
                        dve.memset(limits[:, k:k + 1], float(ET * (k + 1)))
                    for e in range(E):
                        ins = dve.tensor_scalar(tiles_f[:, 0, e:e + 1], next_row[0:1, e:e + 1], float(-e * CAP), None, ALU.add)
                    ch.then(ins)
                    wide = [1, E, MAXT - 1]
                    ch.then(dve.tensor_tensor(over[:, :, :], tiles_f[:, 0, :].unsqueeze(2).broadcast_to(wide),
                                              limits[:, :].unsqueeze(1).broadcast_to(wide), ALU.is_gt))
                    ch.then(dve.tensor_reduce(tiles_f[:, 0, :], over[:, :, :], AX, ALU.add))
                    ch.then(dve.tensor_scalar(tiles_f[:, 0, :], tiles_f[:, 0, :], 1.0, None, ALU.add))
                    ch.then(dve.memset(tiles_f[:, 1, :], 0.0))
                    for e in range(1, E):
                        ch.then(dve.tensor_tensor(tiles_f[:, 1, e:e + 1], tiles_f[:, 1, e - 1:e], tiles_f[:, 0, e - 1:e],
                                                  ALU.add))
                    dve.tensor_copy(tiles_i[:, :, :], tiles_f[:, :, :]).then_inc(tiles_set, 1)

                deviation(dve, LG, 1, LN)
                splits(0, range(0, 5))
                normalise(dve, 1, LN)
                splits(0, range(5, 6))
                lo(dve, 1, LN)
                splits(0, range(6, FC))
                take_router(dve, LG)
                add(0)
                take_logits(dve, LG, LN)
                for step in ("max", "shift", "sum", "recip", "scale", "top"):
                    route(dve, LN, step)
                splits(1, range(0, 1))
                route(dve, LN, "index")
                route(dve, LN, "expert")
                splits(1, range(1, 2))
                route(dve, LN, "masks")
                route(dve, LN, "both")
                splits(1, range(2, 4))
                take_ranks(dve, LG, LN)
                route(dve, LN, "pick")
                route(dve, LN, "slots")
                splits(1, range(4, FC))
                count_tiles()
                add(1)
                w0_part(0)
                w0_part(1)
                splits(2)
                take_x(0)
                w0_part(2)
                w0_part(3)
                add(2)
                dve.wait_ge(tiles_set, 1)
                with dve.Fori(0, E) as e:
                    n, t0 = tiles_of(dve, e)
                    with dve.Fori(0, n) as t:
                        n0 = t0 + t
                        for f in range(FC):
                            dve.wait_ge(rgelu_done, 1 + n0 * FC + (f + 1))
                            if f == 0:
                                dve.wait_ge(rdn_done, 1 + n0)
                            dve.tensor_copy(act_s[:, HI, f, 0:ET], act_f[:, f % 2, 0:ET]).then_inc(ract_hi, 1)
                            dve.wait_ge(ract_hi, n0 * FC + (f + 1))
                            dve.tensor_tensor(act_s[:, LO, f, 0:ET], act_f[:, f % 2, 0:ET], act_s[:, HI, f, 0:ET],
                                              ALU.subtract).then_inc(ract_lo, 1)
                        take_x(n0 + 1)
                n, t0 = tiles_of(dve, E - 1)
                dve.wait_ge(rdn_done, 1 + t0 + n)
                splits(G1)
                add(G1)
                clips = {G1 + 1: range(0, 8), G1 + 2: range(8, 16), G1 + 3: range(16, 20), G1 + 4: range(20, 24)}
                for g in range(G1 + 1, NG):
                    for f in range(FC):
                        split(g, f)
                        for b in clips[g][f - 3:f - 2] if f >= 3 else ():
                            combine(b)
                    for b in clips[g][FC - 3:]:
                        combine(b)
                    add(g)
                for b in range(24, B):
                    combine(b)


_INS = ["x", "L0_tok_W1", "L0_tok_b1", "L0_tok_W2", "L0_tok_b2", "L0_tok_gamma", "L0_tok_beta", "L0_attn_kernel",
        "L0_attn_WO", "L0_ffn_shared_up", "L0_ffn_shared_down", "L0_ffn_routed_up", "L0_ffn_routed_down",
        "L0_ffn_router_w"]


def kernel(**inputs):
    import numpy as np
    import concourse.bacc as bacc
    from concourse.bass_utils import run_bass_kernel_spmd

    nc = bacc.Bacc("TRN2", target_bir_lowering=False, num_devices=1)
    arrays, args = {}, []
    for name in _INS:
        a = np.ascontiguousarray(inputs[name])
        arrays[f"in_{name}"] = a
        args.append(nc.dram_tensor(f"in_{name}", a.shape, mybir.dt.from_np(a.dtype), kind="ExternalInput").ap())
    shape = (inputs["x"].shape[0], 93, inputs["L0_tok_W2"].shape[1])
    args.append(nc.dram_tensor("out_0", shape, F32, kind="ExternalOutput").ap())
    audio_tower_kernel(nc, *args)
    r = run_bass_kernel_spmd(nc, [arrays], core_ids=[0])
    return r.results[0]["out_0"]
```
